# Optimizing a Trainium2 kernel written in Bass

```python
import numpy as np
import jax
import jax.numpy as jnp

def _softmax(x, axis=-1):
    return jax.nn.softmax(x, axis=axis)

def _gelu(x):
    return jax.nn.gelu(x, approximate=True)

def _silu(x):
    return jax.nn.silu(x)

def _sigmoid(x):
    return jax.nn.sigmoid(x)

def _layernorm(x, axis=-1, eps=1e-05):
    m = jnp.mean(x, axis=axis, keepdims=True)
    v = jnp.var(x, axis=axis, keepdims=True)
    return (x - m) / jnp.sqrt(v + eps)

def _scatter_add(tgt, idx, src, axis=0):
    return tgt.at[idx].add(src)

def _segment_sum(src, seg, n):
    return jax.ops.segment_sum(src, seg, n)
kernel_name = 'mk_adaln_ffn_d2_seqx_r4_eef59e'

def setup_inputs(seed: int=0):
    np.random.seed(seed)
    _w = jnp.asarray

    def _rec_inputs():
        import jax
        import jax.numpy as jnp
        _rk = jax.random.key(seed)
        x = 4.136e-05 + 0.9999 * jax.random.normal(jax.random.fold_in(_rk, 1), (4, 512, 256), jnp.float32)
        _lenS = 512 - jax.random.randint(jax.random.fold_in(_rk, 7), (4,), 0, max(1, 512 // 4) + 1, jnp.int32)
        _lenS2 = 512 - jax.random.randint(jax.random.fold_in(_rk, 8), (4,), 0, max(1, 512 // 4) + 1, jnp.int32)
        cond_1024 = -0.00608245 + 1.00131 * jax.random.normal(jax.random.fold_in(_rk, 11), (4, 256), jnp.float32)
        return (x, cond_1024)
    x, cond_1024 = _rec_inputs()

    def _L0_cond_setup():
        import jax, jax.numpy as jnp
        import numpy as np
        B, T, D_IN, V_IN, E = (64, 128, 256, 256, 256)
        key = jax.random.key(seed)
        ks = jax.random.split(key, 16)
        s = 0.01
        return {'video': jax.random.normal(ks[0], (B, V_IN), jnp.float32), 'seq': jax.random.normal(ks[1], (B, T, D_IN), jnp.float32), 'W_z': jax.random.normal(ks[2], (D_IN, E), jnp.float32) * s, 'U_z': jax.random.normal(ks[3], (E, E), jnp.float32) * s, 'C_z': jax.random.normal(ks[4], (V_IN, E), jnp.float32) * s, 'b_z': jnp.zeros((E,), jnp.float32), 'W_r': jax.random.normal(ks[5], (D_IN, E), jnp.float32) * s, 'U_r': jax.random.normal(ks[6], (E, E), jnp.float32) * s, 'C_r': jax.random.normal(ks[7], (V_IN, E), jnp.float32) * s, 'b_r': jnp.zeros((E,), jnp.float32), 'W': jax.random.normal(ks[8], (D_IN, E), jnp.float32) * s, 'U': jax.random.normal(ks[9], (E, E), jnp.float32) * s, 'C': jax.random.normal(ks[10], (V_IN, E), jnp.float32) * s, 'b': jnp.zeros((E,), jnp.float32)}
    _L0_cond_all = _L0_cond_setup()
    _L0_cond_in = {k: v for k, v in _L0_cond_all.items() if k in ('W_z', 'U_z', 'C_z', 'b_z', 'W_r', 'U_r', 'C_r', 'b_r', 'W', 'U', 'C', 'b')}
    del _L0_cond_all

    def _L0_ffn_setup():
        import jax, jax.numpy as jnp
        import numpy as np
        CAPACITY = 0.5
        key = jax.random.key(seed)
        ks = jax.random.split(key, 7)
        b, s, d, h = (4, 2048, 256, 1024)
        sc_r = 1.0 / np.sqrt(d)
        sc_1 = 1.0 / np.sqrt(d)
        sc_2 = 1.0 / np.sqrt(h)
        return {'x': jax.random.normal(ks[0], (b, s, d), dtype=jnp.float32), 'w_r': jax.random.uniform(ks[1], (d, 1), jnp.float32, -sc_r, sc_r), 'b_r': jax.random.uniform(ks[2], (1,), jnp.float32, -sc_r, sc_r), 'W1': jax.random.uniform(ks[3], (d, h), jnp.float32, -sc_1, sc_1), 'b1': jax.random.uniform(ks[4], (h,), jnp.float32, -sc_1, sc_1), 'W2': jax.random.uniform(ks[5], (h, d), jnp.float32, -sc_2, sc_2), 'b2': jax.random.uniform(ks[6], (d,), jnp.float32, -sc_2, sc_2)}
    _L0_ffn_all = _L0_ffn_setup()
    _L0_ffn_in = {k: v for k, v in _L0_ffn_all.items() if k in ('w_r', 'b_r', 'W1', 'b1', 'W2', 'b2')}
    del _L0_ffn_all

    def _L1_cond_setup():
        import jax, jax.numpy as jnp
        import numpy as np
        NUM_EXPERTS = 4
        TOP_K = 2
        key = jax.random.key(seed)
        ks = jax.random.split(key, 16)
        B, L, D, E, H = (8, 192, 256, NUM_EXPERTS, 1024)
        s = 0.02
        return {'context_c': jax.random.normal(ks[0], (B, L, D), jnp.float32), 'time_cond': jax.random.normal(ks[1], (B, D), jnp.float32), 'gate_w': jax.random.normal(ks[2], (3 * D, E), jnp.float32) * s, 'gate_b': jnp.zeros((E,), jnp.float32), 'time_w': jax.random.normal(ks[3], (D, 2 * E), jnp.float32) * s, 'time_b': jnp.zeros((2 * E,), jnp.float32), 'ew1': jax.random.normal(ks[4], (E, D, H), jnp.float32) * s, 'eb1': jnp.zeros((E, H), jnp.float32), 'ew2': jax.random.normal(ks[5], (E, H, D), jnp.float32) * s, 'eb2': jnp.zeros((E, D), jnp.float32), 'sw1': jax.random.normal(ks[6], (D, H), jnp.float32) * s, 'sb1': jnp.zeros((H,), jnp.float32), 'sw2': jax.random.normal(ks[7], (H, D), jnp.float32) * s, 'sb2': jnp.zeros((D,), jnp.float32)}
    _L1_cond_all = _L1_cond_setup()
    _L1_cond_in = {k: v for k, v in _L1_cond_all.items() if k in ('gate_w', 'gate_b', 'time_w', 'time_b', 'ew1', 'eb1', 'ew2', 'eb2', 'sw1', 'sb1', 'sw2', 'sb2')}
    del _L1_cond_all

    def _L1_ffn_setup():
        import jax, jax.numpy as jnp
        import numpy as np
        TOPK = 8
        NUM_EXPERTS = 64
        FFN = 768
        CAPACITY = 160

        def _swiglu(x, w1, w2):
            h = x @ w1.T
            x1, x2 = jnp.split(h, 2, axis=-1)
            return x1 * jax.nn.silu(x2) @ w2.T
        key = jax.random.key(seed)
        ks = jax.random.split(key, 6)
        B, S, H = (1, 128, 256)
        scale = 0.02
        return {'hidden_states': jax.random.normal(ks[0], (B, S, H), jnp.float32), 'wg': jax.random.normal(ks[1], (NUM_EXPERTS, H), jnp.float32) * scale, 'shared_w1': jax.random.normal(ks[2], (2 * FFN, H), jnp.float32) * scale, 'shared_w2': jax.random.normal(ks[3], (H, FFN), jnp.float32) * scale, 'expert_w1': jax.random.normal(ks[4], (NUM_EXPERTS, 2 * FFN, H), jnp.float32) * scale, 'expert_w2': jax.random.normal(ks[5], (NUM_EXPERTS, H, FFN), jnp.float32) * scale}
    _L1_ffn_all = _L1_ffn_setup()
    _L1_ffn_in = {k: v for k, v in _L1_ffn_all.items() if k in ('wg', 'shared_w1', 'shared_w2', 'expert_w1', 'expert_w2')}
    del _L1_ffn_all
    return {'x': x, 'cond_1024': cond_1024, 'L0_cond_W_z': _L0_cond_in['W_z'], 'L0_cond_U_z': _L0_cond_in['U_z'], 'L0_cond_C_z': _L0_cond_in['C_z'], 'L0_cond_b_z': _L0_cond_in['b_z'], 'L0_cond_W_r': _L0_cond_in['W_r'], 'L0_cond_U_r': _L0_cond_in['U_r'], 'L0_cond_C_r': _L0_cond_in['C_r'], 'L0_cond_b_r': _L0_cond_in['b_r'], 'L0_cond_W': _L0_cond_in['W'], 'L0_cond_U': _L0_cond_in['U'], 'L0_cond_C': _L0_cond_in['C'], 'L0_cond_b': _L0_cond_in['b'], 'L0_ffn_w_r': _L0_ffn_in['w_r'], 'L0_ffn_b_r': _L0_ffn_in['b_r'], 'L0_ffn_W1': _L0_ffn_in['W1'], 'L0_ffn_b1': _L0_ffn_in['b1'], 'L0_ffn_W2': _L0_ffn_in['W2'], 'L0_ffn_b2': _L0_ffn_in['b2'], 'L1_cond_gate_w': _L1_cond_in['gate_w'], 'L1_cond_gate_b': _L1_cond_in['gate_b'], 'L1_cond_time_w': _L1_cond_in['time_w'], 'L1_cond_time_b': _L1_cond_in['time_b'], 'L1_cond_ew1': _L1_cond_in['ew1'], 'L1_cond_eb1': _L1_cond_in['eb1'], 'L1_cond_ew2': _L1_cond_in['ew2'], 'L1_cond_eb2': _L1_cond_in['eb2'], 'L1_cond_sw1': _L1_cond_in['sw1'], 'L1_cond_sb1': _L1_cond_in['sb1'], 'L1_cond_sw2': _L1_cond_in['sw2'], 'L1_cond_sb2': _L1_cond_in['sb2'], 'L1_ffn_wg': _L1_ffn_in['wg'], 'L1_ffn_shared_w1': _L1_ffn_in['shared_w1'], 'L1_ffn_shared_w2': _L1_ffn_in['shared_w2'], 'L1_ffn_expert_w1': _L1_ffn_in['expert_w1'], 'L1_ffn_expert_w2': _L1_ffn_in['expert_w2']}

def reference(x, cond_1024, L0_cond_W_z, L0_cond_U_z, L0_cond_C_z, L0_cond_b_z, L0_cond_W_r, L0_cond_U_r, L0_cond_C_r, L0_cond_b_r, L0_cond_W, L0_cond_U, L0_cond_C, L0_cond_b, L0_ffn_w_r, L0_ffn_b_r, L0_ffn_W1, L0_ffn_b1, L0_ffn_W2, L0_ffn_b2, L1_cond_gate_w, L1_cond_gate_b, L1_cond_time_w, L1_cond_time_b, L1_cond_ew1, L1_cond_eb1, L1_cond_ew2, L1_cond_eb2, L1_cond_sw1, L1_cond_sb1, L1_cond_sw2, L1_cond_sb2, L1_ffn_wg, L1_ffn_shared_w1, L1_ffn_shared_w2, L1_ffn_expert_w1, L1_ffn_expert_w2):
    import jax
    import jax.numpy as jnp

    def _L0_cond_ref(video, seq, W_z, U_z, C_z, b_z, W_r, U_r, C_r, b_r, W, U, C, b):
        import jax, jax.numpy as jnp
        import numpy as np
        B, T, D_IN, V_IN, E = (64, 128, 256, 256, 256)
        vz = video @ C_z + b_z
        vr = video @ C_r + b_r
        vh = video @ C + b
        xz = jnp.einsum('btd,de->bte', seq, W_z)
        xr = jnp.einsum('btd,de->bte', seq, W_r)
        xh = jnp.einsum('btd,de->bte', seq, W)

        def step(h, xs):
            xzt, xrt, xht = xs
            z = jax.nn.sigmoid(xzt + h @ U_z + vz)
            r = jax.nn.sigmoid(xrt + h @ U_r + vr)
            hh = jnp.tanh(xht + r * h @ U + vh)
            h_new = (1.0 - z) * h + z * hh
            return (h_new, h_new)
        h0 = jnp.zeros((seq.shape[0], U.shape[0]), seq.dtype)
        xs = (jnp.swapaxes(xz, 0, 1), jnp.swapaxes(xr, 0, 1), jnp.swapaxes(xh, 0, 1))
        _, out_t = jax.lax.scan(step, h0, xs)
        return jnp.swapaxes(out_t, 0, 1)

    def _L0_ffn_ref(x, w_r, b_r, W1, b1, W2, b2):
        import jax, jax.numpy as jnp
        import numpy as np
        CAPACITY = 0.5
        b, s, d = x.shape
        k = int(CAPACITY * s)
        weights = (jnp.einsum('bsd,do->bso', x, w_r) + b_r).squeeze(-1)
        top_vals, _ = jax.lax.top_k(weights, k)
        threshold = top_vals[:, -1]
        selected = weights > threshold[:, None]
        hidden = jax.nn.gelu(jnp.einsum('bsd,dh->bsh', x, W1) + b1, approximate=False)
        blk = jnp.einsum('bsh,hd->bsd', hidden, W2) + b2
        m = selected[..., None]
        return jnp.where(m, blk, x)

    def _L1_cond_ref(context_c, time_cond, gate_w, gate_b, time_w, time_b, ew1, eb1, ew2, eb2, sw1, sb1, sw2, sb2):
        import jax, jax.numpy as jnp
        import numpy as np
        NUM_EXPERTS = 4
        TOP_K = 2
        B, L, D = context_c.shape
        E, K = (NUM_EXPERTS, TOP_K)
        L_head = L_wrist = L // 3
        head = context_c[:, :L_head]
        wrist = context_c[:, L_head:L_head + L_wrist]
        proprio = context_c[:, L_head + L_wrist:]
        full_agg = context_c.mean(axis=1)
        hp_agg = jnp.concatenate([head, proprio], axis=1).mean(axis=1)
        wp_agg = jnp.concatenate([wrist, proprio], axis=1).mean(axis=1)
        gate_in = jnp.concatenate([full_agg, hp_agg, wp_agg], axis=-1)
        gate_logits = gate_in @ gate_w + gate_b
        mod = jax.nn.silu(time_cond) @ time_w + time_b
        scale, shift = jnp.split(mod, 2, axis=-1)
        gate_logits = gate_logits * (1.0 + scale) + shift
        gate_scores = jax.nn.softmax(gate_logits, axis=-1)
        topk_w, topk_i = jax.lax.top_k(gate_scores, K)
        topk_w = topk_w / (topk_w.sum(axis=-1, keepdims=True) + 1e-08)
        onehot = (topk_i[..., None] == jnp.arange(E)[None, None, :]).astype(context_c.dtype)
        w_be = jnp.sum(topk_w[..., None] * onehot, axis=1)
        mask = np.ones((E, L), dtype=np.float32)
        mask[1, L_head:L_head + L_wrist] = 0.0
        mask[2, :L_head] = 0.0
        mask = jnp.asarray(mask)
        out = jnp.zeros_like(context_c)
        for e in range(E):
            h = jax.nn.gelu(context_c @ ew1[e] + eb1[e], approximate=True)
            y = h @ ew2[e] + eb2[e]
            out = out + w_be[:, e][:, None, None] * mask[e][None, :, None] * y
        shared = jax.nn.gelu(context_c @ sw1 + sb1, approximate=True) @ sw2 + sb2
        return out + shared

    def _L1_ffn_ref(hidden_states, wg, shared_w1, shared_w2, expert_w1, expert_w2):
        import jax, jax.numpy as jnp
        import numpy as np
        TOPK = 8
        NUM_EXPERTS = 64
        FFN = 768
        CAPACITY = 160

        def _swiglu(x, w1, w2):
            h = x @ w1.T
            x1, x2 = jnp.split(h, 2, axis=-1)
            return x1 * jax.nn.silu(x2) @ w2.T
        B, S, H = hidden_states.shape
        T = B * S
        x = hidden_states.reshape(T, H)
        shared_out = _swiglu(x, shared_w1, shared_w2)
        logits = x.astype(jnp.float32) @ wg.T
        gates = jax.nn.softmax(logits, axis=-1)
        w_topk, idx_topk = jax.lax.top_k(gates, TOPK)
        denom = jnp.maximum(w_topk.sum(-1, keepdims=True), jnp.finfo(jnp.float32).eps)
        w_topk = w_topk / denom
        A = T * TOPK
        flat_e = idx_topk.reshape(A)
        flat_w = w_topk.reshape(A)
        flat_t = jnp.repeat(jnp.arange(T), TOPK)
        order = jnp.argsort(flat_e)
        se, st, sw = (flat_e[order], flat_t[order], flat_w[order])
        counts = jnp.zeros(NUM_EXPERTS, jnp.int32).at[flat_e].add(1)
        starts = jnp.cumsum(counts) - counts
        rank = jnp.arange(A) - starts[se]
        valid = rank < CAPACITY
        buf = jnp.zeros((NUM_EXPERTS, CAPACITY, H), x.dtype).at[se, rank].set(x[st], mode='drop')
        h = jnp.einsum('ech,efh->ecf', buf, expert_w1)
        x1, x2 = jnp.split(h, 2, axis=-1)
        out = jnp.einsum('ecf,ehf->ech', x1 * jax.nn.silu(x2), expert_w2)
        y = out[se, jnp.clip(rank, 0, CAPACITY - 1)]
        y = jnp.where(valid[:, None], y * sw[:, None].astype(y.dtype), 0.0)
        combined = jnp.zeros((T, H), x.dtype).at[st].add(y)
        return (shared_out + combined).reshape(B, S, H)
    x = x + _L0_ffn_ref(_L0_cond_ref(cond_1024, x, L0_cond_W_z, L0_cond_U_z, L0_cond_C_z, L0_cond_b_z, L0_cond_W_r, L0_cond_U_r, L0_cond_C_r, L0_cond_b_r, L0_cond_W, L0_cond_U, L0_cond_C, L0_cond_b), L0_ffn_w_r, L0_ffn_b_r, L0_ffn_W1, L0_ffn_b1, L0_ffn_W2, L0_ffn_b2)
    x = x + _L1_ffn_ref(_L1_cond_ref(x, cond_1024, L1_cond_gate_w, L1_cond_gate_b, L1_cond_time_w, L1_cond_time_b, L1_cond_ew1, L1_cond_eb1, L1_cond_ew2, L1_cond_eb2, L1_cond_sw1, L1_cond_sb1, L1_cond_sw2, L1_cond_sb2), L1_ffn_wg, L1_ffn_shared_w1, L1_ffn_shared_w2, L1_ffn_expert_w1, L1_ffn_expert_w2)
    return x

_drawn_inputs = setup_inputs


def setup_inputs(seed=0):
    import zlib

    import numpy as np

    out = dict(_drawn_inputs(seed))
    spreads = {'L0_cond_b_z': (0.0, 0.1),
     'L0_cond_b_r': (0.0, 0.1),
     'L0_cond_b': (0.0, 0.1),
     'L1_cond_gate_b': (0.0, 0.1),
     'L1_cond_time_b': (0.0, 0.1),
     'L1_cond_eb1': (0.0, 0.1),
     'L1_cond_eb2': (0.0, 0.1),
     'L1_cond_sb1': (0.0, 0.1),
     'L1_cond_sb2': (0.0, 0.1)}
    factors = {}
    for name, (base, spread) in spreads.items():
        noise = np.random.default_rng([zlib.crc32(name.encode()), seed]).standard_normal(out[name].shape)
        drawn = base * np.exp(spread * noise) if base else spread * noise
        out[name] = jnp.asarray(drawn.astype(out[name].dtype))
    for name, factor in factors.items():
        out[name] = (out[name] * factor).astype(out[name].dtype)
    return out
```

```python
from contextlib import ExitStack

import numpy as np
import concourse.bass as bass
from concourse import mybir

F32 = mybir.dt.float32
BF16 = mybir.dt.bfloat16
F16 = mybir.dt.float16
U32 = mybir.dt.uint32
ALU = mybir.AluOpType
ACT = mybir.ActivationFunctionType
AX = mybir.AxisListType

P = 128
B, S, D = 4, 512, 256
KD = D // P
T = B * S
HID = 1024
KH = HID // P
GATES = 3
PARTS = 3
SEG = 16
SELECT = S // 2
NE0, TOP0 = 4, 2
REGIONS = ((0, 170), (170, 340), (340, 512))
NE, TOPK, FFN, CAP = 64, 8, 768, 160
KF = FFN // P
TILES = T // P
HALF = TILES // 2
ROW = D + NE
CAPS = ((0, P), (P, CAP))
WROW = KD * 2 * FFN + KF * D
ROUNDS = CAP // 8
RING = 4
EPS = float(np.finfo(np.float32).eps)


def program(nc, A, out):
    with ExitStack() as ctx:
        def sb(name, shape, dt=F32):
            return ctx.enter_context(nc.sbuf_tensor(name, shape, dt))

        def sem(name):
            return ctx.enter_context(nc.semaphore(name))

        bank = [ctx.enter_context(nc.psum_tensor(f"bank{i}", [P, 512], F32)) for i in range(8)]
        ctx_rows = nc.dram_tensor("ctx_rows", [T + CAP, ROW], F32, kind="Internal").ap()

        xT = sb("xT", [P, KD, B, S + SEG])
        hist = sb("hist", [P, KD, B, S])
        ident = sb("ident", [P, P])
        ones = sb("ones", [P, P])
        ones_bf = sb("ones_bf", [P, P], BF16)
        condT = sb("condT", [P, KD, B])
        slot_row = sb("slot_row", [P, 2])
        arena = sb("arena", [P, RING * WROW])

        def cut(at, *shape):
            n = int(np.prod(shape))
            v = arena[:, at:at + n]
            if len(shape) == 2:
                v = v.rearrange("p (a b) -> p a b", a=shape[0])
            return v

        s_x = sem("x_loaded")
        s_const = sem("const_loaded")
        gru(nc, sb, sem, A, bank, xT, hist, ident, ones, ones_bf, condT, slot_row, s_x, s_const)
        layer0_ffn(nc, sb, sem, A, bank, xT, hist, ident, ones_bf, cut)
        layer1_context(nc, sb, sem, A, bank, xT, hist, ident, ones, condT, cut)
        tables = routing(nc, sb, sem, A, bank, xT, hist, ident, ones, slot_row, cut, ctx_rows, out)
        experts(nc, sb, sem, A, bank, ident, arena, ctx_rows, out, *tables)


def gru(nc, sb, sem, A, bank, xT, hist, ident, ones, ones_bf, condT, slot_row, s_x, s_const):
    with ExitStack() as own:
        def t(name, shape, dt=F32):
            return own.enter_context(nc.sbuf_tensor(name, shape, dt))

        U = t("U", [P, GATES, KD, D])
        rest = t("rest", [P, GATES, KD, D])
        Us = t("Us", [P, GATES, PARTS, KD, D], BF16)
        W = t("W", [P, GATES, KD, D])
        C = t("C", [P, GATES, KD, D])
        bias = t("bias", [1, GATES, D])
        vb = t("vb", [B, GATES, D])
        which = t("which", [B, SEG * B])
        ring = t("ring", [P, 2 * SEG + 1, KD * B])
        r = t("r", [P, KD * B])
        z = t("z", [P, KD * B])
        cand = t("cand", [P, KD * B])
        rh = t("rh", [P, KD * B])
        neg_keep = t("neg_keep", [P, KD * B])
        step_in = t("step_in", [P, KD * B])
        h_part = t("h_part", [P, 2, KD * B], F16)
        rh_part = t("rh_part", [P, 2, KD * B], F16)

        s_w = sem("gru_weights_loaded")
        s_split = sem("weights_split")
        s_v = sem("cond_term")
        s_vb = sem("cond_term_copied")
        s_one = sem("ones_set")
        s_hhi, s_hlo, s_h = sem("h_hi"), sem("h_lo"), sem("h_full")
        s_rp, s_zp, s_cp = sem("r_pre"), sem("z_pre"), sem("cand_pre")
        s_r, s_z, s_c = sem("r_done"), sem("z_done"), sem("cand_done")
        s_rhhi, s_rhlo, s_rh = sem("rh_hi"), sem("rh_lo"), sem("rh_full")
        s_nk, s_in = sem("neg_keep_done"), sem("step_in_done")
        s_carry = sem("carried")
        s_hist = sem("hist_copied")

        names = (("W_r", "U_r", "C_r", "b_r"), ("W_z", "U_z", "C_z", "b_z"), ("W", "U", "C", "b"))
        PART_OF = ((0, 1, 2), (0, 1))
        pre = [[bank[2 * g + q][:, 0:SEG * KD * B].rearrange("p (t m b) -> p t m b", t=SEG, m=KD)
                for q in range(2)] for g in range(GATES)]

        with nc.Block() as block:
            @block.sync
            def _(sp):
                for g, (_w, u, c, b) in enumerate(names):
                    sp.dma_start(U[:, g], A["L0_cond_" + u].rearrange("(k p) e -> p k e", p=P)).then_inc(s_w, 16)
                    sp.dma_start(C[:, g], A["L0_cond_" + c].rearrange("(k p) e -> p k e", p=P)).then_inc(s_w, 16)
                    sp.dma_start(W[:, g], A["L0_cond_" + _w].rearrange("(k p) e -> p k e", p=P)).then_inc(s_w, 16)
                    sp.dma_start(bias[:, g, :], A["L0_cond_" + b].rearrange("(a e) -> a e", a=1)).then_inc(s_w, 16)
                sp.dma_start(condT[:], A["condT"].rearrange("(k p) b -> p k b", p=P)).then_inc(s_w, 16)
                sp.dma_start(which[:], A["which"]).then_inc(s_w, 16)

            @block.scalar
            def _(act):
                for k in range(KD):
                    act.dma_start(xT[:, k, :, 0:S],
                                  A["xT"][k * P:(k + 1) * P, :].rearrange("p (b s) -> p b s", b=B)).then_inc(s_x, 16)
                act.dma_start(ident[:], A["ident"]).then_inc(s_const, 16)
                act.dma_start(slot_row[:], A["slot_row"]).then_inc(s_const, 16)
                act.wait_ge(s_v, 1)
                nc.scalar.activation(vb[:, 0:2].rearrange("p g e -> p (g e)"), bank[6][0:B, :], ACT.Copy)
                nc.scalar.activation(vb[:, 2], bank[7][0:B, 0:D], ACT.Copy).then_inc(s_vb, 1)
                with act.Fori(0, S // (2 * SEG)) as i:
                    n = i * (2 * SEG)
                    for j in range(2 * SEG):
                        q, jj = j // SEG, j % SEG
                        act.wait_ge(s_rp, n + (j + 1))
                        nc.scalar.activation(r[:], pre[0][q][:, jj].rearrange("p m b -> p (m b)"), ACT.Sigmoid).then_inc(s_r, 1)
                        act.wait_ge(s_zp, n + (j + 1))
                        nc.scalar.activation(z[:], pre[1][q][:, jj].rearrange("p m b -> p (m b)"), ACT.Sigmoid).then_inc(s_z, 1)
                        act.wait_ge(s_cp, n + (j + 1))
                        nc.scalar.activation(cand[:], pre[2][q][:, jj].rearrange("p m b -> p (m b)"), ACT.Tanh).then_inc(s_c, 1)

            @block.gpsimd
            def _(pool):
                nc.gpsimd.memset(xT[:, :, :, S:S + SEG], 0.0).then_inc(s_one, 1)
                nc.gpsimd.memset(ones[:], 1.0).then_inc(s_one, 1)
                nc.gpsimd.memset(ones_bf[:], 1.0).then_inc(s_one, 1)
                pool.sem_inc(s_hist, 2)
                with pool.Fori(0, S // (2 * SEG)) as i:
                    n = i * (2 * SEG)
                    for q in range(2):
                        pool.wait_ge(s_h, n + (q * SEG + SEG + 1))
                        nc.gpsimd.tensor_copy(
                            hist[:, :, :, bass.ds(n + q * SEG, SEG)].rearrange("p k b t -> p (k b) t"),
                            ring[:, 1 + q * SEG:1 + q * SEG + SEG, :].rearrange("p t c -> p c t")).then_inc(s_hist, 1)

            @block.vector
            def _(dve):
                dve.wait_ge(s_w, 16 * 14)
                nc.vector.tensor_copy(Us[:, :, 0], U[:]).then_inc(s_split, 1)
                dve.wait_ge(s_split, 1)
                nc.vector.tensor_tensor(rest[:], U[:], Us[:, :, 0], ALU.subtract).then_inc(s_split, 1)
                dve.wait_ge(s_split, 2)
                nc.vector.tensor_copy(Us[:, :, 1], rest[:]).then_inc(s_split, 1)
                dve.wait_ge(s_split, 3)
                nc.vector.tensor_tensor(Us[:, :, 2], rest[:], Us[:, :, 1], ALU.subtract).then_inc(s_split, 1)
                nc.vector.memset(ring[:, 0], 0.0).then_inc(s_h, 1)
                nc.vector.memset(h_part[:, 0], 0.0).then_inc(s_hhi, 1)
                nc.vector.memset(h_part[:, 1], 0.0).then_inc(s_hlo, 1)
                dve.sem_inc(s_carry, 1)
                with dve.Fori(0, S // (2 * SEG)) as i:
                    n = i * (2 * SEG)
                    dve.wait_ge(s_carry, i + 1)
                    for j in range(2 * SEG):
                        h, h_new = ring[:, j], ring[:, j + 1]
                        dve.wait_ge(s_r, n + (j + 1))
                        dve.wait_ge(s_h, n + (j + 1))
                        nc.vector.tensor_tensor(rh_part[:, 0], r[:], h, ALU.mult).then_inc(s_rhhi, 1)
                        nc.vector.tensor_tensor(rh[:], r[:], h, ALU.mult).then_inc(s_rh, 1)
                        dve.wait_ge(s_rhhi, n + (j + 1))
                        dve.wait_ge(s_rh, n + (j + 1))
                        nc.vector.tensor_tensor(rh_part[:, 1], rh[:], rh_part[:, 0], ALU.subtract).then_inc(s_rhlo, 1)
                        dve.wait_ge(s_z, n + (j + 1))
                        nc.vector.scalar_tensor_tensor(out=neg_keep[:], in0=z[:], scalar=1.0, in1=h,
                                                       op0=ALU.subtract, op1=ALU.mult).then_inc(s_nk, 1)
                        dve.wait_ge(s_c, n + (j + 1))
                        nc.vector.tensor_tensor(step_in[:], z[:], cand[:], ALU.mult).then_inc(s_in, 1)
                        dve.wait_ge(s_nk, n + (j + 1))
                        dve.wait_ge(s_in, n + (j + 1))
                        nc.vector.tensor_tensor(h_part[:, 0], step_in[:], neg_keep[:], ALU.subtract).then_inc(s_hhi, 1)
                        if j % SEG == 0:
                            dve.wait_ge(s_hist, 2 * i + (1 + j // SEG))
                        nc.vector.tensor_tensor(h_new, step_in[:], neg_keep[:], ALU.subtract).then_inc(s_h, 1)
                        dve.wait_ge(s_hhi, n + (j + 2))
                        dve.wait_ge(s_h, n + (j + 2))
                        nc.vector.tensor_tensor(h_part[:, 1], h_new, h_part[:, 0], ALU.subtract).then_inc(s_hlo, 1)
                    nc.vector.tensor_copy(ring[:, 0], ring[:, 2 * SEG]).then_inc(s_carry, 1)

            @block.tensor
            def _(pe):
                pe.wait_ge(s_w, 16 * 14)
                pe.wait_ge(s_one, 3)
                for g in range(GATES):
                    o = bank[6][0:B, g * D:(g + 1) * D] if g < 2 else bank[7][0:B, 0:D]
                    for k in range(KD):
                        nc.tensor.matmul(o, condT[:, k], C[:, g, k], start=(k == 0), stop=False)
                    last = nc.tensor.matmul(o, ones[0:1, 0:B], bias[:, g], start=False, stop=True)
                last.then_inc(s_v, 1)
                pe.wait_ge(s_vb, 1)
                pe.wait_ge(s_x, 32)
                pe.wait_ge(s_const, 32)

                def input_terms(q, t0):
                    for g in range(GATES):
                        for m in range(KD):
                            o = pre[g][q][:, :, m, :]
                            cols = slice(m * P, (m + 1) * P)
                            for k in range(KD):
                                yield lambda o=o, g=g, k=k, m=m, cols=cols: nc.tensor.matmul(
                                    o, W[:, g, k, cols], xT[:, k, :, bass.ds(t0, SEG)].rearrange("p b t -> p t b"),
                                    start=(m == 0 and k == 0), stop=False, skip_group_check=True)
                            yield lambda o=o, g=g, cols=cols: nc.tensor.matmul(
                                o, vb[:, g, cols], which[:], start=False, stop=False, skip_group_check=True)

                def recur(g, q, jj, x, part):
                    for m in range(KD):
                        for k in range(KD):
                            for p in PART_OF[part]:
                                last = nc.tensor.matmul(pre[g][q][:, jj, m, :], Us[:, g, p, k, m * P:(m + 1) * P],
                                                        x[:, part, k * B:(k + 1) * B],
                                                        start=False, stop=False, skip_group_check=True)
                    return last

                for f in input_terms(0, 0):
                    f()
                pe.wait_ge(s_split, 4)
                with pe.Fori(0, S // (2 * SEG)) as i:
                    n = i * (2 * SEG)
                    for q in range(2):
                        ahead = list(input_terms(1 - q, n + (q + 1) * SEG))
                        for jj in range(SEG):
                            j = q * SEG + jj
                            pe.wait_ge(s_hhi, n + (j + 1))
                            recur(0, q, jj, h_part, 0)
                            pe.wait_ge(s_hlo, n + (j + 1))
                            recur(0, q, jj, h_part, 1).then_inc(s_rp, 1)
                            recur(1, q, jj, h_part, 0)
                            recur(1, q, jj, h_part, 1).then_inc(s_zp, 1)
                            pe.wait_ge(s_rhhi, n + (j + 1))
                            recur(2, q, jj, rh_part, 0)
                            pe.wait_ge(s_rhlo, n + (j + 1))
                            recur(2, q, jj, rh_part, 1).then_inc(s_cp, 1)
                            for f in ahead[len(ahead) * jj // SEG:len(ahead) * (jj + 1) // SEG]:
                                f()


def layer0_ffn(nc, sb, sem, A, bank, xT, hist, ident, ones_bf, cut):
    with ExitStack() as own:
        def t(name, shape, dt=F32):
            return own.enter_context(nc.sbuf_tensor(name, shape, dt))

        W1 = cut(0, KD, HID)
        W2 = cut(KD * HID, KH, D)
        wr = t("wr", [P, KD])
        wr_rep = t("wr_rep", [P, KD, P])
        br = t("br", [P, 1])
        b1 = t("b1", [P, KH])
        b2 = t("b2", [P, KD])
        ws = t("ws", [P, S])
        wcol = t("wcol", [P, S // P])
        ge = t("ge", [P, S // P, S], BF16)
        mask = t("mask", [P, S], U32)
        hid = t("hid", [P, KH, S])
        blk = t("blk", [P, KD, S])
        sel = t("sel", [P, KD, S])

        s_w = sem("ffn_weights_loaded")
        s_rep = sem("router_weights_spread")
        s_sp, s_s = sem("scores_pre"), sem("scores_done")
        s_tp, s_t = sem("scores_turned"), sem("score_cols")
        s_ge, s_cnt, s_m = sem("compared"), sem("counted"), sem("mask_done")
        s_fp, s_f = sem("hidden_pre"), sem("hidden_done")
        s_dp, s_d = sem("block_pre"), sem("block_done")
        s_sel, s_y = sem("selected"), sem("layer0_done")
        s_pass = sem("ffn_waits_passed")

        with nc.Block() as block:
            @block.sync
            def _(sp):
                sp.dma_start(wr[:], A["L0_ffn_w_r"]).then_inc(s_w, 16)
                sp.dma_start(br[:], A["L0_ffn_b_r"].rearrange("(a o) -> a o", a=1).to_broadcast([P, 1])).then_inc(s_w, 16)
                sp.dma_start(b1[:], A["L0_ffn_b1"]).then_inc(s_w, 16)
                sp.dma_start(b2[:], A["L0_ffn_b2"]).then_inc(s_w, 16)
                sp.dma_start(W1, A["L0_ffn_W1"].rearrange("(k p) f -> p k f", p=P)).then_inc(s_w, 16)
                sp.dma_start(W2, A["L0_ffn_W2"].rearrange("(f p) d -> p f d", p=P)).then_inc(s_w, 16)

            @block.tensor
            def _(pe):
                pe.wait_ge(s_w, 96)
                pe.wait_ge(s_rep, KD)
                with pe.Fori(0, B) as b:
                    def state(k):
                        return hist[:, k, bass.ds(b, 1), :].rearrange("p b t -> p (b t)")

                    for k in range(KD):
                        last = nc.tensor.matmul(bank[0][:], wr_rep[:, k], state(k), start=(k == 0), stop=(k == KD - 1))
                    last.then_inc(s_sp, 1)
                    for f in range(KH):
                        if f >= 2:
                            pe.wait_ge(s_f, b * KH + (f - 1))
                        for k in range(KD):
                            last = nc.tensor.matmul(bank[3 + f % 2][:], W1[:, k, f * P:(f + 1) * P], state(k),
                                                    start=(k == 0), stop=(k == KD - 1))
                        last.then_inc(s_fp, 1)
                        if f == 1:
                            pe.wait_ge(s_s, b + 1)
                            for j in range(S // P):
                                last = nc.tensor.transpose(bank[1][:, j * P:(j + 1) * P], ws[:, j * P:(j + 1) * P], ident[:])
                            last.then_inc(s_tp, 1)
                        if f == 5:
                            pe.wait_ge(s_ge, b + 1)
                            for j in range(S // P):
                                last = nc.tensor.matmul(bank[2][:], ones_bf[:], ge[:, j], start=(j == 0), stop=(j == S // P - 1))
                            last.then_inc(s_cnt, 1)
                    for d in range(KD):
                        for f in range(KH):
                            if d == 0:
                                pe.wait_ge(s_f, b * KH + (f + 1))
                            last = nc.tensor.matmul(bank[5 + d][:], W2[:, f, d * P:(d + 1) * P], hid[:, f],
                                                    start=(f == 0), stop=(f == KH - 1))
                        last.then_inc(s_dp, 1)

            @block.scalar
            def _(act):
                act.wait_ge(s_w, 96)
                with act.Fori(0, B) as b:
                    act.wait_ge(s_sp, b + 1)
                    nc.scalar.activation(ws[:], bank[0][:], ACT.Identity, bias=br[:, 0:1]).then_inc(s_s, 1)
                    for f in range(KH):
                        act.wait_ge(s_fp, b * KH + (f + 1))
                        nc.scalar.activation(hid[:, f], bank[3 + f % 2][:], ACT.Gelu, bias=b1[:, f:f + 1]).then_inc(s_f, 1)
                    for d in range(KD):
                        act.wait_ge(s_dp, b * KD + (d + 1))
                        nc.scalar.activation(blk[:, d], bank[5 + d][:], ACT.Identity, bias=b2[:, d:d + 1]).then_inc(s_d, 1)

            @block.vector
            def _(dve):
                dve.wait_ge(s_w, 96)
                for k in range(KD):
                    nc.vector.tensor_copy(wr_rep[:, k], wr[:, k:k + 1].to_broadcast([P, P])).then_inc(s_rep, 1)
                with dve.Fori(0, B) as b:
                    dve.wait_ge(s_tp, b + 1)
                    nc.vector.tensor_copy(wcol[:], bank[1][:].rearrange("p (j c) -> p j c", c=P)[:, :, 0]).then_inc(s_t, 1)
                    dve.wait_ge(s_t, b + 1)
                    dve.wait_ge(s_s, b + 1)
                    for j in range(S // P):
                        last = nc.vector.tensor_scalar(ge[:, j], ws[:], wcol[:, j:j + 1], None, ALU.is_le)
                    last.then_inc(s_ge, 1)
                    dve.wait_ge(s_cnt, b + 1)
                    nc.vector.tensor_scalar(mask[:], bank[2][:], float(SELECT - 1), None, ALU.is_le).then_inc(s_m, 1)
                    dve.wait_ge(s_m, b + 1)
                    for d in range(KD):
                        h = hist[:, d, bass.ds(b, 1), :].rearrange("p b t -> p (b t)")
                        x = xT[:, d, bass.ds(b, 1), 0:S].rearrange("p b t -> p (b t)")
                        nc.vector.tensor_copy(sel[:, d], h).then_inc(s_sel, 1)
                        dve.wait_ge(s_sel, (b * KD + d) * 2 + 1)
                        dve.wait_ge(s_d, b * KD + (d + 1))
                        dve.sem_inc(s_pass, 1)
                        nc.vector.copy_predicated(sel[:, d], mask[:], blk[:, d]).then_inc(s_sel, 1)
                        dve.wait_ge(s_sel, (b * KD + d) * 2 + 2)
                        nc.vector.tensor_tensor(x, x, sel[:, d], ALU.add).then_inc(s_y, 1)


def layer1_context(nc, sb, sem, A, bank, xT, hist, ident, ones, condT, cut):
    with ExitStack() as own:
        def t(name, shape, dt=F32):
            return own.enter_context(nc.sbuf_tensor(name, shape, dt))

        FF = KD * HID + KH * D
        w1 = [cut(u * FF, KD, HID) for u in range(1 + TOP0)]
        w2 = [cut(u * FF + KD * HID, KH, D) for u in range(1 + TOP0)]
        b1 = t("eb1", [P, 1 + TOP0, KH])
        b2 = t("eb2", [P, 1 + TOP0, KD])
        hid = t("ehid", [P, KH, S])
        tmp = t("etmp", [P, KD, S])
        sums = t("sums", [P, 3, KD, B])
        gate_in = t("gate_in", [P, 3, KD, B])
        gw = t("gw", [P, 3 * KD, NE0])
        gb = t("gb", [1, NE0])
        tw = t("tw", [P, KD, 2 * NE0])
        tb = t("tb", [1, 2 * NE0])
        silu_c = t("silu_c", [P, KD, B])
        mod = t("mod", [B, 2 * NE0])
        lg = t("lg", [B, 3, NE0])
        sm = t("sm", [B, 8])
        score = t("score", [B, 8])
        top = t("top", [B, 8])
        idx = t("idx", [B, 8], U32)
        idxf = t("idxf", [B, TOP0])
        wk = t("wk", [B, TOP0])
        off = t("off", [B, TOP0, 2])
        ck = t("ck", [B, TOP0, 3])
        ckd = t("ckd", [B, B, TOP0, 3])
        coef = t("coef", [P, B, TOP0, 3])

        s_w, s_sw = sem("gate_weights_loaded"), sem("shared_loaded")
        s_ew = [sem(f"expert_loaded{k}") for k in range(TOP0)]
        s_silu = sem("cond_silu")
        s_g = sem("gate_chain")
        s_gin, s_gp, s_ex = sem("gate_in_done"), sem("gate_pre"), sem("gate_exp")
        s_idx, s_ckd, s_cf = sem("experts_chosen"), sem("coef_rows"), sem("coef_spread")
        s_coef = sem("coef_done")
        s_fp, s_f = sem("ehidden_pre"), sem("ehidden_done")
        s_dp, s_d = sem("eblock_pre"), sem("eblock_done")
        s_add = sem("eblock_added")
        UN = 1 + TOP0

        with nc.Block() as block:
            @block.sync
            def _(sp):
                sp.dma_start(gw[:], A["L1_cond_gate_w"].rearrange("(c p) e -> p c e", p=P)).then_inc(s_w, 16)
                sp.dma_start(gb[:], A["L1_cond_gate_b"].rearrange("(a e) -> a e", a=1)).then_inc(s_w, 16)
                sp.dma_start(tw[:], A["L1_cond_time_w"].rearrange("(k p) e -> p k e", p=P)).then_inc(s_w, 16)
                sp.dma_start(tb[:], A["L1_cond_time_b"].rearrange("(a e) -> a e", a=1)).then_inc(s_w, 16)
                sp.dma_start(w1[0], A["L1_cond_sw1"].rearrange("(k p) f -> p k f", p=P)).then_inc(s_sw, 16)
                sp.dma_start(w2[0], A["L1_cond_sw2"].rearrange("(f p) d -> p f d", p=P)).then_inc(s_sw, 16)
                sp.dma_start(b1[:, 0], A["L1_cond_sb1"]).then_inc(s_sw, 16)
                sp.dma_start(b2[:, 0], A["L1_cond_sb2"]).then_inc(s_sw, 16)
                sp.wait_ge(s_idx, 1)
                for b in range(B):
                    for k in range(TOP0):
                        e = sp.value_load(idx[b:b + 1, k:k + 1], min_val=0, max_val=NE0 - 1)
                        u = 1 + k
                        if b:
                            sp.wait_ge(s_d, ((b - 1) * UN + u + 1) * KD)
                        one = bass.ds(e, 1)
                        sp.dma_start(w1[u], A["L1_cond_ew1"][one].rearrange("o (k p) f -> p (o k) f", p=P)).then_inc(s_ew[k], 16)
                        sp.dma_start(w2[u], A["L1_cond_ew2"][one].rearrange("o (f p) d -> p (o f) d", p=P)).then_inc(s_ew[k], 16)
                        sp.dma_start(b1[:, u], A["L1_cond_eb1"][one].rearrange("o p f -> p (o f)")).then_inc(s_ew[k], 16)
                        sp.dma_start(b2[:, u], A["L1_cond_eb2"][one].rearrange("o p k -> p (o k)")).then_inc(s_ew[k], 16)

            @block.tensor
            def _(pe):
                pe.wait_ge(s_w, 64)
                pe.wait_ge(s_silu, 1)
                for k in range(KD):
                    nc.tensor.matmul(bank[1][0:B, 0:2 * NE0], silu_c[:, k], tw[:, k], start=(k == 0), stop=False)
                nc.tensor.matmul(bank[1][0:B, 0:2 * NE0], ones[0:1, 0:B], tb[:], start=False, stop=True).then_inc(s_gp, 1)
                pe.wait_ge(s_gin, 1)
                for c in range(3 * KD):
                    nc.tensor.matmul(bank[0][0:B, 0:NE0], gate_in[:, c // KD, c % KD], gw[:, c], start=(c == 0), stop=False)
                nc.tensor.matmul(bank[0][0:B, 0:NE0], ones[0:1, 0:B], gb[:], start=False, stop=True).then_inc(s_gp, 1)

                def unit(b, u, base):
                    x = [xT[:, k, bass.ds(b, 1), 0:S].rearrange("p b t -> p (b t)") for k in range(KD)]
                    for f in range(KH):
                        if f >= 2 or u:
                            pe.wait_ge(s_f, base * KH + (u * KH + f - 1))
                        for k in range(KD):
                            last = nc.tensor.matmul(bank[3 + f % 2][:], w1[u][:, k, f * P:(f + 1) * P], x[k],
                                                    start=(k == 0), stop=(k == KD - 1))
                        last.then_inc(s_fp, 1)
                    for d in range(KD):
                        for f in range(KH):
                            if d == 0:
                                pe.wait_ge(s_f, base * KH + (u * KH + f + 1))
                            if u and f == 0:
                                pe.wait_ge(s_d, base * KD + ((u - 1) * KD + d + 1))
                            last = nc.tensor.matmul(bank[5 + d][:], w2[u][:, f, d * P:(d + 1) * P], hid[:, f],
                                                    start=(f == 0), stop=(f == KH - 1))
                        last.then_inc(s_dp, 1)

                pe.wait_ge(s_ckd, 1)
                nc.tensor.matmul(bank[2][:, 0:B * TOP0 * 3], ones[0:B, :],
                                 ckd[:].rearrange("q b k r -> q (b k r)"), start=True, stop=True).then_inc(s_cf, 1)
                pe.wait_ge(s_sw, 64)
                with pe.Fori(0, B) as b:
                    unit(b, 0, b * UN)
                    for k in range(TOP0):
                        pe.wait_ge(s_ew[k], b * 64 + 64)
                        unit(b, 1 + k, b * UN)

            @block.scalar
            def _(act):
                nc.scalar.activation(silu_c[:], condT[:], ACT.Silu).then_inc(s_silu, 1)
                act.wait_ge(s_g, 6)
                nc.scalar.activation(lg[:, 2], lg[:, 1], ACT.Exp, bias=sm[:, 0:1], accum_out=sm[:, 1:2]).then_inc(s_ex, 1)
                act.wait_ge(s_sw, 64)
                with act.Fori(0, B) as b:
                    for u in range(UN):
                        if u:
                            act.wait_ge(s_ew[u - 1], b * 64 + 64)
                        for f in range(KH):
                            act.wait_ge(s_fp, b * UN * KH + (u * KH + f + 1))
                            nc.scalar.activation(hid[:, f], bank[3 + f % 2][:], ACT.Gelu_apprx_tanh,
                                                 bias=b1[:, u, f:f + 1]).then_inc(s_f, 1)
                        for d in range(KD):
                            act.wait_ge(s_dp, b * UN * KD + (u * KD + d + 1))
                            o = tmp[:, d] if u else hist[:, d, bass.ds(b, 1), :].rearrange("p b t -> p (b t)")
                            if u:
                                act.wait_ge(s_add, b * TOP0 * KD + ((u - 1) * KD + d + 1))
                            nc.scalar.activation(o, bank[5 + d][:], ACT.Identity, bias=b2[:, u, d:d + 1]).then_inc(s_d, 1)

            @block.vector
            def _(dve):
                dve.sem_inc(s_add, KD)
                g = [0]

                def chain(ins):
                    g[0] += 1
                    ins.then_inc(s_g, 1)
                    dve.wait_ge(s_g, g[0])

                for i, (a, z) in enumerate(REGIONS):
                    last = nc.vector.tensor_reduce(sums[:, i], xT[:, :, :, a:z], AX.X, ALU.add)
                chain(last)
                (h0, h1), (w0, w1_), (p0, p1) = REGIONS
                nc.vector.tensor_tensor(gate_in[:, 1], sums[:, 0], sums[:, 2], ALU.add)
                chain(nc.vector.tensor_tensor(gate_in[:, 2], sums[:, 1], sums[:, 2], ALU.add))
                chain(nc.vector.tensor_tensor(gate_in[:, 0], gate_in[:, 1], sums[:, 1], ALU.add))
                nc.vector.tensor_scalar(gate_in[:, 0], gate_in[:, 0], 1.0 / S, None, ALU.mult)
                nc.vector.tensor_scalar(gate_in[:, 1], gate_in[:, 1], 1.0 / (h1 - h0 + p1 - p0), None, ALU.mult)
                nc.vector.tensor_scalar(gate_in[:, 2], gate_in[:, 2], 1.0 / (w1_ - w0 + p1 - p0), None,
                                        ALU.mult).then_inc(s_gin, 1)
                dve.wait_ge(s_gp, 2)
                chain(nc.vector.tensor_copy(mod[:], bank[1][0:B, 0:2 * NE0]))
                chain(nc.vector.scalar_tensor_tensor(out=lg[:, 0], in0=mod[:, 0:NE0], scalar=1.0, in1=bank[0][0:B, 0:NE0],
                                                     op0=ALU.add, op1=ALU.mult))
                nc.vector.memset(score[:], -1.0)
                nc.vector.tensor_tensor(lg[:, 1], lg[:, 0], mod[:, NE0:], ALU.add).then_inc(s_gin, 1)
                dve.wait_ge(s_gin, 2)
                nc.vector.tensor_reduce(sm[:, 0:1], lg[:, 1], AX.X, ALU.max, negate=True).then_inc(s_g, 1)
                g[0] += 1
                dve.wait_ge(s_ex, 1)
                chain(nc.vector.reciprocal(sm[:, 2:3], sm[:, 1:2]))
                chain(nc.vector.tensor_scalar(score[:, 0:NE0], lg[:, 2], sm[:, 2:3], None, ALU.mult))
                chain(nc.vector.max(top[:], score[:]))
                nc.vector.max_index(idx[:], top[:], score[:]).then_inc(s_idx, 1)
                chain(nc.vector.tensor_reduce(sm[:, 3:4], top[:, 0:TOP0], AX.X, ALU.add))
                chain(nc.vector.tensor_scalar(sm[:, 4:5], sm[:, 3:4], 1e-8, None, ALU.add))
                chain(nc.vector.reciprocal(sm[:, 5:6], sm[:, 4:5]))
                chain(nc.vector.tensor_scalar(wk[:], top[:, 0:TOP0], sm[:, 5:6], None, ALU.mult))
                dve.wait_ge(s_idx, 1)
                chain(nc.vector.tensor_copy(idxf[:], idx[:, 0:TOP0]))
                nc.vector.tensor_scalar(off[:, :, 0], idxf[:], 2.0, None, ALU.not_equal)
                chain(nc.vector.tensor_scalar(off[:, :, 1], idxf[:], 1.0, None, ALU.not_equal))
                nc.vector.tensor_tensor(ck[:, :, 0], off[:, :, 0], wk[:], ALU.mult)
                nc.vector.tensor_tensor(ck[:, :, 1], off[:, :, 1], wk[:], ALU.mult)
                chain(nc.vector.tensor_copy(ck[:, :, 2], wk[:]))
                for b in range(B):
                    last = nc.vector.tensor_scalar(ckd[:, b].rearrange("q k r -> q (k r)"),
                                                   ck[:].rearrange("q k r -> q (k r)"), ident[0:B, b:b + 1], None, ALU.mult)
                last.then_inc(s_ckd, 1)
                dve.wait_ge(s_cf, 1)
                nc.vector.tensor_copy(coef[:].rearrange("p b k r -> p (b k r)"), bank[2][:, 0:B * TOP0 * 3]).then_inc(s_coef, 1)
                dve.wait_ge(s_coef, 1)
                with dve.Fori(0, B) as b:
                    for k in range(TOP0):
                        for d in range(KD):
                            dve.wait_ge(s_d, b * UN * KD + ((1 + k) * KD + d + 1))
                            if k:
                                dve.wait_ge(s_add, b * TOP0 * KD + (k * KD + d + 1))
                            for i, (a, z) in enumerate(REGIONS):
                                acc = hist[:, d, bass.ds(b, 1), a:z].rearrange("p b t -> p (b t)")
                                last = nc.vector.scalar_tensor_tensor(
                                    out=acc, in0=tmp[:, d, a:z], scalar=coef[:, bass.ds(b, 1), k, i:i + 1].rearrange("p b i -> p (b i)"),
                                    in1=acc, op0=ALU.mult, op1=ALU.add)
                            last.then_inc(s_add, 1)
                dve.wait_ge(s_add, KD + B * TOP0 * KD)


def routing(nc, sb, sem, A, bank, xT, hist, ident, ones, slot_row, cut, ctx_rows, out):
    tok = [sb(f"tok{c}", [b - a, NE], U32) for c, (a, b) in enumerate(CAPS)]
    with ExitStack() as own:
        def t(name, shape, dt=F32):
            return own.enter_context(nc.sbuf_tensor(name, shape, dt))

        TH = T // 2
        sw1 = cut(0, KD, 2 * FFN)
        sw2 = cut(KD * 2 * FFN, KF, D)
        at = KD * 2 * FFN + KF * D
        rows = cut(at, TILES, ROW)
        at += TILES * ROW
        act_f = cut(at, KF, S)
        at += KF * S
        lin = cut(at, 2, S)
        at += 2 * S
        maskT = cut(at, TH)
        wg = t("wg", [P, KD, NE])
        gates = t("gates", [P, TILES, NE])
        left = t("left", [P, TILES, NE])
        top8 = t("top8", [P, TILES, TOPK])
        st = t("st", [P, 4, TILES])
        cum = t("cum", [P, TH])
        vrev = t("vrev", [P, TH])
        shift = t("shift", [P, P])
        before = t("before", [P, 1])
        order = t("order", [P, 2, CAP])
        slots = t("slots", [P, 4, NE])
        orow = t("orow", [P, 2, D])

        s_w, s_wg = sem("shared_w_loaded"), sem("router_loaded")
        s_lp, s_c, s_ex = sem("logits_pre"), sem("route_chain"), sem("route_exp")
        s_mt, s_off = sem("mask_turned"), sem("offset_pre")
        s_ot = sem("order_turned")
        s_rt, s_rc = sem("rows_turned"), sem("rows_copied")
        s_dense, s_rows = sem("dense_done"), sem("rows_stored")
        s_z = sem("spare_zero")
        s_up, s_lin, s_act = sem("up_pre"), sem("lin_copied"), sem("gated")
        s_silu = sem("silu_done")
        s_dp, s_base = sem("shared_pre"), sem("base_done")
        s_bt, s_bc = sem("base_turned"), sem("base_copied")
        s_out = [sem(f"base_stored{q}") for q in range(2)]
        s_sum = sem("base_summed")

        def tile_of(i):
            return (i % 2) * HALF + i // 2

        with nc.Block() as block:
            @block.sync
            def _(sp):
                sp.dma_start(wg[:], A["wgT"].rearrange("(k p) e -> p k e", p=P)).then_inc(s_wg, 16)
                sp.dma_start(vrev[:], A["vrev"]).then_inc(s_wg, 16)
                sp.dma_start(shift[:], A["shift"]).then_inc(s_wg, 16)
                sp.dma_start(sw1, A["sw1T"].rearrange("(k p) f -> p k f", p=P)).then_inc(s_w, 16)
                sp.dma_start(sw2, A["sw2T"].rearrange("(f p) d -> p f d", p=P)).then_inc(s_w, 16)
                sp.wait_ge(s_z, 1)
                for a, z in CAPS:
                    sp.dma_start(ctx_rows[T + a:T + z, :], cum[0:z - a, 0:ROW]).then_inc(s_rows, 16)
                    sp.dma_start(out[T + a:T + z, :], cum[0:z - a, 0:D]).then_inc(s_rows, 16)
                sp.wait_ge(s_rows, 64)
                sp.sem_inc(s_z, 1)
                sp.wait_ge(s_rc, TILES)
                sp.wait_ge(s_dense, 1)
                v = ctx_rows[0:T, :].rearrange("(h j p) c -> p j h c", h=2, p=P)
                r4 = rows.rearrange("p (j h) c -> p j h c", h=2)
                for h in range(2):
                    sp.dma_start(v[:, :, h], r4[:, :, h]).then_inc(s_rows, 16)
                for i in range(TILES):
                    sp.wait_ge(s_bc, i + 1)
                    sp.dma_start(out[i * P:(i + 1) * P, :], orow[:, i % 2]).then_inc(s_out[i % 2], 16)
                sp.wait_ge(s_rows, 96)
                for q in range(2):
                    sp.wait_ge(s_out[q], 8 * TILES)

            @block.tensor
            def _(pe):
                pe.wait_ge(s_wg, 48)
                for i in range(TILES):
                    c = tile_of(i)
                    b, o = c * P // S, c * P % S
                    for k in range(KD):
                        last = nc.tensor.matmul(bank[i // 8][:, (i % 8) * NE:(i % 8 + 1) * NE], hist[:, k, b, o:o + P], wg[:, k],
                                                start=(k == 0), stop=(k == KD - 1))
                last.then_inc(s_lp, 1)
                for i in range(TILES):
                    c = tile_of(i)
                    b, o = c * P // S, c * P % S
                    if i >= 2:
                        pe.wait_ge(s_rc, i - 1)
                    for k in range(KD):
                        last = nc.tensor.transpose(bank[2 + i % 2][:, k * P:(k + 1) * P], hist[:, k, b, o:o + P], ident[:])
                    last.then_inc(s_rt, 1)
                pe.wait_ge(s_w, 32)
                for b in range(B):
                    if b == 1:
                        pe.wait_ge(s_dense, 1)
                        for j in range(HALF):
                            last = nc.tensor.transpose(bank[j // 4][:, (j % 4) * P:(j % 4 + 1) * P],
                                                       left[:, 2 * j:2 * j + 2].rearrange("p h e -> p (h e)"), ident[:])
                        last.then_inc(s_mt, 1)
                    for f in range(KF):
                        n = b * KF + f
                        if n:
                            pe.wait_ge(s_lin, n)
                            pe.wait_ge(s_silu, n)
                        for s_, bk in ((0, 4), (1, 5)):
                            for k in range(KD):
                                last = nc.tensor.matmul(bank[bk][:], sw1[:, k, s_ * FFN + f * P:s_ * FFN + (f + 1) * P],
                                                        hist[:, k, b], start=(k == 0), stop=(k == KD - 1))
                            last.then_inc(s_up, 1)
                    for d in range(KD):
                        if b:
                            pe.wait_ge(s_base, (b - 1) * KD + d + 1)
                        for f in range(KF):
                            if d == 0:
                                pe.wait_ge(s_act, b * KF + f + 1)
                            last = nc.tensor.matmul(bank[6 + d][:], sw2[:, f, d * P:(d + 1) * P], act_f[:, f],
                                                    start=(f == 0), stop=(f == KF - 1))
                        last.then_inc(s_dp, 1)
                    if b == 1:
                        pe.wait_ge(s_off, 1)
                        nc.tensor.matmul(bank[2][:, 0:1], shift[:], cum[:, TH - 1:TH], start=True, stop=True).then_inc(s_off, 1)
                for i in range(TILES):
                    b, o = i * P // S, i * P % S
                    if i == 0:
                        pe.wait_ge(s_rc, TILES)
                    if i % (S // P) == 0:
                        pe.wait_ge(s_sum, b + 1)
                    if i >= 2:
                        pe.wait_ge(s_bc, i - 1)
                    for k in range(KD):
                        last = nc.tensor.transpose(bank[4 + i % 2][:, k * P:(k + 1) * P], xT[:, k, b, o:o + P], ident[:])
                    last.then_inc(s_bt, 1)
                pe.wait_ge(s_ot, 1)
                nc.tensor.transpose(bank[0][:, 0:P], order[:, 1, 0:P], ident[:])
                nc.tensor.transpose(bank[1][0:CAP - P, 0:P], order[:, 1, P:CAP], ident[:]).then_inc(s_ot, 1)

            @block.scalar
            def _(act):
                act.wait_ge(s_c, 2)
                nc.scalar.activation(gates[:].rearrange("p t e -> p (t e)"), left[:].rearrange("p t e -> p (t e)"), ACT.Exp).then_inc(s_ex, 1)
                for i in range(TILES):
                    act.wait_ge(s_rt, i + 1)
                    nc.scalar.activation(rows[:, i, 0:D], bank[2 + i % 2][:, 0:D], ACT.Copy).then_inc(s_rc, 1)
                for b in range(B):
                    for f in range(KF):
                        n = b * KF + f
                        act.wait_ge(s_up, 2 * n + 1)
                        if n >= 2:
                            act.wait_ge(s_act, n - 1)
                        nc.scalar.activation(lin[:, n % 2], bank[4][:], ACT.Copy).then_inc(s_lin, 1)
                        act.wait_ge(s_up, 2 * n + 2)
                        nc.scalar.activation(act_f[:, f], bank[5][:], ACT.Silu).then_inc(s_silu, 1)
                    for d in range(KD):
                        act.wait_ge(s_dp, b * KD + d + 1)
                        act.wait_ge(s_act, (b + 1) * KF)
                        nc.scalar.activation(hist[:, d, b], bank[6 + d][:], ACT.Copy).then_inc(s_base, 1)
                for i in range(TILES):
                    act.wait_ge(s_bt, i + 1)
                    if i >= 2:
                        act.wait_ge(s_out[i % 2], 16 * (i // 2))
                    nc.scalar.activation(orow[:, i % 2], bank[4 + i % 2][:, 0:D], ACT.Copy).then_inc(s_bc, 1)

            @block.gpsimd
            def _(pool):
                nc.gpsimd.memset(cum[:, 0:ROW], 0.0).then_inc(s_z, 1)
                for b in range(B):
                    for f in range(KF):
                        n = b * KF + f
                        pool.wait_ge(s_silu, n + 1)
                        pool.wait_ge(s_lin, n + 1)
                        nc.gpsimd.tensor_tensor(act_f[:, f], act_f[:, f], lin[:, n % 2], ALU.mult).then_inc(s_act, 1)
                    pool.wait_ge(s_base, (b + 1) * KD)
                    nc.gpsimd.tensor_tensor(xT[:, :, b, 0:S], xT[:, :, b, 0:S], hist[:, :, b], ALU.add).then_inc(s_sum, 1)

            @block.vector
            def _(dve):
                g = [0]

                def chain(ins):
                    g[0] += 1
                    ins.then_inc(s_c, 1)
                    dve.wait_ge(s_c, g[0])

                def spread(col):
                    return st[:, col, :].unsqueeze(2).to_broadcast([P, TILES, NE])

                dve.wait_ge(s_lp, 1)
                for i in range(2):
                    last = nc.vector.tensor_reduce(st[:, 0, 8 * i:8 * i + 8], bank[i][:].rearrange("p (t e) -> p t e", e=NE), AX.X, ALU.max)
                chain(last)
                for i in range(2):
                    last = nc.vector.tensor_tensor(left[:, 8 * i:8 * i + 8], bank[i][:].rearrange("p (t e) -> p t e", e=NE),
                                                   st[:, 0, 8 * i:8 * i + 8].unsqueeze(2).to_broadcast([P, 8, NE]), ALU.subtract)
                chain(last)
                dve.wait_ge(s_ex, 1)
                chain(nc.vector.tensor_reduce(st[:, 1], gates[:], AX.X, ALU.add))
                chain(nc.vector.reciprocal(st[:, 2], st[:, 1]))
                chain(nc.vector.tensor_tensor(gates[:], gates[:], spread(2), ALU.mult))
                for i in range(TILES):
                    last = nc.vector.max(top8[:, i], gates[:, i])
                chain(last)
                for i in range(TILES):
                    last = nc.vector.match_replace(left[:, i], top8[:, i], gates[:, i], -1.0)
                chain(last)
                nc.vector.tensor_reduce(st[:, 0], top8[:], AX.X, ALU.add)
                chain(nc.vector.tensor_scalar(left[:], left[:], 0.0, None, ALU.is_lt))
                chain(nc.vector.tensor_scalar(st[:, 1], st[:, 0], EPS, None, ALU.max))
                chain(nc.vector.reciprocal(st[:, 3], st[:, 1]))
                chain(nc.vector.tensor_tensor(gates[:], gates[:], left[:], ALU.mult))
                nc.vector.tensor_tensor(rows[:, :, D:], gates[:], spread(3), ALU.mult).then_inc(s_dense, 1)
                dve.wait_ge(s_mt, 1)
                for i in range(2):
                    last = nc.vector.tensor_copy(maskT[:, 512 * i:512 * i + 512], bank[i][:])
                chain(last)
                dve.wait_ge(s_z, 2)
                chain(nc.vector.tensor_tensor_scan(cum[:], ones[:, 0:1].to_broadcast([P, TH]), maskT, 0.0, ALU.mult, ALU.add))
                dve.sem_inc(s_off, 1)
                dve.wait_ge(s_off, 2)
                chain(nc.vector.tensor_copy(before[:], bank[2][:, 0:1]))
                chain(nc.vector.tensor_scalar(cum[:], cum[:], before[:, 0:1], float(CAP), ALU.add, ALU.is_le))
                chain(nc.vector.tensor_tensor(cum[:], cum[:], maskT, ALU.mult))
                chain(nc.vector.tensor_tensor(cum[:], cum[:], vrev[:], ALU.mult))
                for i in range(ROUNDS):
                    top = order[:, 0, 8 * i:8 * i + 8]
                    chain(nc.vector.max(top, cum[:]))
                    chain(nc.vector.match_replace(cum[:], top, cum[:], 0.0))
                nc.vector.tensor_copy(order[0:NE, 1, :], order[0:NE, 0, :])
                chain(nc.vector.tensor_copy(order[NE:P, 1, :], order[NE:P, 0, ::-1]))
                dve.sem_inc(s_ot, 1)
                dve.wait_ge(s_ot, 2)
                for c, (a, z) in enumerate(CAPS):
                    n = z - a
                    chain(nc.vector.tensor_copy(slots[0:n, 0], bank[c][0:n, 0:NE]))
                    chain(nc.vector.tensor_tensor(slots[0:n, 1], slots[0:n, 0], bank[c][0:n, NE:P], ALU.max))
                    chain(nc.vector.tensor_scalar(slots[0:n, 2], slots[0:n, 1], 0.0, None, ALU.is_equal))
                    chain(nc.vector.tensor_scalar(slots[0:n, 1], slots[0:n, 1], -1.0, float(T), ALU.mult, ALU.add))
                    chain(nc.vector.tensor_scalar(slots[0:n, 2], slots[0:n, 2], slot_row[0:n, c:c + 1], None, ALU.mult))
                    chain(nc.vector.tensor_tensor(tok[c][:], slots[0:n, 1], slots[0:n, 2], ALU.add))
    return (tok,)


def experts(nc, sb, sem, A, bank, ident, arena, ctx_rows, out, tok):
    UP = KD * 2 * FFN
    w1 = [arena[:, i * WROW:i * WROW + UP].rearrange("p (k f) -> p k f", k=KD) for i in range(RING)]
    w2 = [arena[:, i * WROW + UP:(i + 1) * WROW].rearrange("p (f d) -> p f d", f=KF) for i in range(RING)]
    with ExitStack() as own:
        def t(name, shape, dt=F32):
            return own.enter_context(nc.sbuf_tensor(name, shape, dt))

        got = [[t(f"got{q}{c}", [z - a, ROW]) for c, (a, z) in enumerate(CAPS)] for q in range(RING)]
        idx = [[t(f"row{q}{c}", [z - a, 1], U32) for c, (a, z) in enumerate(CAPS)] for q in range(RING)]
        xe = [t(f"xe{q}", [P, KD, CAP]) for q in range(2)]
        gate = t("gate_f", [P, 2, CAP])
        mid = [t(f"mid{q}", [P, KF, CAP]) for q in range(2)]
        ye = [t(f"ye{q}", [P, KD, CAP]) for q in range(2)]
        res = [[t(f"res{q}{c}", [z - a, D]) for c, (a, z) in enumerate(CAPS)] for q in range(2)]

        s_w = [sem(f"weights{q}") for q in range(RING)]
        s_got = [sem(f"gathered{q}") for q in range(RING)]
        s_idx = sem("rows_named")
        s_pass = sem("waits_passed")
        s_xt, s_xe = sem("tokens_turned"), sem("tokens_copied")
        s_up, s_silu, s_mid = sem("pair_pre"), sem("pair_silu"), sem("pair_done")
        s_y, s_ye = sem("down_pre"), sem("down_copied")
        s_yt, s_res, s_add = sem("down_turned"), sem("weighted"), sem("added")

        def wait(eng, s, n):
            if not isinstance(n, int) or n > 0:
                eng.wait_ge(s, n)

        def run(eng, body):
            for u in range(RING):
                body(u, u)
            with eng.Fori(1, NE // RING - 1) as i:
                for u in range(RING):
                    body(i * RING + u, u)
            for u in range(RING):
                body(NE - RING + u, u)

        def first(e):
            return isinstance(e, int) and e == 0

        def past(e, n):
            return isinstance(e, int) and e + n >= NE

        def uses(e, u):
            return e - u + RING

        with nc.Block() as block:
            @block.sync
            def _(sp):
                def load(e, u):
                    wait(sp, s_y, e - RING + 1)
                    src = A["ew"][e] if isinstance(e, int) else A["ew"][bass.ds(e, 1)].rearrange("o p n -> p (o n)")
                    sp.dma_start(arena[:, u * WROW:(u + 1) * WROW], src).then_inc(s_w[u], 16)

                run(sp, load)

            @block.gpsimd
            def _(pool):
                def gather(e, u):
                    for c in range(2):
                        nc.gpsimd.tensor_copy(idx[u][c][:], tok[c][:, e:e + 1] if isinstance(e, int) else tok[c][:, bass.ds(e, 1)])\
                            .then_inc(s_idx, 1)
                    pool.wait_ge(s_idx, e * 2 + 2)
                    pool.sem_inc(s_pass, 1)
                    for c in range(2):
                        nc.gpsimd.indirect_dma_start(
                            out=got[u][c][:], out_offset=None, in_=ctx_rows[:, :],
                            in_offset=bass.IndirectOffsetOnAxis(ap=idx[u][c][:, 0:1], axis=0)).then_inc(s_got[u], 16)

                def add(e, u):
                    pool.wait_ge(s_res, e + 1)
                    wait(pool, s_add, e * 32)
                    pool.sem_inc(s_pass, 1)
                    for c in range(2):
                        nc.gpsimd.indirect_dma_start(
                            out=out[:, :], out_offset=bass.IndirectOffsetOnAxis(ap=idx[u][c][:, 0:1], axis=0),
                            in_=res[u % 2][c][:], in_offset=None, compute_op=ALU.add).then_inc(s_add, 16)

                def body(e, u):
                    if not first(e):
                        add(e - 1, (u - 1) % RING)
                    if not past(e, 2):
                        wait(pool, s_add, (e - 1) * 32)
                        gather(e + 2, (u + 2) % RING)

                gather(0, 0)
                gather(1, 1)
                run(pool, body)
                add(NE - 1, RING - 1)
                pool.wait_ge(s_add, NE * 32)

            @block.tensor
            def _(pe):
                def turn_in(e, u):
                    pe.wait_ge(s_got[u], uses(e, u) * (32 // RING))
                    wait(pe, s_xe, e)
                    for c, (a, z) in enumerate(CAPS):
                        for k in range(KD):
                            last = nc.tensor.transpose(bank[7][:, k * CAP + a:k * CAP + z], got[u][c][:, k * P:(k + 1) * P],
                                                       ident[0:z - a, 0:z - a])
                    last.then_inc(s_xt, 1)

                def turn_out(e, u):
                    pe.wait_ge(s_ye, e + 1)
                    wait(pe, s_res, e)
                    for c, (a, z) in enumerate(CAPS):
                        for k in range(KD):
                            last = nc.tensor.transpose(bank[6][0:z - a, c * D + k * P:c * D + (k + 1) * P], ye[u % 2][:, k, a:z], ident[:])
                    last.then_inc(s_yt, 1)

                def body(e, u):
                    pe.wait_ge(s_w[u], uses(e, u) * (16 // RING))
                    pe.wait_ge(s_xe, e + 1)
                    for f in range(KF):
                        wait(pe, s_mid, e * KF + (f - 2))
                        for s_ in range(2):
                            for k in range(KD):
                                last = nc.tensor.matmul(bank[f % 3][:, s_ * CAP:(s_ + 1) * CAP],
                                                        w1[u][:, k, s_ * FFN + f * P:s_ * FFN + (f + 1) * P], xe[u % 2][:, k],
                                                        start=(k == 0), stop=(k == KD - 1))
                        last.then_inc(s_up, 1)
                    if not first(e):
                        turn_out(e - 1, (u - 1) % RING)
                    if not past(e, 1):
                        turn_in(e + 1, (u + 1) % RING)
                    for d in range(KD):
                        for f in range(KF):
                            if d == 0:
                                pe.wait_ge(s_mid, e * KF + (f + 1))
                            last = nc.tensor.matmul(bank[4 + u % 2][:, d * CAP:(d + 1) * CAP], w2[u][:, f, d * P:(d + 1) * P], mid[u % 2][:, f],
                                                    start=(f == 0), stop=(f == KF - 1))
                    last.then_inc(s_y, 1)

                turn_in(0, 0)
                run(pe, body)
                turn_out(NE - 1, RING - 1)

            @block.scalar
            def _(act):
                def copy_in(e, u):
                    act.wait_ge(s_xt, e + 1)
                    nc.scalar.activation(xe[u % 2][:].rearrange("p k t -> p (k t)"), bank[7][:, 0:KD * CAP], ACT.Copy).then_inc(s_xe, 1)

                def body(e, u):
                    for f in range(KF):
                        act.wait_ge(s_up, e * KF + (f + 1))
                        wait(act, s_mid, e * KF + (f - 1))
                        nc.scalar.activation(gate[:, f % 2], bank[f % 3][:, CAP:2 * CAP], ACT.Silu).then_inc(s_silu, 1)
                    if not past(e, 1):
                        copy_in(e + 1, (u + 1) % RING)
                    act.wait_ge(s_y, e + 1)
                    nc.scalar.activation(ye[u % 2][:].rearrange("p k t -> p (k t)"), bank[4 + u % 2][:, 0:KD * CAP], ACT.Copy).then_inc(s_ye, 1)

                copy_in(0, 0)
                run(act, body)

            @block.vector
            def _(dve):
                def weigh(e, u):
                    dve.wait_ge(s_yt, e + 1)
                    wait(dve, s_add, e * 32 - 32)
                    dve.wait_ge(s_got[u], uses(e, u) * (32 // RING))
                    for c, (a, z) in enumerate(CAPS):
                        col = got[u][c][:, D + e:D + e + 1] if isinstance(e, int) else got[u][c][:, bass.ds(e + D, 1)]
                        last = nc.vector.tensor_scalar(res[u % 2][c][:], bank[6][0:z - a, c * D:(c + 1) * D], col, None, ALU.mult)
                    last.then_inc(s_res, 1)

                def body(e, u):
                    for f in range(KF):
                        dve.wait_ge(s_silu, e * KF + (f + 1))
                        nc.vector.tensor_tensor(mid[u % 2][:, f], bank[f % 3][:, 0:CAP], gate[:, f % 2], ALU.mult).then_inc(s_mid, 1)
                    if not first(e):
                        weigh(e - 1, (u - 1) % RING)

                run(dve, body)
                weigh(NE - 1, RING - 1)


def _layout(inputs):
    def f(name):
        return np.asarray(inputs[name])

    a = {k: f(k) for k in inputs if k.startswith("L0_") or k.startswith("L1_cond")}
    for n in ("L0_ffn_w_r", "L0_ffn_b1", "L0_ffn_b2", "L1_cond_sb1", "L1_cond_sb2"):
        a[n] = a[n].reshape(-1, P).T
    for n in ("L1_cond_eb1", "L1_cond_eb2"):
        a[n] = a[n].reshape(NE0, -1, P).transpose(0, 2, 1)
    a["xT"] = f("x").reshape(T, D).T
    a["condT"] = f("cond_1024").T
    a["wgT"] = f("L1_ffn_wg").T
    a["sw1T"] = f("L1_ffn_shared_w1").T
    a["sw2T"] = f("L1_ffn_shared_w2").T
    up = f("L1_ffn_expert_w1").transpose(0, 2, 1).reshape(NE, KD, P, 2 * FFN).transpose(0, 2, 1, 3).reshape(NE, P, -1)
    down = f("L1_ffn_expert_w2").transpose(0, 2, 1).reshape(NE, KF, P, D).transpose(0, 2, 1, 3).reshape(NE, P, -1)
    a["ew"] = np.concatenate([up, down], axis=2)
    a["ident"] = np.eye(P, dtype=np.float32)
    a["which"] = np.tile(np.eye(B, dtype=np.float32), (1, SEG))
    a["shift"] = np.eye(P, k=NE, dtype=np.float32)
    half = np.arange(T // 2, dtype=np.float32)
    a["vrev"] = np.repeat(np.stack([T - half, T // 2 - half]), NE, axis=0).astype(np.float32)
    a["slot_row"] = np.stack([np.arange(P), np.arange(P, 2 * P)], axis=1).astype(np.float32)
    return {k: np.ascontiguousarray(v) for k, v in a.items()}


def kernel(**inputs):
    import concourse.bacc as bacc
    from concourse.bass_utils import run_bass_kernel_spmd

    nc = bacc.Bacc("TRN2", target_bir_lowering=False, num_devices=1)
    arrays = {f"in_{k}": v for k, v in _layout(inputs).items()}
    A = {k[3:]: nc.dram_tensor(k, v.shape, mybir.dt.from_np(v.dtype), kind="ExternalInput").ap() for k, v in arrays.items()}
    out = nc.dram_tensor("out_rows", (T + CAP, D), F32, kind="ExternalOutput").ap()
    program(nc, A, out)
    r = run_bass_kernel_spmd(nc, [arrays], core_ids=[0])
    return r.results[0]["out_rows"][0:T].reshape(B, S, D)
```

```python
from contextlib import ExitStack

import numpy as np
import concourse.bass as bass
from concourse import mybir

F32 = mybir.dt.float32
BF16 = mybir.dt.bfloat16
F16 = mybir.dt.float16
F32R = mybir.dt.float32r
U32 = mybir.dt.uint32
ALU = mybir.AluOpType
ACT = mybir.ActivationFunctionType
AX = mybir.AxisListType

P = 128
B, S, D = 4, 512, 256
KD = D // P
T = B * S
HID = 1024
KH = HID // P
GATES = 3
PARTS = 3
SEG = 16
SELECT = S // 2
NE0, TOP0 = 4, 2
REGIONS = ((0, 170), (170, 340), (340, 512))
NE, TOPK, FFN, CAP = 64, 8, 768, 160
KF = FFN // P
TILES = T // P
HALF = TILES // 2
ROW = P + NE + P
CAPS = ((0, P), (P, CAP))
WROW = KD * 2 * FFN + KF * D
ROUNDS = CAP // 8
RING = 4
EPS = float(np.finfo(np.float32).eps)
MEET = ((0, 0), (1, 0), (0, 1))


def program(nc, A, out):
    with ExitStack() as ctx:
        def sb(name, shape, dt=F32):
            return ctx.enter_context(nc.sbuf_tensor(name, shape, dt))

        def sem(name):
            return ctx.enter_context(nc.semaphore(name))

        bank = [ctx.enter_context(nc.psum_tensor(f"bank{i}", [P, 512], F32)) for i in range(8)]
        ctx_rows = nc.dram_tensor("ctx_rows", [T + CAP, ROW], F32, kind="Internal").ap()

        xT = sb("xT", [P, KD, B, S + SEG])
        hist = sb("hist", [P, KD, B, S])
        ident = sb("ident", [P, P])
        ones = sb("ones", [P, P])
        ones_bf = sb("ones_bf", [P, P], BF16)
        condT = sb("condT", [P, KD, B])
        slot_row = sb("slot_row", [P, 2])
        FF = KD * HID + KH * D
        dense_w = sb("dense_w", [P, max(FF, WROW)])
        raw = sb("raw", [P, FF])

        def cut(at, *shape):
            n = int(np.prod(shape))
            return dense_w[:, at:at + n].rearrange("p (a b) -> p a b", a=shape[0])

        wr, br = sb("wr", [P, KD]), sb("br", [P, 1])
        b1, b2 = sb("b1", [P, KH]), sb("b2", [P, KD])
        W1, W2 = cut(0, KD, HID), cut(KD * HID, KH, D)
        s_ffn = sem("ffn_weights_loaded")

        def load_ffn(eng):
            eng.dma_start(wr[:], A["L0_ffn_w_r"]).then_inc(s_ffn, 16)
            eng.dma_start(br[:], A["L0_ffn_b_r"].rearrange("(a o) -> a o", a=1).to_broadcast([P, 1])).then_inc(s_ffn, 16)
            eng.dma_start(b1[:], A["L0_ffn_b1"]).then_inc(s_ffn, 16)
            eng.dma_start(b2[:], A["L0_ffn_b2"]).then_inc(s_ffn, 16)
            eng.dma_start(W1, A["L0_ffn_W1"].rearrange("(k p) f -> p k f", p=P)).then_inc(s_ffn, 16)
            eng.dma_start(W2, A["L0_ffn_W2"].rearrange("(f p) d -> p f d", p=P)).then_inc(s_ffn, 16)

        s_x = sem("x_loaded")
        s_const = sem("const_loaded")
        gru(nc, sb, sem, A, bank, xT, hist, ident, ones, ones_bf, condT, slot_row, s_x, s_const, load_ffn)

        gw, gb = sb("gw", [P, 3 * KD, NE0]), sb("gb", [1, NE0])
        tw, tb = sb("tw", [P, KD, 2 * NE0]), sb("tb", [1, 2 * NE0])
        eb1, eb2 = sb("eb1", [P, 1 + TOP0, KH]), sb("eb2", [P, 1 + TOP0, KD])
        s_gate, s_shared = sem("gate_weights_loaded"), sem("shared_loaded")

        def load_gate(eng):
            eng.dma_start(gw[:], A["L1_cond_gate_w"].rearrange("(c p) e -> p c e", p=P)).then_inc(s_gate, 16)
            eng.dma_start(gb[:], A["L1_cond_gate_b"].rearrange("(a e) -> a e", a=1)).then_inc(s_gate, 16)
            eng.dma_start(tw[:], A["L1_cond_time_w"].rearrange("(k p) e -> p k e", p=P)).then_inc(s_gate, 16)
            eng.dma_start(tb[:], A["L1_cond_time_b"].rearrange("(a e) -> a e", a=1)).then_inc(s_gate, 16)
            eng.dma_start(raw[:, 0:KD * HID].rearrange("p (k f) -> p k f", k=KD),
                          A["L1_cond_sw1"].rearrange("(k p) f -> p k f", p=P)).then_inc(s_shared, 16)
            eng.dma_start(raw[:, KD * HID:].rearrange("p (f d) -> p f d", f=KH),
                          A["L1_cond_sw2"].rearrange("(f p) d -> p f d", p=P)).then_inc(s_shared, 16)
            eng.dma_start(eb1[:, 0], A["L1_cond_sb1"]).then_inc(s_shared, 16)
            eng.dma_start(eb2[:, 0], A["L1_cond_sb2"]).then_inc(s_shared, 16)

        turn = sb("turn", [P, KD, P + NE])
        sw1, sw2 = cut(0, KD, 2 * FFN), cut(KD * 2 * FFN, KF, D)
        s_wg, s_sw = sem("router_loaded"), sem("shared_expert_loaded")

        def load_router(eng):
            eng.dma_start(turn[:], A["turn"]).then_inc(s_wg, 16)
            eng.dma_start(sw1, A["sw1T"].rearrange("(k p) f -> p k f", p=P)).then_inc(s_sw, 16)
            eng.dma_start(sw2, A["sw2T"].rearrange("(f p) d -> p f d", p=P)).then_inc(s_sw, 16)

        with ExitStack() as dense:
            parts = [[dense.enter_context(nc.sbuf_tensor(f"weights{q}_part{p}", [P, FF], F32R)) for p in range(2)] for q in range(2)]
            layer0_ffn(nc, sb, sem, bank, xT, hist, ident, ones_bf, (wr, br, b1, b2, W1, W2), s_ffn, load_gate,
                       s_shared, raw, parts[0])
            layer1_context(nc, sb, sem, A, bank, xT, hist, ident, ones, condT, (gw, gb, tw, tb, eb1, eb2),
                           raw, parts, s_gate, load_router)

        arena = sb("arena", [P, RING * WROW])
        s_ew = [sem(f"weights{q}") for q in range(RING)]

        def load_experts(eng):
            for u in range(RING):
                eng.dma_start(arena[:, u * WROW:(u + 1) * WROW], A["ew"][u]).then_inc(s_ew[u], 16)

        tok = routing(nc, sb, sem, A, bank, xT, hist, ident, ones, slot_row, (turn, sw1, sw2), raw[:].rearrange("p (n s) -> p n s", s=S),
                      s_wg, s_sw, load_experts, ctx_rows, out)
        experts(nc, sb, sem, A, bank, ident, arena, s_ew, ctx_rows, out, tok)


def gru(nc, sb, sem, A, bank, xT, hist, ident, ones, ones_bf, condT, slot_row, s_x, s_const, load_next):
    with ExitStack() as own:
        def t(name, shape, dt=F32):
            return own.enter_context(nc.sbuf_tensor(name, shape, dt))

        EARLY = 4 * SEG
        C2 = KD * B
        TOP_EXP = 14
        EXP_BITS, BIAS, MANTISSA = 0x7f800000, 127, 23
        U = t("U", [P, GATES, KD, D])
        W = t("W", [P, GATES, KD, D])
        rest = t("rest", [P, GATES, KD, D])
        Us = t("Us", [P, GATES, 2, KD, D], F16)
        Ws = t("Ws", [P, GATES, PARTS, KD, D], BF16)
        xs = t("xs", [P, PARTS, KD, B, S + SEG], BF16)
        x_rest = t("x_rest", [P, KD, B, S + SEG])
        C = t("C", [P, GATES, KD, D])
        bias = t("bias", [1, GATES, D])
        vb = t("vb", [B, GATES, D])
        vb_rest = t("vb_rest", [B, GATES, D])
        vbs = t("vbs", [B, PARTS, GATES, D], BF16)
        which = t("which", [B, SEG * B])
        which_bf = t("which_bf", [B, SEG * B], BF16)
        peak = t("peak", [P, GATES])
        peaks = t("peaks", [GATES, 4])
        scales = t("scales", [GATES, 2 * GATES])
        scale = t("scale", [P, 2 * GATES + 1])
        ring = t("ring", [P, 2 * SEG + 1, C2])
        nz, keep, step_in = t("nz", [P, C2]), t("keep", [P, C2]), t("step_in", [P, C2])
        h_part, keep_part = t("h_part", [P, 2, C2], F16), t("keep_part", [P, 2, C2], F16)
        r_h, z_cand = t("r_h", [P, C2, 3]), t("z_cand", [P, C2, 3])
        rh_high, step_high = t("rh_high", [P, C2, 3], F16), t("step_high", [P, C2, 3], F16)
        rh_low, step_low = t("rh_low", [P, C2, 3], F16), t("step_low", [P, C2, 3], F16)
        r, z, cand = r_h[:, :, 1], z_cand[:, :, 1], z_cand[:, :, 2]

        s_w, s_cw, s_uw = sem("input_weights_loaded"), sem("cond_weights_loaded"), sem("recurrent_loaded")
        s_ws, s_us, s_vs = sem("input_weights_split"), sem("recurrent_split"), sem("cond_term_split")
        s_xs, s_xl = sem("early_inputs_split"), sem("late_inputs_split")
        s_v, s_vb = sem("cond_term"), sem("cond_term_copied")
        s_one = sem("ones_set")
        s_peak, s_pt, s_sc = sem("peaks_found"), sem("scale_products"), sem("scale_chain")
        s_scale, s_wsc = sem("scale_spread"), sem("input_weights_scaled")
        s_hhi, s_hlo, s_h, s_hr = sem("h_hi"), sem("h_lo"), sem("h_full"), sem("h_beside_r")
        s_rp, s_zp, s_cp = sem("r_pre"), sem("z_pre"), sem("cand_pre")
        s_r, s_z, s_nz, s_c = sem("r_done"), sem("z_done"), sem("one_less_z_done"), sem("cand_done")
        s_rhhi, s_rhlo = sem("rh_hi"), sem("rh_lo")
        s_khi, s_klo, s_k = sem("keep_hi"), sem("keep_lo"), sem("keep_full")
        s_shi, s_slo, s_s = sem("step_hi"), sem("step_lo"), sem("step_full")
        s_carry = sem("carried")
        s_zero = sem("factors_set")
        s_hist = sem("hist_copied")

        names = (("W_r", "U_r", "C_r", "b_r"), ("W_z", "U_z", "C_z", "b_z"), ("W", "U", "C", "b"))
        PART_OF = ((0, 1), (0,))
        PAIRS = ((0, 0), (0, 1), (1, 0), (0, 2), (1, 1), (2, 0))
        pre = [[bank[2 * g + q][:, 0:SEG * C2].rearrange("p (t m b) -> p t m b", t=SEG, m=KD)
                for q in range(2)] for g in range(GATES)]

        def pre_of(g, q, jj):
            return pre[g][q][:, jj].rearrange("p m b -> p (m b)")

        with nc.Block() as block:
            @block.sync
            def _(sp):
                for g, (w, u, c, b) in enumerate(names):
                    sp.dma_start(U[:, g], A["L0_cond_" + u].rearrange("(k p) e -> p k e", p=P)).then_inc(s_uw, 16)
                for g, (w, u, c, b) in enumerate(names):
                    sp.dma_start(W[:, g], A["L0_cond_" + w].rearrange("(k p) e -> p k e", p=P)).then_inc(s_w, 16)
                for g, (w, u, c, b) in enumerate(names):
                    sp.dma_start(C[:, g], A["L0_cond_" + c].rearrange("(k p) e -> p k e", p=P)).then_inc(s_cw, 16)
                    sp.dma_start(bias[:, g, :], A["L0_cond_" + b].rearrange("(a e) -> a e", a=1)).then_inc(s_cw, 16)
                sp.dma_start(condT[:], A["condT"].rearrange("(k p) b -> p k b", p=P)).then_inc(s_cw, 16)
                sp.dma_start(which[:], A["which"]).then_inc(s_cw, 16)
                load_next(sp)

            @block.scalar
            def _(act):
                for k in range(KD):
                    act.dma_start(xT[:, k, :, 0:S],
                                  A["xT"][k * P:(k + 1) * P, :].rearrange("p (b s) -> p b s", b=B)).then_inc(s_x, 16)
                act.dma_start(ident[:], A["ident"]).then_inc(s_const, 16)
                act.dma_start(slot_row[:], A["slot_row"]).then_inc(s_const, 16)
                nc.scalar.preload_act_table(ACT.Sigmoid)
                act.wait_ge(s_v, 1)
                nc.scalar.activation(vb[:, 0:2].rearrange("p g e -> p (g e)"), bank[6][0:B, :], ACT.Copy)
                nc.scalar.activation(vb[:, 2], bank[7][0:B, 0:D], ACT.Copy).then_inc(s_vb, 1)
                act.wait_ge(s_scale, 2)
                inv = [act.alloc_register(f"inverse_scale{c}") for c in range(GATES + 1)]
                for c in range(GATES + 1):
                    act.reg_load(inv[c], scale[0:1, GATES + c:GATES + c + 1].bitcast(U32))
                with act.Fori(0, S // (2 * SEG)) as i:
                    n = i * (2 * SEG)
                    for j in range(2 * SEG):
                        q, jj = j // SEG, j % SEG
                        act.wait_ge(s_rp, n + (j + 1))
                        nc.scalar.activation(r, pre_of(0, q, jj), ACT.Sigmoid, scale=inv[0]).then_inc(s_r, 1)
                        act.wait_ge(s_zp, n + (j + 1))
                        nc.scalar.activation(nz[:], pre_of(1, q, jj), ACT.Sigmoid, scale=inv[3]).then_inc(s_nz, 1)
                        nc.scalar.activation(z, pre_of(1, q, jj), ACT.Sigmoid, scale=inv[1]).then_inc(s_z, 1)
                        act.wait_ge(s_cp, n + (j + 1))
                        nc.scalar.activation(cand, pre_of(2, q, jj), ACT.Tanh, scale=inv[2]).then_inc(s_c, 1)

            @block.gpsimd
            def _(pool):
                nc.gpsimd.memset(xT[:, :, :, S:S + SEG], 0.0).then_inc(s_one, 1)
                nc.gpsimd.memset(ones[:], 1.0).then_inc(s_one, 1)
                nc.gpsimd.memset(ones_bf[:], 1.0).then_inc(s_one, 1)
                pool.wait_ge(s_x, 32)
                pool.wait_ge(s_one, 1)
                x, left = xT[:, :, :, EARLY:], x_rest[:, :, :, EARLY:]
                part = [xs[:, p, :, :, EARLY:] for p in range(PARTS)]
                for k in range(KD):
                    nc.gpsimd.tensor_copy(part[0][:, k], x[:, k]).then_inc(s_xl, 1)
                pool.wait_ge(s_xl, KD)
                for k in range(KD):
                    nc.gpsimd.tensor_tensor(left[:, k], x[:, k], part[0][:, k], ALU.subtract).then_inc(s_xl, 1)
                pool.wait_ge(s_xl, 2 * KD)
                for k in range(KD):
                    nc.gpsimd.tensor_copy(part[1][:, k], left[:, k]).then_inc(s_xl, 1)
                pool.wait_ge(s_xl, 3 * KD)
                for k in range(KD):
                    nc.gpsimd.tensor_tensor(part[2][:, k], left[:, k], part[1][:, k], ALU.subtract).then_inc(s_xl, 1)
                pool.sem_inc(s_hist, 2)
                with pool.Fori(0, S // (2 * SEG)) as i:
                    n = i * (2 * SEG)
                    for q in range(2):
                        pool.wait_ge(s_h, n + (q * SEG + SEG + 1))
                        nc.gpsimd.tensor_copy(
                            hist[:, :, :, bass.ds(n + q * SEG, SEG)].rearrange("p k b t -> p (k b) t"),
                            ring[:, 1 + q * SEG:1 + q * SEG + SEG, :].rearrange("p t c -> p c t")).then_inc(s_hist, 1)

            @block.vector
            def _(dve):
                def split(parts, src, left, done):
                    nc.vector.tensor_copy(parts[0], src).then_inc(done, 1)
                    dve.wait_ge(done, 1)
                    nc.vector.tensor_tensor(left, src, parts[0], ALU.subtract).then_inc(done, 1)
                    dve.wait_ge(done, 2)
                    nc.vector.tensor_copy(parts[1], left).then_inc(done, 1)
                    dve.wait_ge(done, 3)
                    nc.vector.tensor_tensor(parts[2], left, parts[1], ALU.subtract).then_inc(done, 1)
                    dve.wait_ge(done, 4)

                dve.wait_ge(s_uw, 16 * GATES)
                for g in range(GATES):
                    last = nc.vector.tensor_reduce(peak[:, g:g + 1], U[:, g].rearrange("p k e -> p (k e)"), AX.X, ALU.max,
                                                   apply_absolute_value=True)
                last.then_inc(s_peak, 1)
                dve.wait_ge(s_pt, 1)
                nc.vector.tensor_reduce(peaks[:, 0:1], bank[5][0:GATES, 0:P], AX.X, ALU.max).then_inc(s_sc, 1)
                dve.wait_ge(s_sc, 1)
                nc.vector.tensor_scalar(peaks[:, 0:1], peaks[:, 0:1], 1e-20, None, ALU.max).then_inc(s_sc, 1)
                dve.wait_ge(s_sc, 2)
                bits = peaks[:].bitcast(U32)
                nc.vector.tensor_scalar(bits[:, 1:2], bits[:, 0:1], EXP_BITS, None, ALU.bitwise_and).then_inc(s_sc, 1)
                dve.wait_ge(s_sc, 3)
                nc.vector.tensor_scalar(bits[:, 2:3], bits[:, 1:2], -1.0, float((2 * BIAS + TOP_EXP) << MANTISSA),
                                        ALU.mult, ALU.add)
                nc.vector.tensor_scalar(bits[:, 3:4], bits[:, 1:2], float(TOP_EXP << MANTISSA), None,
                                        ALU.subtract).then_inc(s_sc, 1)
                dve.wait_ge(s_sc, 4)
                dve.wait_ge(s_const, 32)
                for c in range(2):
                    last = nc.vector.tensor_scalar(scales[:, c * GATES:(c + 1) * GATES], ident[0:GATES, 0:GATES],
                                                   peaks[:, 2 + c:3 + c], None, ALU.mult)
                last.then_inc(s_sc, 1)
                dve.wait_ge(s_pt, 2)
                nc.vector.tensor_copy(scale[:, 0:2 * GATES], bank[3][:, 0:2 * GATES]).then_inc(s_scale, 1)
                dve.wait_ge(s_scale, 1)
                nc.vector.tensor_scalar(scale[:, 2 * GATES:], scale[:, GATES + 1:GATES + 2], -1.0, None, ALU.mult).then_inc(s_scale, 1)
                dve.wait_ge(s_w, 16 * GATES)
                for g in range(GATES):
                    last = nc.vector.tensor_scalar(W[:, g], W[:, g], scale[:, g:g + 1], None, ALU.mult)
                last.then_inc(s_wsc, 1)
                dve.wait_ge(s_wsc, 1)
                split([Ws[:, :, p] for p in range(PARTS)], W[:], rest[:], s_ws)
                dve.wait_ge(s_x, 32)
                for k in range(KD):
                    x, left = xT[:, k, :, 0:EARLY], x_rest[:, k, :, 0:EARLY]
                    p = [xs[:, i, k, :, 0:EARLY] for i in range(PARTS)]
                    nc.vector.tensor_copy(p[0], x).then_inc(s_xs, 1)
                    dve.wait_ge(s_xs, 4 * k + 1)
                    nc.vector.tensor_tensor(left, x, p[0], ALU.subtract).then_inc(s_xs, 1)
                    dve.wait_ge(s_xs, 4 * k + 2)
                    nc.vector.tensor_copy(p[1], left).then_inc(s_xs, 1)
                    dve.wait_ge(s_xs, 4 * k + 3)
                    nc.vector.tensor_tensor(p[2], left, p[1], ALU.subtract).then_inc(s_xs, 1)
                dve.wait_ge(s_vb, 1)
                nc.vector.tensor_copy(which_bf[:], which[:])
                for g in range(GATES):
                    last = nc.vector.tensor_scalar(vb[:, g], vb[:, g], scale[0:B, g:g + 1], None, ALU.mult)
                last.then_inc(s_wsc, 1)
                dve.wait_ge(s_wsc, 2)
                split([vbs[:, p] for p in range(PARTS)], vb[:], vb_rest[:], s_vs)
                for g in range(GATES):
                    last = nc.vector.tensor_scalar(Us[:, g, 0], U[:, g], scale[:, g:g + 1], None, ALU.mult)
                last.then_inc(s_us, 1)
                dve.wait_ge(s_us, 1)
                for g in range(GATES):
                    last = nc.vector.scalar_tensor_tensor(out=Us[:, g, 1], in0=U[:, g], scalar=scale[:, g:g + 1], in1=Us[:, g, 0],
                                                          op0=ALU.mult, op1=ALU.subtract)
                last.then_inc(s_us, 1)
                nc.vector.memset(ring[:, 0], 0.0).then_inc(s_h, 1)
                nc.vector.memset(h_part[:, 0], 0.0).then_inc(s_hhi, 1)
                nc.vector.memset(h_part[:, 1], 0.0).then_inc(s_hlo, 1)
                for f in (r_h, z_cand, rh_high, step_high, step_low):
                    nc.vector.memset(f[:], 0.0).then_inc(s_zero, 1)
                dve.wait_ge(s_zero, 5)
                nc.vector.memset(rh_high[:, :, 0], -1.0).then_inc(s_zero, 1)
                nc.vector.memset(step_high[:, :, 0], -1.0).then_inc(s_shi, 1)
                dve.wait_ge(s_zero, 6)
                dve.sem_inc(s_hr, 1)
                dve.sem_inc(s_slo, 1)
                dve.sem_inc(s_carry, 1)
                def low_part(low, factors, high):
                    return nc.vector.tensor_tensor_scan(low[:].rearrange("p c s -> p (c s)"), factors[:].rearrange("p c s -> p (c s)"),
                                                        high[:].rearrange("p c s -> p (c s)"), 0.0, ALU.mult, ALU.subtract)

                with dve.Fori(0, S // (2 * SEG)) as i:
                    n = i * (2 * SEG)
                    dve.wait_ge(s_carry, i + 1)
                    for j in range(2 * SEG):
                        h, h_new = ring[:, j], ring[:, j + 1]
                        m = n + (j + 1)
                        dve.wait_ge(s_r, m)
                        dve.wait_ge(s_h, m)
                        nc.vector.tensor_tensor(rh_high[:, :, 2], r, h, ALU.mult).then_inc(s_rhhi, 1)
                        dve.wait_ge(s_rhhi, m)
                        dve.wait_ge(s_hr, m)
                        low_part(rh_low, r_h, rh_high).then_inc(s_rhlo, 1)
                        dve.wait_ge(s_nz, m)
                        nc.vector.tensor_tensor(keep_part[:, 0], nz[:], h, ALU.mult).then_inc(s_khi, 1)
                        nc.vector.tensor_tensor(keep[:], nz[:], h, ALU.mult).then_inc(s_k, 1)
                        dve.wait_ge(s_khi, m)
                        dve.wait_ge(s_k, m)
                        nc.vector.tensor_tensor(keep_part[:, 1], keep[:], keep_part[:, 0], ALU.subtract).then_inc(s_klo, 1)
                        dve.wait_ge(s_c, m)
                        dve.wait_ge(s_z, m)
                        nc.vector.tensor_tensor(step_high[:, :, 2], z, cand, ALU.mult).then_inc(s_shi, 1)
                        nc.vector.tensor_tensor(step_in[:], z, cand, ALU.mult).then_inc(s_s, 1)
                        dve.wait_ge(s_shi, m + 1)
                        low_part(step_low, z_cand, step_high).then_inc(s_slo, 1)
                        dve.wait_ge(s_s, m)
                        nc.vector.tensor_tensor(h_part[:, 0], step_in[:], keep[:], ALU.add).then_inc(s_hhi, 1)
                        if j % SEG == 0:
                            dve.wait_ge(s_hist, 2 * i + (1 + j // SEG))
                        nc.vector.tensor_tensor(h_new, step_in[:], keep[:], ALU.add).then_inc(s_h, 1)
                        nc.vector.tensor_tensor(r_h[:, :, 2], step_in[:], keep[:], ALU.add).then_inc(s_hr, 1)
                        dve.wait_ge(s_hhi, m + 1)
                        dve.wait_ge(s_h, m + 1)
                        nc.vector.tensor_tensor(h_part[:, 1], h_new, h_part[:, 0], ALU.subtract).then_inc(s_hlo, 1)
                    nc.vector.tensor_copy(ring[:, 0], ring[:, 2 * SEG]).then_inc(s_carry, 1)

            @block.tensor
            def _(pe):
                pe.wait_ge(s_one, 3)
                pe.wait_ge(s_const, 32)
                pe.wait_ge(s_peak, 1)
                nc.tensor.transpose(bank[5][0:GATES, 0:P], peak[:], ident[:]).then_inc(s_pt, 1)
                pe.wait_ge(s_sc, 5)
                nc.tensor.matmul(bank[3][:, 0:2 * GATES], ones[0:GATES, :], scales[:], start=True, stop=True).then_inc(s_pt, 1)
                pe.wait_ge(s_cw, 16 * (2 * GATES + 2))
                for g in range(GATES):
                    o = bank[6][0:B, g * D:(g + 1) * D] if g < 2 else bank[7][0:B, 0:D]
                    for k in range(KD):
                        nc.tensor.matmul(o, condT[:, k], C[:, g, k], start=(k == 0), stop=False)
                    last = nc.tensor.matmul(o, ones[0:1, 0:B], bias[:, g], start=False, stop=True)
                last.then_inc(s_v, 1)

                def input_terms(q, t0):
                    for g in range(GATES):
                        for m in range(KD):
                            o = pre[g][q][:, :, m, :]
                            cols = slice(m * P, (m + 1) * P)
                            for k in range(KD):
                                for w, x in PAIRS:
                                    yield lambda o=o, g=g, k=k, w=w, x=x, cols=cols, m=m: nc.tensor.matmul(
                                        o, Ws[:, g, w, k, cols], xs[:, x, k, :, bass.ds(t0, SEG)].rearrange("p b t -> p t b"),
                                        start=(m == 0 and k == 0 and w == 0 and x == 0), stop=False, skip_group_check=True)
                            for p in range(PARTS):
                                yield lambda o=o, g=g, p=p, cols=cols: nc.tensor.matmul(
                                    o, vbs[:, p, g, cols], which_bf[:], start=False, stop=False, skip_group_check=True)

                state = [h_part[:, p] for p in range(2)]
                kept = [keep_part[:, p] for p in range(2)]
                reset = [rh_high[:, :, 2], rh_low[:, :, 2]]
                step = [step_high[:, :, 2], step_low[:, :, 2]]

                def recur(g, q, jj, x, part):
                    for m in range(KD):
                        for k in range(KD):
                            for p in PART_OF[part]:
                                last = nc.tensor.matmul(pre[g][q][:, jj, m, :], Us[:, g, p, k, m * P:(m + 1) * P],
                                                        x[part][:, k * B:(k + 1) * B],
                                                        start=False, stop=False, skip_group_check=True)
                    return last

                pe.wait_ge(s_ws, 4)
                pe.wait_ge(s_xs, 4 * KD)
                pe.wait_ge(s_vs, 4)
                for f in input_terms(0, 0):
                    f()
                pe.wait_ge(s_us, 2)
                with pe.Fori(0, S // (2 * SEG)) as i:
                    n = i * (2 * SEG)
                    for q in range(2):
                        ahead = list(input_terms(1 - q, n + (q + 1) * SEG))
                        slots = 2 * (SEG - 1)

                        def fill(slot):
                            for f in ahead[len(ahead) * slot // slots:len(ahead) * (slot + 1) // slots]:
                                f()

                        for jj in range(SEG):
                            j = q * SEG + jj
                            m = n + (j + 1)
                            pe.wait_ge(s_shi, m)
                            recur(0, q, jj, step, 0)
                            pe.wait_ge(s_slo, m)
                            recur(0, q, jj, step, 1).then_inc(s_rp, 1)
                            pe.wait_ge(s_hhi, m)
                            recur(1, q, jj, state, 0)
                            pe.wait_ge(s_hlo, m)
                            recur(1, q, jj, state, 1).then_inc(s_zp, 1)
                            if jj < SEG - 1:
                                fill(2 * jj)
                            pe.wait_ge(s_rhhi, m)
                            recur(2, q, jj, reset, 0)
                            pe.wait_ge(s_rhlo, m)
                            recur(2, q, jj, reset, 1).then_inc(s_cp, 1)
                            nq, njj = (q, jj + 1) if jj < SEG - 1 else (1 - q, 0)
                            pe.wait_ge(s_khi, m)
                            recur(0, nq, njj, kept, 0)
                            pe.wait_ge(s_klo, m)
                            recur(0, nq, njj, kept, 1)
                            if jj < SEG - 1:
                                fill(2 * jj + 1)
                    pe.wait_ge(s_xl, 4 * KD)


def layer0_ffn(nc, sb, sem, bank, xT, hist, ident, ones_bf, weights, s_w, load_next, s_raw, raw, raw_parts):
    with ExitStack() as own:
        def t(name, shape, dt=F32):
            return own.enter_context(nc.sbuf_tensor(name, shape, dt))

        wr, br, b1, b2, W1, W2 = weights
        wr_rep = t("wr_rep", [P, KD, P])
        ws = t("ws", [P, S])
        wcol = t("wcol", [P, S // P])
        ge = t("ge", [P, S // P, S], BF16)
        mask = t("mask", [P, S], U32)
        hid = t("hid", [P, KH, S])
        blk = t("blk", [P, KD, S])
        sel = t("sel", [P, KD, S])

        s_rep = sem("router_weights_spread")
        s_sp, s_s = sem("scores_pre"), sem("scores_done")
        s_tp, s_t = sem("scores_turned"), sem("score_cols")
        s_ge, s_cnt, s_m = sem("compared"), sem("counted"), sem("mask_done")
        s_fp, s_f = sem("hidden_pre"), sem("hidden_done")
        s_dp, s_d = sem("block_pre"), sem("block_done")
        s_sel, s_y = sem("selected"), sem("layer0_done")
        s_pass = sem("ffn_waits_passed")
        s_high, s_low = sem("next_high_parts"), sem("next_low_parts")

        with nc.Block() as block:
            @block.sync
            def _(sp):
                load_next(sp)

            @block.tensor
            def _(pe):
                pe.wait_ge(s_w, 96)
                pe.wait_ge(s_rep, KD)
                with pe.Fori(0, B) as b:
                    def state(k):
                        return hist[:, k, bass.ds(b, 1), :].rearrange("p b t -> p (b t)")

                    for k in range(KD):
                        last = nc.tensor.matmul(bank[0][:], wr_rep[:, k], state(k), start=(k == 0), stop=(k == KD - 1))
                    last.then_inc(s_sp, 1)
                    for f in range(KH):
                        if f >= 2:
                            pe.wait_ge(s_f, b * KH + (f - 1))
                        for k in range(KD):
                            last = nc.tensor.matmul(bank[3 + f % 2][:], W1[:, k, f * P:(f + 1) * P], state(k),
                                                    start=(k == 0), stop=(k == KD - 1))
                        last.then_inc(s_fp, 1)
                        if f == 1:
                            pe.wait_ge(s_s, b + 1)
                            for j in range(S // P):
                                last = nc.tensor.transpose(bank[1][:, j * P:(j + 1) * P], ws[:, j * P:(j + 1) * P], ident[:])
                            last.then_inc(s_tp, 1)
                        if f == 5:
                            pe.wait_ge(s_ge, b + 1)
                            for j in range(S // P):
                                last = nc.tensor.matmul(bank[2][:], ones_bf[:], ge[:, j], start=(j == 0), stop=(j == S // P - 1))
                            last.then_inc(s_cnt, 1)
                    for d in range(KD):
                        for f in range(KH):
                            if d == 0:
                                pe.wait_ge(s_f, b * KH + (f + 1))
                            last = nc.tensor.matmul(bank[5 + d][:], W2[:, f, d * P:(d + 1) * P], hid[:, f],
                                                    start=(f == 0), stop=(f == KH - 1))
                        last.then_inc(s_dp, 1)

            @block.scalar
            def _(act):
                act.wait_ge(s_w, 96)
                with act.Fori(0, B) as b:
                    act.wait_ge(s_sp, b + 1)
                    nc.scalar.activation(ws[:], bank[0][:], ACT.Identity, bias=br[:, 0:1]).then_inc(s_s, 1)
                    for f in range(KH):
                        act.wait_ge(s_fp, b * KH + (f + 1))
                        nc.scalar.activation(hid[:, f], bank[3 + f % 2][:], ACT.Gelu, bias=b1[:, f:f + 1]).then_inc(s_f, 1)
                    for d in range(KD):
                        act.wait_ge(s_dp, b * KD + (d + 1))
                        nc.scalar.activation(blk[:, d], bank[5 + d][:], ACT.Identity, bias=b2[:, d:d + 1]).then_inc(s_d, 1)

            @block.gpsimd
            def _(pool):
                high, low = raw_parts
                pool.wait_ge(s_raw, 64)
                for i in range(raw.shape[1] // S):
                    piece = slice(i * S, (i + 1) * S)
                    nc.gpsimd.tensor_copy(high[:, piece], raw[:, piece]).then_inc(s_high, 1)
                    pool.wait_ge(s_high, i + 1)
                    nc.gpsimd.tensor_tensor(low[:, piece], raw[:, piece], high[:, piece].bitcast(F32), ALU.subtract).then_inc(s_low, 1)
                pool.wait_ge(s_low, raw.shape[1] // S)

            @block.vector
            def _(dve):
                dve.wait_ge(s_w, 96)
                for k in range(KD):
                    nc.vector.tensor_copy(wr_rep[:, k], wr[:, k:k + 1].to_broadcast([P, P])).then_inc(s_rep, 1)
                with dve.Fori(0, B) as b:
                    dve.wait_ge(s_tp, b + 1)
                    nc.vector.tensor_copy(wcol[:], bank[1][:].rearrange("p (j c) -> p j c", c=P)[:, :, 0]).then_inc(s_t, 1)
                    dve.wait_ge(s_t, b + 1)
                    dve.wait_ge(s_s, b + 1)
                    for j in range(S // P):
                        last = nc.vector.tensor_scalar(ge[:, j], ws[:], wcol[:, j:j + 1], None, ALU.is_le)
                    last.then_inc(s_ge, 1)
                    dve.wait_ge(s_cnt, b + 1)
                    nc.vector.tensor_scalar(mask[:], bank[2][:], float(SELECT - 1), None, ALU.is_le).then_inc(s_m, 1)
                    dve.wait_ge(s_m, b + 1)
                    for d in range(KD):
                        h = hist[:, d, bass.ds(b, 1), :].rearrange("p b t -> p (b t)")
                        x = xT[:, d, bass.ds(b, 1), 0:S].rearrange("p b t -> p (b t)")
                        nc.vector.tensor_copy(sel[:, d], h).then_inc(s_sel, 1)
                        dve.wait_ge(s_sel, (b * KD + d) * 2 + 1)
                        dve.wait_ge(s_d, b * KD + (d + 1))
                        dve.sem_inc(s_pass, 1)
                        nc.vector.copy_predicated(sel[:, d], mask[:], blk[:, d]).then_inc(s_sel, 1)
                        dve.wait_ge(s_sel, (b * KD + d) * 2 + 2)
                        nc.vector.tensor_tensor(x, x, sel[:, d], ALU.add).then_inc(s_y, 1)


def layer1_context(nc, sb, sem, A, bank, xT, hist, ident, ones, condT, weights, raw, parts, s_w, load_next):
    with ExitStack() as own:
        def t(name, shape, dt=F32):
            return own.enter_context(nc.sbuf_tensor(name, shape, dt))

        gw, gb, tw, tb, b1, b2 = weights
        UP = KD * HID
        PIECES = raw.shape[1] // S
        w1 = [[v[:, 0:UP].rearrange("p (k f) -> p k f", k=KD) for v in q] for q in parts]
        w2 = [[v[:, UP:].rearrange("p (f d) -> p f d", f=KH) for v in q] for q in parts]
        xs = [t(f"x_part{p}", [P, KD, B, S], F32R) for p in range(2)]
        hid = [t(f"ehid_part{p}", [P, KH, S], F32R) for p in range(2)]
        full = t("ehid_full", [P, 2, S])
        tmp = t("etmp", [P, KD, S])
        sums = t("sums", [P, 3, KD, B])
        gate_in = t("gate_in", [P, 3, KD, B])
        silu_c = t("silu_c", [P, KD, B])
        mod = t("mod", [B, 2 * NE0])
        lg = t("lg", [B, 3, NE0])
        sm = t("sm", [B, 8])
        score = t("score", [B, 8])
        top = t("top", [B, 8])
        idx = t("idx", [B, 8], U32)
        idxf = t("idxf", [B, TOP0])
        wk = t("wk", [B, TOP0])
        off = t("off", [B, TOP0, 2])
        ck = t("ck", [B, TOP0, 3])
        ckd = t("ckd", [B, B, TOP0, 3])
        coef = t("coef", [P, B, TOP0, 3])

        s_ew = [sem(f"expert_loaded{k}") for k in range(TOP0)]
        s_silu = sem("cond_silu")
        s_g = sem("gate_chain")
        s_gin, s_gp, s_ex = sem("gate_in_done"), sem("gate_pre"), sem("gate_exp")
        s_idx, s_ckd, s_cf = sem("experts_chosen"), sem("coef_rows"), sem("coef_spread")
        s_coef = sem("coef_done")
        s_xhi, s_xlo = sem("x_high"), sem("x_low")
        s_whi, s_wlo = sem("weights_high"), sem("weights_low")
        s_fp, s_f, s_flo = sem("ehidden_pre"), sem("ehidden_done"), sem("ehidden_low")
        s_dp, s_d = sem("eblock_pre"), sem("eblock_done")
        s_add = sem("eblock_added")
        up = bank[1:5]
        GATE_STEPS = 6

        def place(k):
            return 1 - k

        def expert(b, k):
            return b * TOP0 + k

        with nc.Block() as block:
            @block.sync
            def _(sp):
                sp.wait_ge(s_idx, 1)
                for n in range(B * TOP0):
                    b, k = n // TOP0, n % TOP0
                    e = sp.value_load(idx[b:b + 1, k:k + 1], min_val=0, max_val=NE0 - 1)
                    one, u = bass.ds(e, 1), 1 + k
                    if n:
                        sp.wait_ge(s_wlo, n * PIECES)
                    if b:
                        sp.wait_ge(s_d, (B + n - TOP0 + 1) * KD)
                    sp.dma_start(raw[:, 0:UP].rearrange("p (k f) -> p k f", k=KD),
                                 A["L1_cond_ew1"][one].rearrange("o (k p) f -> p (o k) f", p=P)).then_inc(s_ew[k], 16)
                    sp.dma_start(raw[:, UP:].rearrange("p (f d) -> p f d", f=KH),
                                 A["L1_cond_ew2"][one].rearrange("o (f p) d -> p (o f) d", p=P)).then_inc(s_ew[k], 16)
                    sp.dma_start(b1[:, u], A["L1_cond_eb1"][one].rearrange("o p f -> p (o f)")).then_inc(s_ew[k], 16)
                    sp.dma_start(b2[:, u], A["L1_cond_eb2"][one].rearrange("o p k -> p (o k)")).then_inc(s_ew[k], 16)
                    if n == 0:
                        load_next(sp)

            @block.tensor
            def _(pe):
                def unit(m, b, q):
                    for f in range(KH):
                        if f >= len(up) or not isinstance(m, int) or m:
                            pe.wait_ge(s_f, m * KH + (f + 1 - len(up)))
                        for k in range(KD):
                            for w, x in MEET:
                                last = nc.tensor.matmul(up[f % len(up)][:], w1[q][w][:, k, f * P:(f + 1) * P],
                                                        xs[x][:, k, bass.ds(b, 1), :].rearrange("p b t -> p (b t)"),
                                                        start=(k == 0 and w == 0 and x == 0), stop=(k == KD - 1 and x == 1))
                        last.then_inc(s_fp, 1)
                    for d in range(KD):
                        if not isinstance(m, int) or m:
                            pe.wait_ge(s_d, m * KD + (d + 1 - KD))
                        for f in range(KH):
                            if d == 0:
                                pe.wait_ge(s_flo, m * KH + (f + 1))
                            for w, x in MEET:
                                last = nc.tensor.matmul(bank[5 + d][:], w2[q][w][:, f, d * P:(d + 1) * P], hid[x][:, f],
                                                        start=(f == 0 and w == 0 and x == 0), stop=(f == KH - 1 and x == 1))
                        last.then_inc(s_dp, 1)

                def shared(b):
                    pe.wait_ge(s_xlo, b + 1)
                    unit(b, b, 0)

                def chosen(b, k):
                    pe.wait_ge(s_wlo, expert(b, k) * PIECES + PIECES)
                    unit(expert(b, k) + B, b, place(k))

                shared(0)
                pe.wait_ge(s_w, 64)
                pe.wait_ge(s_silu, 1)
                for k in range(KD):
                    nc.tensor.matmul(bank[7][0:B, 0:2 * NE0], silu_c[:, k], tw[:, k], start=(k == 0), stop=False)
                nc.tensor.matmul(bank[7][0:B, 0:2 * NE0], ones[0:1, 0:B], tb[:], start=False, stop=True).then_inc(s_gp, 1)
                pe.wait_ge(s_gin, 1)
                for c in range(3 * KD):
                    nc.tensor.matmul(bank[0][0:B, 0:NE0], gate_in[:, c // KD, c % KD], gw[:, c], start=(c == 0), stop=False)
                nc.tensor.matmul(bank[0][0:B, 0:NE0], ones[0:1, 0:B], gb[:], start=False, stop=True).then_inc(s_gp, 1)
                with pe.Fori(1, B) as b:
                    shared(b)
                pe.wait_ge(s_ckd, 1)
                nc.tensor.matmul(bank[7][:, 0:B * TOP0 * 3], ones[0:B, :],
                                 ckd[:].rearrange("q b k r -> q (b k r)"), start=True, stop=True).then_inc(s_cf, 1)
                with pe.Fori(0, B) as b:
                    for k in range(TOP0):
                        chosen(b, k)

            @block.scalar
            def _(act):
                for b in range(B):
                    nc.scalar.activation(xs[0][:, :, b], xT[:, :, b, 0:S], ACT.Copy).then_inc(s_xhi, 1)
                nc.scalar.activation(silu_c[:], condT[:], ACT.Silu).then_inc(s_silu, 1)

                def unit(m, b, u, out_of, split_next=None):
                    for f in range(KH):
                        act.wait_ge(s_fp, m * KH + (f + 1))
                        if f >= 2 or not isinstance(m, int) or m:
                            act.wait_ge(s_flo, m * KH + (f - 1))
                        nc.scalar.activation(hid[0][:, f], up[f % len(up)][:], ACT.Gelu_apprx_tanh, bias=b1[:, u, f:f + 1])
                        nc.scalar.activation(full[:, f % 2], up[f % len(up)][:], ACT.Gelu_apprx_tanh,
                                             bias=b1[:, u, f:f + 1]).then_inc(s_f, 1)
                    if split_next:
                        split_next()
                    for d in range(KD):
                        act.wait_ge(s_dp, m * KD + (d + 1))
                        out_of(d)

                def split(b, k):
                    act.wait_ge(s_ew[k], b * 64 + 64)
                    for i in range(PIECES):
                        piece = slice(i * S, (i + 1) * S)
                        nc.scalar.activation(parts[place(k)][0][:, piece], raw[:, piece], ACT.Copy).then_inc(s_whi, 1)

                def shared(b, split_next=None):
                    def out_of(d):
                        nc.scalar.activation(hist[:, d, bass.ds(b, 1), :].rearrange("p b t -> p (b t)"), bank[5 + d][:],
                                             ACT.Identity, bias=b2[:, 0, d:d + 1]).then_inc(s_d, 1)

                    unit(b, b, 0, out_of, split_next)

                def chosen(b, k, split_next=None):
                    def out_of(d):
                        act.wait_ge(s_add, expert(b, k) * KD + (d + 1))
                        nc.scalar.activation(tmp[:, d], bank[5 + d][:], ACT.Identity, bias=b2[:, 1 + k, d:d + 1]).then_inc(s_d, 1)

                    unit(expert(b, k) + B, b, 1 + k, out_of, split_next)

                shared(0)
                act.wait_ge(s_g, GATE_STEPS)
                nc.scalar.activation(lg[:, 2], lg[:, 1], ACT.Exp, bias=sm[:, 0:1], accum_out=sm[:, 1:2]).then_inc(s_ex, 1)
                with act.Fori(1, B - 1) as b:
                    shared(b)
                shared(B - 1, lambda: split(0, 0))
                with act.Fori(0, B - 1) as b:
                    chosen(b, 0, lambda: split(b, 1))
                    chosen(b, 1, lambda: split(b + 1, 0))
                chosen(B - 1, 0, lambda: split(B - 1, 1))
                chosen(B - 1, 1)

            @block.gpsimd
            def _(pool):
                for b in range(1, B):
                    pool.wait_ge(s_xhi, b + 1)
                    pool.wait_ge(s_xlo, b)
                    nc.gpsimd.tensor_tensor(xs[1][:, :, b], xT[:, :, b, 0:S], xs[0][:, :, b].bitcast(F32), ALU.subtract).then_inc(s_xlo, 1)

            @block.vector
            def _(dve):
                dve.sem_inc(s_add, KD)
                done = [0]

                def chain(ins):
                    done[0] += 1
                    ins.then_inc(s_g, 1)
                    dve.wait_ge(s_g, done[0])

                def low_tile(m, f):
                    dve.wait_ge(s_f, m * KH + (f + 1))
                    nc.vector.tensor_tensor(hid[1][:, f], full[:, f % 2], hid[0][:, f].bitcast(F32), ALU.subtract).then_inc(s_flo, 1)

                def split(b, k):
                    for i in range(PIECES):
                        piece = slice(i * S, (i + 1) * S)
                        dve.wait_ge(s_whi, expert(b, k) * PIECES + (i + 1))
                        nc.vector.tensor_tensor(parts[place(k)][1][:, piece], raw[:, piece],
                                                parts[place(k)][0][:, piece].bitcast(F32), ALU.subtract).then_inc(s_wlo, 1)

                def shared(b):
                    for f in range(KH):
                        low_tile(b, f)

                def chosen(b, k, split_next=None):
                    for f in range(KH):
                        low_tile(expert(b, k) + B, f)
                    if split_next:
                        split_next()
                    for d in range(KD):
                        dve.wait_ge(s_d, (expert(b, k) + B) * KD + (d + 1))
                        if k:
                            dve.wait_ge(s_add, expert(b, k) * KD + (d + 1))
                        for i, (a, z) in enumerate(REGIONS):
                            acc = hist[:, d, bass.ds(b, 1), a:z].rearrange("p b t -> p (b t)")
                            last = nc.vector.scalar_tensor_tensor(
                                out=acc, in0=tmp[:, d, a:z], scalar=coef[:, bass.ds(b, 1), k, i:i + 1].rearrange("p b i -> p (b i)"),
                                in1=acc, op0=ALU.mult, op1=ALU.add)
                        last.then_inc(s_add, 1)

                dve.wait_ge(s_xhi, 1)
                nc.vector.tensor_tensor(xs[1][:, :, 0], xT[:, :, 0, 0:S], xs[0][:, :, 0].bitcast(F32), ALU.subtract).then_inc(s_xlo, 1)
                (h0, h1), (w0, w1_), (p0, p1) = REGIONS
                for f in range(KH):
                    low_tile(0, f)
                    if f % 2 and f // 2 < 3:
                        a, z = REGIONS[f // 2]
                        last = nc.vector.tensor_reduce(sums[:, f // 2], xT[:, :, :, a:z], AX.X, ALU.add)
                chain(last)
                nc.vector.tensor_tensor(gate_in[:, 1], sums[:, 0], sums[:, 2], ALU.add)
                chain(nc.vector.tensor_tensor(gate_in[:, 2], sums[:, 1], sums[:, 2], ALU.add))
                chain(nc.vector.tensor_tensor(gate_in[:, 0], gate_in[:, 1], sums[:, 1], ALU.add))
                nc.vector.tensor_scalar(gate_in[:, 0], gate_in[:, 0], 1.0 / S, None, ALU.mult)
                nc.vector.tensor_scalar(gate_in[:, 1], gate_in[:, 1], 1.0 / (h1 - h0 + p1 - p0), None, ALU.mult)
                nc.vector.tensor_scalar(gate_in[:, 2], gate_in[:, 2], 1.0 / (w1_ - w0 + p1 - p0), None,
                                        ALU.mult).then_inc(s_gin, 1)
                dve.wait_ge(s_gp, 2)
                chain(nc.vector.tensor_copy(mod[:], bank[7][0:B, 0:2 * NE0]))
                chain(nc.vector.scalar_tensor_tensor(out=lg[:, 0], in0=mod[:, 0:NE0], scalar=1.0, in1=bank[0][0:B, 0:NE0],
                                                     op0=ALU.add, op1=ALU.mult))
                nc.vector.memset(score[:], -1.0)
                nc.vector.tensor_tensor(lg[:, 1], lg[:, 0], mod[:, NE0:], ALU.add).then_inc(s_gin, 1)
                dve.wait_ge(s_gin, 2)
                nc.vector.tensor_reduce(sm[:, 0:1], lg[:, 1], AX.X, ALU.max, negate=True).then_inc(s_g, 1)
                done[0] += 1
                assert done[0] == GATE_STEPS
                dve.wait_ge(s_ex, 1)
                chain(nc.vector.reciprocal(sm[:, 2:3], sm[:, 1:2]))
                chain(nc.vector.tensor_scalar(score[:, 0:NE0], lg[:, 2], sm[:, 2:3], None, ALU.mult))
                chain(nc.vector.max(top[:], score[:]))
                nc.vector.max_index(idx[:], top[:], score[:]).then_inc(s_idx, 1)
                chain(nc.vector.tensor_reduce(sm[:, 3:4], top[:, 0:TOP0], AX.X, ALU.add))
                chain(nc.vector.tensor_scalar(sm[:, 4:5], sm[:, 3:4], 1e-8, None, ALU.add))
                chain(nc.vector.reciprocal(sm[:, 5:6], sm[:, 4:5]))
                chain(nc.vector.tensor_scalar(wk[:], top[:, 0:TOP0], sm[:, 5:6], None, ALU.mult))
                dve.wait_ge(s_idx, 1)
                chain(nc.vector.tensor_copy(idxf[:], idx[:, 0:TOP0]))
                nc.vector.tensor_scalar(off[:, :, 0], idxf[:], 2.0, None, ALU.not_equal)
                chain(nc.vector.tensor_scalar(off[:, :, 1], idxf[:], 1.0, None, ALU.not_equal))
                nc.vector.tensor_tensor(ck[:, :, 0], off[:, :, 0], wk[:], ALU.mult)
                nc.vector.tensor_tensor(ck[:, :, 1], off[:, :, 1], wk[:], ALU.mult)
                chain(nc.vector.tensor_copy(ck[:, :, 2], wk[:]))
                for b in range(B):
                    last = nc.vector.tensor_scalar(ckd[:, b].rearrange("q k r -> q (k r)"),
                                                   ck[:].rearrange("q k r -> q (k r)"), ident[0:B, b:b + 1], None, ALU.mult)
                last.then_inc(s_ckd, 1)
                with dve.Fori(1, B) as b:
                    shared(b)
                split(0, 0)
                dve.wait_ge(s_cf, 1)
                nc.vector.tensor_copy(coef[:].rearrange("p b k r -> p (b k r)"), bank[7][:, 0:B * TOP0 * 3]).then_inc(s_coef, 1)
                dve.wait_ge(s_coef, 1)
                with dve.Fori(0, B - 1) as b:
                    chosen(b, 0, lambda: split(b, 1))
                    chosen(b, 1, lambda: split(b + 1, 0))
                chosen(B - 1, 0, lambda: split(B - 1, 1))
                chosen(B - 1, 1)
                dve.wait_ge(s_add, KD + B * TOP0 * KD)


def routing(nc, sb, sem, A, bank, xT, hist, ident, ones, slot_row, weights, scratch, s_wg, s_w, load_next, ctx_rows, out):
    tok = [sb(f"tok{c}", [b - a, NE], U32) for c, (a, b) in enumerate(CAPS)]
    with ExitStack() as own:
        def t(name, shape, dt=F32):
            return own.enter_context(nc.sbuf_tensor(name, shape, dt))

        TH = T // 2
        GROUPS, GT = 2, TILES // 2
        BT = S // P
        turn, sw1, sw2 = weights
        vrev = t("vrev", [P, TH])
        shift = t("shift", [P, P])
        rows = t("rows", [P, TILES, ROW])
        act_f, lin = scratch[:, 0:KF], scratch[:, KF:KF + 2]
        maskT = t("maskT", [P, TH])
        gates = t("gates", [P, TILES, NE])
        left = t("left", [P, TILES, NE])
        top8 = t("top8", [P, TILES, TOPK])
        st = t("st", [P, 4, TILES])
        cum = t("cum", [P, TH])
        before = t("before", [P, 1])
        order = t("order", [P, 2, CAP])
        slots = t("slots", [P, 4, NE])
        orow = t("orow", [P, 2, BT, D])

        s_c, s_lg, s_ex = sem("route_chain"), sem("logits_less_max"), sem("route_exp")
        s_mt, s_off = sem("mask_turned"), sem("offset_pre")
        s_ot = sem("order_turned")
        s_rt, s_rc = sem("rows_turned"), sem("rows_copied")
        s_dense, s_rows = sem("dense_done"), sem("rows_stored")
        s_v, s_z = sem("list_constants_loaded"), sem("spare_zero")
        s_up, s_lin, s_act = sem("up_pre"), sem("lin_copied"), sem("gated")
        s_silu = sem("silu_done")
        s_dp, s_base = sem("shared_pre"), sem("base_done")
        s_bt, s_bc = sem("base_turned"), sem("base_copied")
        s_out = [sem(f"base_stored{q}") for q in range(2)]
        s_sum = sem("base_summed")
        up = [(bank[0], bank[1]), (bank[2], bank[3])]
        down = [bank[4], bank[5]]

        def tile_of(i):
            return (i % 2) * HALF + i // 2

        with nc.Block() as block:
            @block.sync
            def _(sp):
                sp.dma_start(vrev[:], A["vrev"]).then_inc(s_v, 16)
                sp.dma_start(shift[:], A["shift"]).then_inc(s_v, 16)
                load_next(sp)
                sp.wait_ge(s_z, 1)
                for a, z in CAPS:
                    sp.dma_start(ctx_rows[T + a:T + z, :], cum[0:z - a, 0:ROW]).then_inc(s_rows, 16)
                    sp.dma_start(out[T + a:T + z, :], cum[0:z - a, 0:D]).then_inc(s_rows, 16)
                sp.wait_ge(s_rows, 64)
                sp.sem_inc(s_z, 1)
                sp.wait_ge(s_dense, GROUPS)
                sp.wait_ge(s_rc, TILES)
                v = ctx_rows[0:T, :].rearrange("(h j p) c -> p j h c", h=2, p=P)
                r4 = rows[:].rearrange("p (j h) c -> p j h c", h=2)
                for h in range(2):
                    sp.dma_start(v[:, :, h], r4[:, :, h]).then_inc(s_rows, 16)
                for b in range(B):
                    sp.wait_ge(s_bc, (b + 1) * KD)
                    sp.dma_start(out[b * S:(b + 1) * S, :].rearrange("(j p) d -> p j d", p=P), orow[:, b % 2]).then_inc(s_out[b % 2], 16)
                sp.wait_ge(s_rows, 96)
                for q in range(2):
                    sp.wait_ge(s_out[q], 8 * B)

            @block.tensor
            def _(pe):
                pe.wait_ge(s_wg, 16)
                for i in range(TILES):
                    c = tile_of(i)
                    b, o = c * P // S, c * P % S
                    if i >= 4:
                        pe.wait_ge(s_rc, i - 3)
                    for k in range(KD):
                        last = nc.tensor.matmul(bank[i % 4][:, k * P:k * P + P + NE], hist[:, k, b, o:o + P], turn[:, k],
                                                start=(k == 0), stop=(k == KD - 1), skip_group_check=True)
                    last.then_inc(s_rt, 1)

                def turn_base(b):
                    pe.wait_ge(s_sum, b + 1)
                    for j in range(BT):
                        for k in range(KD):
                            last = nc.tensor.transpose(down[j // 2][:, (j % 2) * D + k * P:(j % 2) * D + (k + 1) * P],
                                                       xT[:, k, b, j * P:(j + 1) * P], ident[:])
                        if j % 2:
                            last.then_inc(s_bt, 1)

                pe.wait_ge(s_rc, TILES)
                pe.wait_ge(s_w, 32)
                for b in range(B):
                    for f in range(KF):
                        n = b * KF + f
                        if n >= 2:
                            pe.wait_ge(s_silu, n - 1)
                            pe.wait_ge(s_lin, n - 1)
                        for s_ in range(2):
                            for k in range(KD):
                                last = nc.tensor.matmul(up[n % 2][s_][:], sw1[:, k, s_ * FFN + f * P:s_ * FFN + (f + 1) * P],
                                                        hist[:, k, b], start=(k == 0), stop=(k == KD - 1))
                            last.then_inc(s_up, 1)
                        if b and f == 2:
                            turn_base(b - 1)
                        if b == B - 1 and f == 0:
                            pe.wait_ge(s_ot, 1)
                            nc.tensor.transpose(bank[6][:, 0:P], order[:, 1, 0:P], ident[:])
                            nc.tensor.transpose(bank[7][0:CAP - P, 0:P], order[:, 1, P:CAP], ident[:]).then_inc(s_ot, 1)
                    if b == 0:
                        pe.wait_ge(s_dense, GROUPS)
                        for j in range(HALF):
                            last = nc.tensor.transpose(bank[6 + j // 4][:, (j % 4) * P:(j % 4 + 1) * P],
                                                       left[:, 2 * j:2 * j + 2].rearrange("p h e -> p (h e)"), ident[:])
                        last.then_inc(s_mt, 1)
                    for d in range(KD):
                        if b:
                            pe.wait_ge(s_bc, (b - 1) * KD + d + 1)
                        for f in range(KF):
                            if d == 0:
                                pe.wait_ge(s_act, b * KF + f + 1)
                            last = nc.tensor.matmul(down[d][:], sw2[:, f, d * P:(d + 1) * P], act_f[:, f],
                                                    start=(f == 0), stop=(f == KF - 1))
                        last.then_inc(s_dp, 1)
                        if b == 0 and d == 0:
                            pe.wait_ge(s_off, 1)
                            pe.wait_ge(s_v, 32)
                            nc.tensor.matmul(bank[6][:, 0:1], shift[:], cum[:, TH - 1:TH], start=True, stop=True).then_inc(s_off, 1)
                turn_base(B - 1)

            @block.scalar
            def _(act):
                def exp(g):
                    act.wait_ge(s_lg, g + 1)
                    nc.scalar.activation(gates[:, g * GT:(g + 1) * GT].rearrange("p t e -> p (t e)"),
                                         left[:, g * GT:(g + 1) * GT].rearrange("p t e -> p (t e)"), ACT.Exp).then_inc(s_ex, 1)

                for i in range(TILES):
                    act.wait_ge(s_rt, i + 1)
                    nc.scalar.activation(rows[:, i], bank[i % 4][:, 0:ROW], ACT.Copy).then_inc(s_rc, 1)
                    if i == GT + 3:
                        exp(0)
                exp(1)

                def store_base(b):
                    for h in range(KD):
                        act.wait_ge(s_bt, b * KD + h + 1)
                        if h == 0 and b >= 2:
                            act.wait_ge(s_out[b % 2], 16 * (b // 2))
                        nc.scalar.activation(orow[:, b % 2, 2 * h:2 * h + 2].rearrange("p j d -> p (j d)"), down[h][:], ACT.Copy).then_inc(s_bc, 1)

                for b in range(B):
                    for f in range(KF):
                        n = b * KF + f
                        act.wait_ge(s_up, 2 * n + 1)
                        if n >= 2:
                            act.wait_ge(s_act, n - 1)
                        nc.scalar.activation(lin[:, n % 2], up[n % 2][0][:], ACT.Copy).then_inc(s_lin, 1)
                        act.wait_ge(s_up, 2 * n + 2)
                        nc.scalar.activation(act_f[:, f], up[n % 2][1][:], ACT.Silu).then_inc(s_silu, 1)
                        if b and f == 3:
                            store_base(b - 1)
                    for d in range(KD):
                        act.wait_ge(s_dp, b * KD + d + 1)
                        act.wait_ge(s_up, 2 * (b + 1) * KF)
                        nc.scalar.activation(hist[:, d, b], down[d][:], ACT.Copy).then_inc(s_base, 1)
                store_base(B - 1)

            @block.gpsimd
            def _(pool):
                nc.gpsimd.memset(cum[:, 0:ROW], 0.0).then_inc(s_z, 1)
                for b in range(B):
                    for f in range(KF):
                        n = b * KF + f
                        pool.wait_ge(s_silu, n + 1)
                        pool.wait_ge(s_lin, n + 1)
                        nc.gpsimd.tensor_tensor(act_f[:, f], act_f[:, f], lin[:, n % 2], ALU.mult).then_inc(s_act, 1)
                    pool.wait_ge(s_base, (b + 1) * KD)
                    nc.gpsimd.tensor_tensor(xT[:, :, b, 0:S], xT[:, :, b, 0:S], hist[:, :, b], ALU.add).then_inc(s_sum, 1)

            @block.vector
            def _(dve):
                done = [0]

                def chain(ins):
                    done[0] += 1
                    ins.then_inc(s_c, 1)
                    dve.wait_ge(s_c, done[0])

                def spread(col, g):
                    return st[:, col, g * GT:(g + 1) * GT].unsqueeze(2).to_broadcast([P, GT, NE])

                of = [slice(g * GT, (g + 1) * GT) for g in range(GROUPS)]
                for g in range(GROUPS):
                    dve.wait_ge(s_rc, (g + 1) * GT)
                    logits = rows[:, of[g], P:P + NE]
                    chain(nc.vector.tensor_reduce(st[:, 0, of[g]], logits, AX.X, ALU.max))
                    nc.vector.tensor_tensor(left[:, of[g]], logits, spread(0, g), ALU.subtract).then_inc(s_lg, 1)
                for g in range(GROUPS):
                    dve.wait_ge(s_ex, g + 1)
                    chain(nc.vector.tensor_reduce(st[:, 1, of[g]], gates[:, of[g]], AX.X, ALU.add))
                    chain(nc.vector.reciprocal(st[:, 2, of[g]], st[:, 1, of[g]]))
                    chain(nc.vector.tensor_tensor(gates[:, of[g]], gates[:, of[g]], spread(2, g), ALU.mult))
                    for i in range(g * GT, (g + 1) * GT):
                        last = nc.vector.max(top8[:, i], gates[:, i])
                    chain(last)
                    for i in range(g * GT, (g + 1) * GT):
                        last = nc.vector.match_replace(left[:, i], top8[:, i], gates[:, i], -1.0)
                    chain(last)
                    nc.vector.tensor_reduce(st[:, 0, of[g]], top8[:, of[g]], AX.X, ALU.add)
                    chain(nc.vector.tensor_scalar(left[:, of[g]], left[:, of[g]], 0.0, None, ALU.is_lt))
                    chain(nc.vector.tensor_scalar(st[:, 1, of[g]], st[:, 0, of[g]], EPS, None, ALU.max))
                    nc.vector.reciprocal(st[:, 3, of[g]], st[:, 1, of[g]])
                    chain(nc.vector.tensor_tensor(gates[:, of[g]], gates[:, of[g]], left[:, of[g]], ALU.mult))
                    nc.vector.tensor_tensor(rows[:, of[g], P:P + NE], gates[:, of[g]], spread(3, g), ALU.mult).then_inc(s_dense, 1)
                dve.wait_ge(s_mt, 1)
                for i in range(2):
                    last = nc.vector.tensor_copy(maskT[:, 512 * i:512 * i + 512], bank[6 + i][:])
                chain(last)
                dve.wait_ge(s_z, 2)
                chain(nc.vector.tensor_tensor_scan(cum[:], ones[:, 0:1].to_broadcast([P, TH]), maskT[:], 0.0, ALU.mult, ALU.add))
                dve.sem_inc(s_off, 1)
                dve.wait_ge(s_off, 2)
                chain(nc.vector.tensor_copy(before[:], bank[6][:, 0:1]))
                dve.wait_ge(s_v, 32)
                chain(nc.vector.tensor_scalar(cum[:], cum[:], before[:, 0:1], float(CAP), ALU.add, ALU.is_le))
                chain(nc.vector.tensor_tensor(cum[:], cum[:], maskT[:], ALU.mult))
                chain(nc.vector.tensor_tensor(cum[:], cum[:], vrev[:], ALU.mult))
                for i in range(ROUNDS):
                    top = order[:, 0, 8 * i:8 * i + 8]
                    chain(nc.vector.max(top, cum[:]))
                    chain(nc.vector.match_replace(cum[:], top, cum[:], 0.0))
                nc.vector.tensor_copy(order[0:NE, 1, :], order[0:NE, 0, :])
                chain(nc.vector.tensor_copy(order[NE:P, 1, :], order[NE:P, 0, ::-1]))
                dve.sem_inc(s_ot, 1)
                dve.wait_ge(s_ot, 2)
                for c, (a, z) in enumerate(CAPS):
                    n = z - a
                    chain(nc.vector.tensor_copy(slots[0:n, 0], bank[6 + c][0:n, 0:NE]))
                    chain(nc.vector.tensor_tensor(slots[0:n, 1], slots[0:n, 0], bank[6 + c][0:n, NE:P], ALU.max))
                    chain(nc.vector.tensor_scalar(slots[0:n, 2], slots[0:n, 1], 0.0, None, ALU.is_equal))
                    chain(nc.vector.tensor_scalar(slots[0:n, 1], slots[0:n, 1], -1.0, float(T), ALU.mult, ALU.add))
                    chain(nc.vector.tensor_scalar(slots[0:n, 2], slots[0:n, 2], slot_row[0:n, c:c + 1], None, ALU.mult))
                    chain(nc.vector.tensor_tensor(tok[c][:], slots[0:n, 1], slots[0:n, 2], ALU.add))
    return tok


def experts(nc, sb, sem, A, bank, ident, arena, s_w, ctx_rows, out, tok):
    UP = KD * 2 * FFN
    w1 = [arena[:, i * WROW:i * WROW + UP].rearrange("p (k f) -> p k f", k=KD) for i in range(RING)]
    w2 = [arena[:, i * WROW + UP:(i + 1) * WROW].rearrange("p (f d) -> p f d", f=KF) for i in range(RING)]
    with ExitStack() as own:
        def t(name, shape, dt=F32):
            return own.enter_context(nc.sbuf_tensor(name, shape, dt))

        got = [[t(f"got{q}{c}", [z - a, ROW]) for c, (a, z) in enumerate(CAPS)] for q in range(RING)]
        idx = [[t(f"row{q}{c}", [z - a, 1], U32) for c, (a, z) in enumerate(CAPS)] for q in range(RING)]
        to_idx = [t(f"to_row{c}", [z - a, 1], U32) for c, (a, z) in enumerate(CAPS)]
        xe = [t(f"xe{q}", [P, KD, CAP]) for q in range(2)]
        gate = t("gate_f", [P, 2, CAP])
        mid = [t(f"mid{q}", [P, KF, CAP]) for q in range(2)]
        ye = [t(f"ye{q}", [P, KD, CAP]) for q in range(2)]
        res = [[t(f"res{q}{c}", [z - a, D]) for c, (a, z) in enumerate(CAPS)] for q in range(2)]

        s_got = [sem(f"gathered{q}") for q in range(RING)]
        s_idx, s_to = sem("rows_named"), sem("add_rows_named")
        s_pass = sem("waits_passed")
        s_xt, s_xe = sem("tokens_turned"), sem("tokens_copied")
        s_up, s_silu, s_mid = sem("pair_pre"), sem("pair_silu"), sem("pair_done")
        s_y, s_ye = sem("down_pre"), sem("down_copied")
        s_yt, s_res, s_add = sem("down_turned"), sem("weighted"), sem("added")

        def wait(eng, s, n):
            if not isinstance(n, int) or n > 0:
                eng.wait_ge(s, n)

        def run(eng, body):
            for u in range(RING):
                body(u, u)
            with eng.Fori(1, NE // RING - 1) as i:
                for u in range(RING):
                    body(i * RING + u, u)
            for u in range(RING):
                body(NE - RING + u, u)

        def first(e):
            return isinstance(e, int) and e == 0

        def past(e, n):
            return isinstance(e, int) and e + n >= NE

        def uses(e, u):
            return e - u + RING

        with nc.Block() as block:
            @block.sync
            def _(sp):
                def load(e, u):
                    if isinstance(e, int) and e < RING:
                        return
                    sp.wait_ge(s_y, e - RING + 1)
                    src = A["ew"][e] if isinstance(e, int) else A["ew"][bass.ds(e, 1)].rearrange("o p n -> p (o n)")
                    sp.dma_start(arena[:, u * WROW:(u + 1) * WROW], src).then_inc(s_w[u], 16)

                run(sp, load)

            @block.gpsimd
            def _(pool):
                def name_rows(to, e, s):
                    for c in range(2):
                        nc.gpsimd.tensor_copy(to[c][:], tok[c][:, e:e + 1] if isinstance(e, int) else tok[c][:, bass.ds(e, 1)])\
                            .then_inc(s, 1)
                    pool.wait_ge(s, e * 2 + 2)

                def gather(e, u):
                    if not isinstance(e, int) or e >= RING:
                        pool.wait_ge(s_got[u], (uses(e, u) - RING) * (32 // RING))
                    name_rows(idx[u], e, s_idx)
                    pool.sem_inc(s_pass, 1)
                    for c in range(2):
                        nc.gpsimd.indirect_dma_start(
                            out=got[u][c][:], out_offset=None, in_=ctx_rows[:, :],
                            in_offset=bass.IndirectOffsetOnAxis(ap=idx[u][c][:, 0:1], axis=0)).then_inc(s_got[u], 16)

                def add(e, u):
                    wait(pool, s_add, e * 32)
                    name_rows(to_idx, e, s_to)
                    pool.wait_ge(s_res, e + 1)
                    pool.sem_inc(s_pass, 1)
                    for c in range(2):
                        nc.gpsimd.indirect_dma_start(
                            out=out[:, :], out_offset=bass.IndirectOffsetOnAxis(ap=to_idx[c][:, 0:1], axis=0),
                            in_=res[u % 2][c][:], in_offset=None, compute_op=ALU.add).then_inc(s_add, 16)

                def body(e, u):
                    if not first(e):
                        add(e - 1, (u - 1) % RING)
                    if not past(e, 3):
                        gather(e + 3, (u + 3) % RING)

                for u in range(RING - 1):
                    gather(u, u)
                run(pool, body)
                add(NE - 1, RING - 1)
                pool.wait_ge(s_add, NE * 32)

            @block.tensor
            def _(pe):
                def turn_in(e, u):
                    pe.wait_ge(s_got[u], uses(e, u) * (32 // RING))
                    wait(pe, s_xe, e)
                    for c, (a, z) in enumerate(CAPS):
                        for k in range(KD):
                            last = nc.tensor.transpose(bank[7][:, k * CAP + a:k * CAP + z], got[u][c][:, k * (P + NE):k * (P + NE) + P],
                                                       ident[0:z - a, 0:z - a])
                    last.then_inc(s_xt, 1)

                def turn_out(e, u):
                    pe.wait_ge(s_ye, e + 1)
                    wait(pe, s_res, e)
                    for c, (a, z) in enumerate(CAPS):
                        for k in range(KD):
                            last = nc.tensor.transpose(bank[6][0:z - a, c * D + k * P:c * D + (k + 1) * P], ye[u % 2][:, k, a:z], ident[:])
                    last.then_inc(s_yt, 1)

                def body(e, u):
                    pe.wait_ge(s_w[u], uses(e, u) * (16 // RING))
                    pe.wait_ge(s_xe, e + 1)
                    for f in range(KF):
                        wait(pe, s_mid, e * KF + (f - 2))
                        for s_ in range(2):
                            for k in range(KD):
                                last = nc.tensor.matmul(bank[f % 3][:, s_ * CAP:(s_ + 1) * CAP],
                                                        w1[u][:, k, s_ * FFN + f * P:s_ * FFN + (f + 1) * P], xe[u % 2][:, k],
                                                        start=(k == 0), stop=(k == KD - 1))
                        last.then_inc(s_up, 1)
                    if not first(e):
                        turn_out(e - 1, (u - 1) % RING)
                    if not past(e, 1):
                        turn_in(e + 1, (u + 1) % RING)
                    for d in range(KD):
                        for f in range(KF):
                            if d == 0:
                                pe.wait_ge(s_mid, e * KF + (f + 1))
                            last = nc.tensor.matmul(bank[4 + u % 2][:, d * CAP:(d + 1) * CAP], w2[u][:, f, d * P:(d + 1) * P], mid[u % 2][:, f],
                                                    start=(f == 0), stop=(f == KF - 1))
                    last.then_inc(s_y, 1)

                turn_in(0, 0)
                run(pe, body)
                turn_out(NE - 1, RING - 1)

            @block.scalar
            def _(act):
                def copy_in(e, u):
                    act.wait_ge(s_xt, e + 1)
                    nc.scalar.activation(xe[u % 2][:].rearrange("p k t -> p (k t)"), bank[7][:, 0:KD * CAP], ACT.Copy).then_inc(s_xe, 1)

                def body(e, u):
                    for f in range(KF):
                        act.wait_ge(s_up, e * KF + (f + 1))
                        wait(act, s_mid, e * KF + (f - 1))
                        nc.scalar.activation(gate[:, f % 2], bank[f % 3][:, CAP:2 * CAP], ACT.Silu).then_inc(s_silu, 1)
                    if not past(e, 1):
                        copy_in(e + 1, (u + 1) % RING)
                    act.wait_ge(s_y, e + 1)
                    nc.scalar.activation(ye[u % 2][:].rearrange("p k t -> p (k t)"), bank[4 + u % 2][:, 0:KD * CAP], ACT.Copy).then_inc(s_ye, 1)

                copy_in(0, 0)
                run(act, body)

            @block.vector
            def _(dve):
                def weigh(e, u):
                    dve.wait_ge(s_yt, e + 1)
                    wait(dve, s_add, e * 32 - 32)
                    dve.wait_ge(s_got[u], uses(e, u) * (32 // RING))
                    for c, (a, z) in enumerate(CAPS):
                        col = got[u][c][:, P + e:P + e + 1] if isinstance(e, int) else got[u][c][:, bass.ds(e + P, 1)]
                        last = nc.vector.tensor_scalar(res[u % 2][c][:], bank[6][0:z - a, c * D:(c + 1) * D], col, None, ALU.mult)
                    last.then_inc(s_res, 1)

                def body(e, u):
                    for f in range(KF):
                        dve.wait_ge(s_silu, e * KF + (f + 1))
                        nc.vector.tensor_tensor(mid[u % 2][:, f], bank[f % 3][:, 0:CAP], gate[:, f % 2], ALU.mult).then_inc(s_mid, 1)
                    if not first(e):
                        weigh(e - 1, (u - 1) % RING)

                run(dve, body)
                weigh(NE - 1, RING - 1)


def _layout(inputs):
    def f(name):
        return np.asarray(inputs[name])

    a = {k: f(k) for k in inputs if k.startswith("L0_") or k.startswith("L1_cond")}
    for n in ("L0_ffn_w_r", "L0_ffn_b1", "L0_ffn_b2", "L1_cond_sb1", "L1_cond_sb2"):
        a[n] = a[n].reshape(-1, P).T
    for n in ("L1_cond_eb1", "L1_cond_eb2"):
        a[n] = a[n].reshape(NE0, -1, P).transpose(0, 2, 1)
    a["xT"] = f("x").reshape(T, D).T
    a["condT"] = f("cond_1024").T
    wg, eye = f("L1_ffn_wg").T.reshape(KD, P, NE), np.eye(P, dtype=np.float32)
    a["turn"] = np.stack([np.concatenate([eye, wg[0]], axis=1), np.concatenate([wg[1], eye], axis=1)], axis=1)
    a["sw1T"] = f("L1_ffn_shared_w1").T
    a["sw2T"] = f("L1_ffn_shared_w2").T
    up = f("L1_ffn_expert_w1").transpose(0, 2, 1).reshape(NE, KD, P, 2 * FFN).transpose(0, 2, 1, 3).reshape(NE, P, -1)
    down = f("L1_ffn_expert_w2").transpose(0, 2, 1).reshape(NE, KF, P, D).transpose(0, 2, 1, 3).reshape(NE, P, -1)
    a["ew"] = np.concatenate([up, down], axis=2)
    a["ident"] = np.eye(P, dtype=np.float32)
    a["which"] = np.tile(np.eye(B, dtype=np.float32), (1, SEG))
    a["shift"] = np.eye(P, k=NE, dtype=np.float32)
    half = np.arange(T // 2, dtype=np.float32)
    a["vrev"] = np.repeat(np.stack([T - half, T // 2 - half]), NE, axis=0).astype(np.float32)
    a["slot_row"] = np.stack([np.arange(P), np.arange(P, 2 * P)], axis=1).astype(np.float32)
    return {k: np.ascontiguousarray(v) for k, v in a.items()}


def kernel(**inputs):
    import concourse.bacc as bacc
    from concourse.bass_utils import run_bass_kernel_spmd

    nc = bacc.Bacc("TRN2", target_bir_lowering=False, num_devices=1)
    arrays = {f"in_{k}": v for k, v in _layout(inputs).items()}
    A = {k[3:]: nc.dram_tensor(k, v.shape, mybir.dt.from_np(v.dtype), kind="ExternalInput").ap() for k, v in arrays.items()}
    out = nc.dram_tensor("out_rows", (T + CAP, D), F32, kind="ExternalOutput").ap()
    program(nc, A, out)
    r = run_bass_kernel_spmd(nc, [arrays], core_ids=[0])
    return r.results[0]["out_rows"][0:T].reshape(B, S, D)
```

```python
from contextlib import ExitStack

import numpy as np
import concourse.bass as bass
from concourse import mybir

F32 = mybir.dt.float32
BF16 = mybir.dt.bfloat16
F16 = mybir.dt.float16
F32R = mybir.dt.float32r
U32 = mybir.dt.uint32
ALU = mybir.AluOpType
ACT = mybir.ActivationFunctionType
AX = mybir.AxisListType

P = 128
B, S, D = 4, 512, 256
KD = D // P
T = B * S
HID = 1024
KH = HID // P
GATES = 3
PARTS = 3
SEG = 16
SELECT = S // 2
NE0, TOP0 = 4, 2
REGIONS = ((0, 170), (170, 340), (340, 512))
NE, TOPK, FFN, CAP = 64, 8, 768, 160
KF = FFN // P
TILES = T // P
HALF = TILES // 2
ROW = P + NE + P
CAPS = ((0, P), (P, CAP))
WROW = KD * 2 * FFN + KF * D
ROUNDS = CAP // 8
RING = 4
EPS = float(np.finfo(np.float32).eps)
MEET = ((0, 0), (1, 0), (0, 1))


def program(nc, A, out):
    with ExitStack() as ctx:
        def sb(name, shape, dt=F32):
            return ctx.enter_context(nc.sbuf_tensor(name, shape, dt))

        def sem(name):
            return ctx.enter_context(nc.semaphore(name))

        bank = [ctx.enter_context(nc.psum_tensor(f"bank{i}", [P, 512], F32)) for i in range(8)]
        ctx_rows = nc.dram_tensor("ctx_rows", [T + CAP, ROW], F32, kind="Internal").ap()

        xT = sb("xT", [P, KD, B, S + SEG])
        hist = sb("hist", [P, KD, B, S])
        ident = sb("ident", [P, P])
        ones = sb("ones", [P, P])
        ones_bf = sb("ones_bf", [P, P], BF16)
        condT = sb("condT", [P, KD, B])
        slot_row = sb("slot_row", [P, 2])
        FF = KD * HID + KH * D
        dense_w = sb("dense_w", [P, max(FF, WROW)])

        def cut(at, *shape):
            n = int(np.prod(shape))
            return dense_w[:, at:at + n].rearrange("p (a b) -> p a b", a=shape[0])

        wr, br = sb("wr", [P, KD]), sb("br", [P, 1])
        b1, b2 = sb("b1", [P, KH]), sb("b2", [P, KD])
        W1, W2 = cut(0, KD, HID), cut(KD * HID, KH, D)
        s_ffn = sem("ffn_weights_loaded")

        def load_ffn(eng):
            eng.dma_start(wr[:], A["L0_ffn_w_r"]).then_inc(s_ffn, 16)
            eng.dma_start(br[:], A["L0_ffn_b_r"].rearrange("(a o) -> a o", a=1).to_broadcast([P, 1])).then_inc(s_ffn, 16)
            eng.dma_start(b1[:], A["L0_ffn_b1"]).then_inc(s_ffn, 16)
            eng.dma_start(b2[:], A["L0_ffn_b2"]).then_inc(s_ffn, 16)
            eng.dma_start(W1, A["L0_ffn_W1"].rearrange("(k p) f -> p k f", p=P)).then_inc(s_ffn, 16)
            eng.dma_start(W2, A["L0_ffn_W2"].rearrange("(f p) d -> p f d", p=P)).then_inc(s_ffn, 16)

        s_x = sem("x_loaded")
        s_const = sem("const_loaded")
        gru(nc, sb, sem, A, bank, xT, hist, ident, ones, ones_bf, condT, slot_row, s_x, s_const, load_ffn)

        gw, gb = sb("gw", [P, 3 * KD, NE0]), sb("gb", [1, NE0])
        tw, tb = sb("tw", [P, KD, 2 * NE0]), sb("tb", [1, 2 * NE0])
        eb1, eb2 = sb("eb1", [P, 1 + TOP0, KH]), sb("eb2", [P, 1 + TOP0, KD])
        s_gate, s_shared = sem("gate_weights_loaded"), sem("shared_loaded")

        def load_gate(eng, raw):
            eng.dma_start(gw[:], A["L1_cond_gate_w"].rearrange("(c p) e -> p c e", p=P)).then_inc(s_gate, 16)
            eng.dma_start(gb[:], A["L1_cond_gate_b"].rearrange("(a e) -> a e", a=1)).then_inc(s_gate, 16)
            eng.dma_start(tw[:], A["L1_cond_time_w"].rearrange("(k p) e -> p k e", p=P)).then_inc(s_gate, 16)
            eng.dma_start(tb[:], A["L1_cond_time_b"].rearrange("(a e) -> a e", a=1)).then_inc(s_gate, 16)
            eng.dma_start(raw[:, 0:KD * HID].rearrange("p (k f) -> p k f", k=KD),
                          A["L1_cond_sw1"].rearrange("(k p) f -> p k f", p=P)).then_inc(s_shared, 16)
            eng.dma_start(raw[:, KD * HID:].rearrange("p (f d) -> p f d", f=KH),
                          A["L1_cond_sw2"].rearrange("(f p) d -> p f d", p=P)).then_inc(s_shared, 16)
            eng.dma_start(eb1[:, 0], A["L1_cond_sb1"]).then_inc(s_shared, 16)
            eng.dma_start(eb2[:, 0], A["L1_cond_sb2"]).then_inc(s_shared, 16)

        turn = sb("turn", [P, KD, P + NE])
        sw1, sw2 = cut(0, KD, 2 * FFN), cut(KD * 2 * FFN, KF, D)
        s_wg, s_sw = sem("router_loaded"), sem("shared_expert_loaded")

        def load_router(eng):
            eng.dma_start(turn[:], A["turn"]).then_inc(s_wg, 16)
            eng.dma_start(sw1, A["sw1T"].rearrange("(k p) f -> p k f", p=P)).then_inc(s_sw, 16)
            eng.dma_start(sw2, A["sw2T"].rearrange("(f p) d -> p f d", p=P)).then_inc(s_sw, 16)

        with ExitStack() as dense:
            raw = dense.enter_context(nc.sbuf_tensor("raw", [P, FF], F32))
            parts = [[dense.enter_context(nc.sbuf_tensor(f"weights{q}_part{p}", [P, FF], F32R)) for p in range(2)] for q in range(2)]
            layer0_ffn(nc, sb, sem, bank, xT, hist, ident, ones_bf, (wr, br, b1, b2, dense_w[:, 0:FF]), s_ffn,
                       lambda eng: load_gate(eng, raw),
                       s_shared, raw, parts)
            layer1_context(nc, sb, sem, A, bank, xT, hist, ident, ones, condT, (gw, gb, tw, tb, eb1, eb2),
                           raw, parts, s_gate, load_router)

        ring = [sb("ring0", [P, WROW])]
        tok = [sb(f"tok{c}", [z - a, NE], U32) for c, (a, z) in enumerate(CAPS)]
        got = [[sb(f"got{q}{c}", [z - a, ROW]) for c, (a, z) in enumerate(CAPS)] for q in range(RING)]
        idx = [[sb(f"row{q}{c}", [z - a, 1], U32) for c, (a, z) in enumerate(CAPS)] for q in range(RING)]
        s_ew = [sem(f"weights{q}") for q in range(RING)]
        s_got = [sem(f"gathered{q}") for q in range(RING)]
        s_idx, s_pass = sem("rows_named"), sem("waits_passed")
        s_base = [sem(f"base_stored{q}") for q in range(2)]

        def load_expert(eng):
            eng.dma_start(ring[0][:], A["ew"][0]).then_inc(s_ew[0], 16)

        def name_rows(pool, to, e, s):
            for c in range(2):
                nc.gpsimd.tensor_copy(to[c][:], tok[c][:, e:e + 1] if isinstance(e, int) else tok[c][:, bass.ds(e, 1)])\
                    .then_inc(s, 1)
            pool.wait_ge(s, e * 2 + 2)

        def gather(pool, e, u):
            name_rows(pool, idx[u], e, s_idx)
            pool.sem_inc(s_pass, 1)
            for c in range(2):
                nc.gpsimd.indirect_dma_start(
                    out=got[u][c][:], out_offset=None, in_=ctx_rows[:, :],
                    in_offset=bass.IndirectOffsetOnAxis(ap=idx[u][c][:, 0:1], axis=0)).then_inc(s_got[u], 16)

        routing(nc, sb, sem, A, bank, xT, hist, ident, ones, slot_row, (turn, sw1, sw2), s_wg, s_sw, load_expert, gather,
                tok, ctx_rows, out, s_base)
        ring += [sb(f"ring{u}", [P, WROW]) for u in range(1, RING)]
        experts(nc, sb, sem, A, bank, ident, ring, s_ew, got, s_got, gather, name_rows, s_pass, out, s_base)


def gru(nc, sb, sem, A, bank, xT, hist, ident, ones, ones_bf, condT, slot_row, s_x, s_const, load_next):
    with ExitStack() as own:
        def t(name, shape, dt=F32):
            return own.enter_context(nc.sbuf_tensor(name, shape, dt))

        EARLY = 4 * SEG
        C2 = KD * B
        TOP_EXP = 14
        EXP_BITS, BIAS, MANTISSA = 0x7f800000, 127, 23
        U = t("U", [P, GATES, KD, D])
        W = t("W", [P, GATES, KD, D])
        rest = t("rest", [P, GATES, KD, D])
        Us = t("Us", [P, GATES, 2, KD, D], F16)
        Ws = t("Ws", [P, GATES, PARTS, KD, D], BF16)
        xs = t("xs", [P, PARTS, KD, B, S + SEG], BF16)
        x_rest = t("x_rest", [P, KD, B, S + SEG])
        C = t("C", [P, GATES, KD, D])
        bias = t("bias", [B, GATES, D])
        vb = t("vb", [B, GATES, D])
        vb_rest = t("vb_rest", [B, GATES, D])
        vbs = t("vbs", [B, PARTS, GATES, D], BF16)
        which = t("which", [B, SEG * B])
        which_bf = t("which_bf", [B, SEG * B], BF16)
        peak = t("peak", [P, GATES])
        peaks = t("peaks", [GATES, 4])
        scales = t("scales", [GATES, 2 * GATES])
        scale = t("scale", [P, 2 * GATES + 1])
        ring = t("ring", [P, 2 * SEG + 1, C2])
        nz, keep, step_in = t("nz", [P, C2]), t("keep", [P, C2]), t("step_in", [P, C2])
        h_part, keep_part = t("h_part", [P, 2, C2], F16), t("keep_part", [P, 2, C2], F16)
        r_h, z_cand = t("r_h", [P, C2, 3]), t("z_cand", [P, C2, 3])
        rh_high, step_high = t("rh_high", [P, C2, 3], F16), t("step_high", [P, C2, 3], F16)
        rh_low, step_low = t("rh_low", [P, C2, 3], F16), t("step_low", [P, C2, 3], F16)
        r, z, cand = r_h[:, :, 1], z_cand[:, :, 1], z_cand[:, :, 2]

        s_w, s_cw, s_uw = sem("input_weights_loaded"), sem("cond_weights_loaded"), sem("recurrent_loaded")
        s_ws, s_us, s_vs = sem("input_weights_split"), sem("recurrent_split"), sem("cond_term_split")
        s_xe, s_id, s_which, s_cb = sem("early_inputs_loaded"), sem("identity_loaded"), sem("columns_loaded"), sem("biases_loaded")
        s_xs, s_xl = sem("early_inputs_split"), sem("late_inputs_split")
        s_v, s_vb = sem("cond_term"), sem("cond_term_copied")
        s_one = sem("ones_set")
        s_peak, s_pt, s_sc = sem("peaks_found"), sem("scale_products"), sem("scale_chain")
        s_scale, s_wsc = sem("scale_spread"), sem("input_weights_scaled")
        s_hhi, s_hlo, s_h, s_hr = sem("h_hi"), sem("h_lo"), sem("h_full"), sem("h_beside_r")
        s_rp, s_zp, s_cp = sem("r_pre"), sem("z_pre"), sem("cand_pre")
        s_r, s_z, s_nz, s_c = sem("r_done"), sem("z_done"), sem("one_less_z_done"), sem("cand_done")
        s_rhhi, s_rhlo = sem("rh_hi"), sem("rh_lo")
        s_khi, s_klo, s_k = sem("keep_hi"), sem("keep_lo"), sem("keep_full")
        s_shi, s_slo, s_s = sem("step_hi"), sem("step_lo"), sem("step_full")
        s_carry = sem("carried")
        s_zero = sem("factors_set")
        s_hist = sem("hist_copied")

        names = (("W_r", "U_r", "C_r", "b_r"), ("W_z", "U_z", "C_z", "b_z"), ("W", "U", "C", "b"))
        FILL = (2, 1, 3)
        PART_OF = ((0, 1), (0,))
        PAIRS = ((0, 0), (0, 1), (1, 0), (0, 2), (1, 1), (2, 0))
        pre = [[bank[2 * g + q][:, 0:SEG * C2].rearrange("p (t m b) -> p t m b", t=SEG, m=KD)
                for q in range(2)] for g in range(GATES)]

        def pre_of(g, q, jj):
            return pre[g][q][:, jj].rearrange("p m b -> p (m b)")

        with nc.Block() as block:
            @block.sync
            def _(sp):
                for g, (w, u, c, b) in enumerate(names):
                    sp.dma_start(U[:, g], A["L0_cond_" + u].rearrange("(k p) e -> p k e", p=P)).then_inc(s_uw, 16)
                for g, (w, u, c, b) in enumerate(names):
                    sp.dma_start(C[:, g], A["L0_cond_" + c].rearrange("(k p) e -> p k e", p=P)).then_inc(s_cw, 16)
                for g, (w, u, c, b) in enumerate(names):
                    sp.dma_start(W[:, g], A["L0_cond_" + w].rearrange("(k p) e -> p k e", p=P)).then_inc(s_w, 16)
                sp.wait_ge(s_x, 32)
                load_next(sp)
                sp.wait_ge(s_const, 16)

            @block.scalar
            def _(act):
                act.dma_start(ident[:], A["ident"]).then_inc(s_id, 16)
                act.dma_start(condT[:], A["condT"].rearrange("(k p) b -> p k b", p=P)).then_inc(s_cw, 16)

                def load_x(steps, done):
                    for k in range(KD):
                        act.dma_start(xT[:, k, :, steps],
                                      A["xT"][k * P:(k + 1) * P, :].rearrange("p (b s) -> p b s", b=B)[:, :, steps]).then_inc(done, 16)

                load_x(slice(0, EARLY), s_xe)
                for g, (w, u, c, b) in enumerate(names):
                    act.dma_start(bias[:, g], A["L0_cond_" + b].rearrange("(a e) -> a e", a=1).to_broadcast([B, D])).then_inc(s_cb, 16)
                act.dma_start(which[:], A["which"]).then_inc(s_which, 16)
                nc.scalar.preload_act_table(ACT.Sigmoid)
                load_x(slice(EARLY, S), s_x)
                act.dma_start(slot_row[:], A["slot_row"]).then_inc(s_const, 16)
                act.wait_ge(s_xe, 32)
                nc.scalar.activation(xs[:, 0, :, :, 0:EARLY], xT[:, :, :, 0:EARLY], ACT.Copy).then_inc(s_xs, 1)
                act.wait_ge(s_which, 16)
                nc.scalar.activation(which_bf[:], which[:], ACT.Copy).then_inc(s_vs, 1)
                act.wait_ge(s_vb, 2)
                nc.scalar.activation(vbs[:, 0], vb[:], ACT.Copy).then_inc(s_vs, 1)
                act.wait_ge(s_ws, 2)
                nc.scalar.activation(Ws[:, :, 1], rest[:], ACT.Copy).then_inc(s_ws, 1)
                act.wait_ge(s_x, 32)
                act.wait_ge(s_one, 1)
                nc.scalar.activation(xs[:, 0, :, :, EARLY:], xT[:, :, :, EARLY:], ACT.Copy).then_inc(s_xl, 1)
                act.wait_ge(s_scale, 2)
                inv = [act.alloc_register(f"inverse_scale{c}") for c in range(GATES + 1)]
                for c in range(GATES + 1):
                    act.reg_load(inv[c], scale[0:1, GATES + c:GATES + c + 1].bitcast(U32))
                with act.Fori(0, S // (2 * SEG)) as i:
                    n = i * (2 * SEG)
                    for j in range(2 * SEG):
                        q, jj = j // SEG, j % SEG
                        act.wait_ge(s_rp, n + (j + 1))
                        nc.scalar.activation(r, pre_of(0, q, jj), ACT.Sigmoid, scale=inv[0]).then_inc(s_r, 1)
                        act.wait_ge(s_zp, n + (j + 1))
                        nc.scalar.activation(nz[:], pre_of(1, q, jj), ACT.Sigmoid, scale=inv[3]).then_inc(s_nz, 1)
                        nc.scalar.activation(z, pre_of(1, q, jj), ACT.Sigmoid, scale=inv[1]).then_inc(s_z, 1)
                        act.wait_ge(s_cp, n + (j + 1))
                        nc.scalar.activation(cand, pre_of(2, q, jj), ACT.Tanh, scale=inv[2]).then_inc(s_c, 1)

            @block.gpsimd
            def _(pool):
                nc.gpsimd.memset(xT[:, :, :, S:S + SEG], 0.0).then_inc(s_one, 1)
                nc.gpsimd.memset(ones[:], 1.0).then_inc(s_one, 1)
                nc.gpsimd.memset(ones_bf[:], 1.0).then_inc(s_one, 1)
                pool.sem_inc(s_hist, 2)
                for first_part, done, steps in ((s_xs, s_xs, slice(0, EARLY)), (s_xl, s_xl, slice(EARLY, S + SEG))):
                    x, left = xT[:, :, :, steps], x_rest[:, :, :, steps]
                    part = [xs[:, p, :, :, steps] for p in range(PARTS)]
                    pool.wait_ge(first_part, 1)
                    for k in range(KD):
                        nc.gpsimd.tensor_tensor(left[:, k], x[:, k], part[0][:, k], ALU.subtract).then_inc(done, 1)
                    for k in range(KD):
                        nc.gpsimd.tensor_tensor(part[1][:, k], x[:, k], part[0][:, k], ALU.subtract).then_inc(done, 1)
                    pool.wait_ge(done, 1 + 2 * KD)
                    for k in range(KD):
                        nc.gpsimd.tensor_tensor(part[2][:, k], left[:, k], part[1][:, k], ALU.subtract).then_inc(done, 1)
                with pool.Fori(0, S // (2 * SEG)) as i:
                    n = i * (2 * SEG)
                    for q in range(2):
                        pool.wait_ge(s_h, n + (q * SEG + SEG + 1))
                        nc.gpsimd.tensor_copy(
                            hist[:, :, :, bass.ds(n + q * SEG, SEG)].rearrange("p k b t -> p (k b) t"),
                            ring[:, 1 + q * SEG:1 + q * SEG + SEG, :].rearrange("p t c -> p c t")).then_inc(s_hist, 1)

            @block.vector
            def _(dve):
                dve.wait_ge(s_uw, 16 * GATES)
                for g in range(GATES):
                    last = nc.vector.tensor_reduce(peak[:, g:g + 1], U[:, g].rearrange("p k e -> p (k e)"), AX.X, ALU.max,
                                                   apply_absolute_value=True)
                last.then_inc(s_peak, 1)
                dve.wait_ge(s_v, 1)
                dve.wait_ge(s_cb, 16 * GATES)
                nc.vector.tensor_tensor(vb[:, 0:2].rearrange("p g e -> p (g e)"), bank[6][0:B, :],
                                        bias[:, 0:2].rearrange("p g e -> p (g e)"), ALU.add).then_inc(s_vb, 1)
                dve.wait_ge(s_pt, 1)
                nc.vector.tensor_reduce(peaks[:, 0:1], bank[5][0:GATES, 0:P], AX.X, ALU.max).then_inc(s_sc, 1)
                dve.wait_ge(s_sc, 1)
                nc.vector.tensor_scalar(peaks[:, 0:1], peaks[:, 0:1], 1e-20, None, ALU.max).then_inc(s_sc, 1)
                dve.wait_ge(s_sc, 2)
                bits = peaks[:].bitcast(U32)
                nc.vector.tensor_scalar(bits[:, 1:2], bits[:, 0:1], EXP_BITS, None, ALU.bitwise_and).then_inc(s_sc, 1)
                dve.wait_ge(s_sc, 3)
                nc.vector.tensor_scalar(bits[:, 2:3], bits[:, 1:2], -1.0, float((2 * BIAS + TOP_EXP) << MANTISSA),
                                        ALU.mult, ALU.add)
                nc.vector.tensor_scalar(bits[:, 3:4], bits[:, 1:2], float(TOP_EXP << MANTISSA), None,
                                        ALU.subtract).then_inc(s_sc, 1)
                dve.wait_ge(s_sc, 4)
                dve.wait_ge(s_id, 16)
                for c in range(2):
                    last = nc.vector.tensor_scalar(scales[:, c * GATES:(c + 1) * GATES], ident[0:GATES, 0:GATES],
                                                   peaks[:, 2 + c:3 + c], None, ALU.mult)
                last.then_inc(s_sc, 1)
                dve.wait_ge(s_pt, 2)
                nc.vector.tensor_copy(scale[:, 0:2 * GATES], bank[3][:, 0:2 * GATES]).then_inc(s_scale, 1)
                dve.wait_ge(s_scale, 1)
                nc.vector.tensor_scalar(scale[:, 2 * GATES:], scale[:, GATES + 1:GATES + 2], -1.0, None, ALU.mult).then_inc(s_scale, 1)
                dve.wait_ge(s_v, 2)
                dve.wait_ge(s_vb, 1)
                nc.vector.tensor_tensor(vb[:, 2], bank[7][0:B, 0:D], bias[:, 2], ALU.add).then_inc(s_wsc, 1)
                dve.wait_ge(s_wsc, 1)
                for g in range(GATES):
                    last = nc.vector.tensor_scalar(vb[:, g], vb[:, g], scale[0:B, g:g + 1], None, ALU.mult)
                last.then_inc(s_vb, 1)
                dve.wait_ge(s_w, 16 * GATES)
                for g in range(GATES):
                    last = nc.vector.tensor_scalar(Ws[:, g, 0], W[:, g], scale[:, g:g + 1], None, ALU.mult)
                last.then_inc(s_ws, 1)
                dve.wait_ge(s_ws, 1)
                for g in range(GATES):
                    last = nc.vector.scalar_tensor_tensor(out=rest[:, g], in0=W[:, g], scalar=scale[:, g:g + 1], in1=Ws[:, g, 0],
                                                          op0=ALU.mult, op1=ALU.subtract)
                last.then_inc(s_ws, 1)
                dve.wait_ge(s_vs, 2)
                nc.vector.tensor_tensor(vb_rest[:], vb[:], vbs[:, 0], ALU.subtract).then_inc(s_vs, 1)
                nc.vector.tensor_tensor(vbs[:, 1], vb[:], vbs[:, 0], ALU.subtract).then_inc(s_vs, 1)
                dve.wait_ge(s_ws, 3)
                nc.vector.tensor_tensor(Ws[:, :, 2], rest[:], Ws[:, :, 1], ALU.subtract).then_inc(s_ws, 1)
                dve.wait_ge(s_vs, 4)
                nc.vector.tensor_tensor(vbs[:, 2], vb_rest[:], vbs[:, 1], ALU.subtract).then_inc(s_vs, 1)
                for g in range(GATES):
                    last = nc.vector.tensor_scalar(Us[:, g, 0], U[:, g], scale[:, g:g + 1], None, ALU.mult)
                last.then_inc(s_us, 1)
                dve.wait_ge(s_us, 1)
                for g in range(GATES):
                    last = nc.vector.scalar_tensor_tensor(out=Us[:, g, 1], in0=U[:, g], scalar=scale[:, g:g + 1], in1=Us[:, g, 0],
                                                          op0=ALU.mult, op1=ALU.subtract)
                last.then_inc(s_us, 1)
                nc.vector.memset(ring[:, 0], 0.0).then_inc(s_h, 1)
                nc.vector.memset(h_part[:, 0], 0.0).then_inc(s_hhi, 1)
                nc.vector.memset(h_part[:, 1], 0.0).then_inc(s_hlo, 1)
                for f in (r_h, z_cand, rh_high, step_high, step_low):
                    nc.vector.memset(f[:], 0.0).then_inc(s_zero, 1)
                dve.wait_ge(s_zero, 5)
                nc.vector.memset(rh_high[:, :, 0], -1.0).then_inc(s_zero, 1)
                nc.vector.memset(step_high[:, :, 0], -1.0).then_inc(s_shi, 1)
                dve.wait_ge(s_zero, 6)
                dve.sem_inc(s_hr, 1)
                dve.sem_inc(s_slo, 1)
                dve.sem_inc(s_carry, 1)

                def low_part(low, factors, high):
                    return nc.vector.tensor_tensor_scan(low[:].rearrange("p c s -> p (c s)"), factors[:].rearrange("p c s -> p (c s)"),
                                                        high[:].rearrange("p c s -> p (c s)"), 0.0, ALU.mult, ALU.subtract)

                with dve.Fori(0, S // (2 * SEG)) as i:
                    n = i * (2 * SEG)
                    dve.wait_ge(s_carry, i + 1)
                    for j in range(2 * SEG):
                        h, h_new = ring[:, j], ring[:, j + 1]
                        m = n + (j + 1)
                        dve.wait_ge(s_r, m)
                        nc.vector.tensor_tensor(rh_high[:, :, 2], r, h, ALU.mult).then_inc(s_rhhi, 1)
                        dve.wait_ge(s_rhhi, m)
                        dve.wait_ge(s_hr, m)
                        low_part(rh_low, r_h, rh_high).then_inc(s_rhlo, 1)
                        dve.wait_ge(s_nz, m)
                        nc.vector.tensor_tensor(keep_part[:, 0], nz[:], h, ALU.mult).then_inc(s_khi, 1)
                        nc.vector.tensor_tensor(keep[:], nz[:], h, ALU.mult).then_inc(s_k, 1)
                        dve.wait_ge(s_khi, m)
                        dve.wait_ge(s_k, m)
                        nc.vector.tensor_tensor(keep_part[:, 1], keep[:], keep_part[:, 0], ALU.subtract).then_inc(s_klo, 1)
                        dve.wait_ge(s_c, m)
                        dve.wait_ge(s_z, m)
                        nc.vector.tensor_tensor(step_high[:, :, 2], z, cand, ALU.mult).then_inc(s_shi, 1)
                        nc.vector.tensor_tensor(step_in[:], z, cand, ALU.mult).then_inc(s_s, 1)
                        dve.wait_ge(s_shi, m + 1)
                        low_part(step_low, z_cand, step_high).then_inc(s_slo, 1)
                        dve.wait_ge(s_s, m)
                        nc.vector.tensor_tensor(h_part[:, 0], step_in[:], keep[:], ALU.add).then_inc(s_hhi, 1)
                        if j % SEG == 0:
                            dve.wait_ge(s_hist, 2 * i + (1 + j // SEG))
                        nc.vector.tensor_tensor(h_new, step_in[:], keep[:], ALU.add).then_inc(s_h, 1)
                        nc.vector.tensor_tensor(r_h[:, :, 2], step_in[:], keep[:], ALU.add).then_inc(s_hr, 1)
                        dve.wait_ge(s_h, m + 1)
                        dve.wait_ge(s_hhi, m + 1)
                        nc.vector.tensor_tensor(h_part[:, 1], h_new, h_part[:, 0], ALU.subtract).then_inc(s_hlo, 1)
                    nc.vector.tensor_copy(ring[:, 0], ring[:, 2 * SEG]).then_inc(s_carry, 1)

            @block.tensor
            def _(pe):
                def cond_term(gates):
                    for g in gates:
                        o = bank[6][0:B, g * D:(g + 1) * D] if g < 2 else bank[7][0:B, 0:D]
                        for k in range(KD):
                            last = nc.tensor.matmul(o, condT[:, k], C[:, g, k], start=(k == 0), stop=(k == KD - 1))
                    last.then_inc(s_v, 1)

                pe.wait_ge(s_cw, 16 * (GATES + 1))
                cond_term((0, 1))
                pe.wait_ge(s_one, 3)
                pe.wait_ge(s_id, 16)
                pe.wait_ge(s_peak, 1)
                nc.tensor.transpose(bank[5][0:GATES, 0:P], peak[:], ident[:]).then_inc(s_pt, 1)
                cond_term((2,))
                pe.wait_ge(s_sc, 5)
                nc.tensor.matmul(bank[3][:, 0:2 * GATES], ones[0:GATES, :], scales[:], start=True, stop=True).then_inc(s_pt, 1)

                def input_terms(q, t0):
                    for g in range(GATES):
                        for m in range(KD):
                            o = pre[g][q][:, :, m, :]
                            cols = slice(m * P, (m + 1) * P)
                            for k in range(KD):
                                for w, x in PAIRS:
                                    yield lambda o=o, g=g, k=k, w=w, x=x, cols=cols, m=m: nc.tensor.matmul(
                                        o, Ws[:, g, w, k, cols], xs[:, x, k, :, bass.ds(t0, SEG)].rearrange("p b t -> p t b"),
                                        start=(m == 0 and k == 0 and w == 0 and x == 0), stop=False, skip_group_check=True)
                            for p in range(PARTS):
                                yield lambda o=o, g=g, p=p, cols=cols: nc.tensor.matmul(
                                    o, vbs[:, p, g, cols], which_bf[:], start=False, stop=False, skip_group_check=True)

                state = [h_part[:, p] for p in range(2)]
                kept = [keep_part[:, p] for p in range(2)]
                reset = [rh_high[:, :, 2], rh_low[:, :, 2]]
                step = [step_high[:, :, 2], step_low[:, :, 2]]

                def recur(g, q, jj, x, part):
                    for m in range(KD):
                        for k in range(KD):
                            for p in PART_OF[part]:
                                last = nc.tensor.matmul(pre[g][q][:, jj, m, :], Us[:, g, p, k, m * P:(m + 1) * P],
                                                        x[part][:, k * B:(k + 1) * B],
                                                        start=False, stop=False, skip_group_check=True)
                    return last

                pe.wait_ge(s_ws, 4)
                pe.wait_ge(s_xs, 1 + 3 * KD)
                pe.wait_ge(s_vs, 5)
                for f in input_terms(0, 0):
                    f()
                pe.wait_ge(s_us, 2)
                with pe.Fori(0, S // (2 * SEG)) as i:
                    n = i * (2 * SEG)
                    for q in range(2):
                        ahead = list(input_terms(1 - q, n + (q + 1) * SEG))
                        assert len(ahead) <= sum(FILL) * (SEG - 1)

                        def fill(jj, slot):
                            at = jj * sum(FILL) + sum(FILL[:slot])
                            if jj < SEG - 1:
                                for f in ahead[at:at + FILL[slot]]:
                                    f()

                        for jj in range(SEG):
                            j = q * SEG + jj
                            m = n + (j + 1)
                            pe.wait_ge(s_shi, m)
                            recur(0, q, jj, step, 0)
                            pe.wait_ge(s_slo, m)
                            recur(0, q, jj, step, 1).then_inc(s_rp, 1)
                            pe.wait_ge(s_hhi, m)
                            recur(1, q, jj, state, 0)
                            fill(jj, 0)
                            pe.wait_ge(s_hlo, m)
                            recur(1, q, jj, state, 1).then_inc(s_zp, 1)
                            fill(jj, 1)
                            pe.wait_ge(s_rhhi, m)
                            recur(2, q, jj, reset, 0)
                            pe.wait_ge(s_rhlo, m)
                            recur(2, q, jj, reset, 1).then_inc(s_cp, 1)
                            nq, njj = (q, jj + 1) if jj < SEG - 1 else (1 - q, 0)
                            pe.wait_ge(s_khi, m)
                            recur(0, nq, njj, kept, 0)
                            fill(jj, 2)
                            pe.wait_ge(s_klo, m)
                            recur(0, nq, njj, kept, 1)
                    pe.wait_ge(s_xl, 1 + 3 * KD)


def layer0_ffn(nc, sb, sem, bank, xT, hist, ident, ones_bf, weights, s_w, load_next, s_raw, raw, parts):
    with ExitStack() as own:
        def t(name, shape, dt=F32):
            return own.enter_context(nc.sbuf_tensor(name, shape, dt))

        wr, br, b1, b2, whole = weights
        UP = KD * HID
        w1 = [v[:, 0:UP].rearrange("p (k f) -> p k f", k=KD) for v in parts[1]]
        w2 = [v[:, UP:].rearrange("p (f d) -> p f d", f=KH) for v in parts[1]]
        PIECES = raw.shape[1] // S
        ORDER = (0, 2, 1, 3) + tuple(range(4, PIECES))
        FIRST = UP // S
        wr_rep = t("wr_rep", [P, KD, P])
        ws = t("ws", [P, S])
        wcol = t("wcol", [P, S // P])
        ge = t("ge", [P, S // P, S], BF16)
        mask = t("mask", [P, S], U32)
        state = [t(f"state_part{p}", [P, KD, S], F32R) for p in range(2)]
        hid = [t(f"hid_part{p}", [P, KH, S], F32R) for p in range(2)]
        full = t("hid_full", [P, 2, S])
        blk = t("blk", [P, KD, S])
        sel = t("sel", [P, KD, S])

        s_rep = sem("router_weights_spread")
        s_whi, s_wlo = sem("ffn_weights_high"), sem("ffn_weights_low")
        s_sthi, s_stlo = sem("state_high"), sem("state_low")
        s_sp, s_s = sem("scores_pre"), sem("scores_done")
        s_tp, s_t = sem("scores_turned"), sem("score_cols")
        s_ge, s_cnt, s_m = sem("compared"), sem("counted"), sem("mask_done")
        s_fp, s_f, s_flo = sem("hidden_pre"), sem("hidden_done"), sem("hidden_low")
        s_dp, s_d = sem("block_pre"), sem("block_done")
        s_sel, s_y = sem("selected"), sem("layer0_done")
        s_pass = sem("ffn_waits_passed")
        s_high, s_low = sem("next_high_parts"), sem("next_low_parts")
        up = [bank[3], bank[4], bank[7]]

        def piece(i):
            return slice(i * S, (i + 1) * S)

        def states(b):
            return hist[:, :, bass.ds(b, 1), :].rearrange("p k b t -> p k (b t)")

        with nc.Block() as block:
            @block.sync
            def _(sp):
                load_next(sp)

            @block.tensor
            def _(pe):
                pe.wait_ge(s_rep, KD)
                with pe.Fori(0, B) as b:
                    for k in range(KD):
                        last = nc.tensor.matmul(bank[0][:], wr_rep[:, k], hist[:, k, bass.ds(b, 1), :].rearrange("p b t -> p (b t)"),
                                                start=(k == 0), stop=(k == KD - 1))
                    last.then_inc(s_sp, 1)
                    pe.wait_ge(s_stlo, b + 1)
                    for f in range(KH):
                        if f >= len(up):
                            pe.wait_ge(s_f, b * KH + (f + 1 - len(up)))
                        if f == 0 or f == KH // 2:
                            pe.wait_ge(s_wlo, FIRST if f else FIRST // 2)
                        for k in range(KD):
                            for w, x in MEET:
                                last = nc.tensor.matmul(up[f % len(up)][:], w1[w][:, k, f * P:(f + 1) * P], state[x][:, k],
                                                        start=(k == 0 and w == 0 and x == 0), stop=(k == KD - 1 and x == 1))
                        last.then_inc(s_fp, 1)
                        if f == 1:
                            pe.wait_ge(s_s, b + 1)
                            for j in range(S // P):
                                last = nc.tensor.transpose(bank[1][:, j * P:(j + 1) * P], ws[:, j * P:(j + 1) * P], ident[:])
                            last.then_inc(s_tp, 1)
                        if f == 5:
                            pe.wait_ge(s_ge, b + 1)
                            for j in range(S // P):
                                last = nc.tensor.matmul(bank[2][:], ones_bf[:], ge[:, j], start=(j == 0), stop=(j == S // P - 1))
                            last.then_inc(s_cnt, 1)
                    pe.wait_ge(s_wlo, PIECES)
                    for d in range(KD):
                        for f in range(KH):
                            if d == 0:
                                pe.wait_ge(s_flo, b * KH + (f + 1))
                            for w, x in MEET:
                                last = nc.tensor.matmul(bank[5 + d][:], w2[w][:, f, d * P:(d + 1) * P], hid[x][:, f],
                                                        start=(f == 0 and w == 0 and x == 0), stop=(f == KH - 1 and x == 1))
                        last.then_inc(s_dp, 1)

            @block.scalar
            def _(act):
                def high_states(b):
                    nc.scalar.activation(state[0][:], states(b), ACT.Copy).then_inc(s_sthi, 1)

                def body(b, more):
                    act.wait_ge(s_sp, b + 1)
                    nc.scalar.activation(ws[:], bank[0][:], ACT.Identity, bias=br[:, 0:1]).then_inc(s_s, 1)
                    for f in range(KH):
                        act.wait_ge(s_fp, b * KH + (f + 1))
                        if f >= 2:
                            act.wait_ge(s_flo, b * KH + (f - 1))
                        nc.scalar.activation(hid[0][:, f], up[f % len(up)][:], ACT.Gelu, bias=b1[:, f:f + 1])
                        nc.scalar.activation(full[:, f % 2], up[f % len(up)][:], ACT.Gelu, bias=b1[:, f:f + 1]).then_inc(s_f, 1)
                    if more:
                        high_states(b + 1)
                    for d in range(KD):
                        act.wait_ge(s_dp, b * KD + (d + 1))
                        nc.scalar.activation(blk[:, d], bank[5 + d][:], ACT.Identity, bias=b2[:, d:d + 1]).then_inc(s_d, 1)

                act.wait_ge(s_w, 96)
                high_states(0)
                for i in ORDER:
                    nc.scalar.activation(parts[1][0][:, piece(i)], whole[:, piece(i)], ACT.Copy).then_inc(s_whi, 1)
                with act.Fori(0, B - 1) as b:
                    body(b, True)
                body(B - 1, False)

            @block.gpsimd
            def _(pool):
                high, low = parts[0]
                pool.wait_ge(s_raw, 64)
                for i in range(PIECES):
                    nc.gpsimd.tensor_copy(high[:, piece(i)], raw[:, piece(i)]).then_inc(s_high, 1)
                    pool.wait_ge(s_high, i + 1)
                    nc.gpsimd.tensor_tensor(low[:, piece(i)], raw[:, piece(i)], high[:, piece(i)].bitcast(F32), ALU.subtract).then_inc(s_low, 1)
                pool.wait_ge(s_low, PIECES)

            @block.vector
            def _(dve):
                def low_states(b):
                    dve.wait_ge(s_sthi, b + 1)
                    nc.vector.tensor_tensor(state[1][:], states(b), state[0][:].bitcast(F32), ALU.subtract).then_inc(s_stlo, 1)

                def body(b, more):
                    for f in range(KH):
                        dve.wait_ge(s_f, b * KH + (f + 1))
                        nc.vector.tensor_tensor(hid[1][:, f], full[:, f % 2], hid[0][:, f].bitcast(F32), ALU.subtract).then_inc(s_flo, 1)
                        if f == 1:
                            dve.wait_ge(s_tp, b + 1)
                            nc.vector.tensor_copy(wcol[:], bank[1][:].rearrange("p (j c) -> p j c", c=P)[:, :, 0]).then_inc(s_t, 1)
                        if f == 2:
                            dve.wait_ge(s_t, b + 1)
                            dve.wait_ge(s_s, b + 1)
                            for j in range(S // P):
                                last = nc.vector.tensor_scalar(ge[:, j], ws[:], wcol[:, j:j + 1], None, ALU.is_le)
                            last.then_inc(s_ge, 1)
                    dve.wait_ge(s_cnt, b + 1)
                    nc.vector.tensor_scalar(mask[:], bank[2][:], float(SELECT - 1), None, ALU.is_le).then_inc(s_m, 1)
                    if more:
                        low_states(b + 1)
                    dve.wait_ge(s_m, b + 1)
                    for d in range(KD):
                        h = hist[:, d, bass.ds(b, 1), :].rearrange("p b t -> p (b t)")
                        x = xT[:, d, bass.ds(b, 1), 0:S].rearrange("p b t -> p (b t)")
                        nc.vector.tensor_copy(sel[:, d], h).then_inc(s_sel, 1)
                        dve.wait_ge(s_sel, (b * KD + d) * 2 + 1)
                        dve.wait_ge(s_d, b * KD + (d + 1))
                        dve.sem_inc(s_pass, 1)
                        nc.vector.copy_predicated(sel[:, d], mask[:], blk[:, d]).then_inc(s_sel, 1)
                        dve.wait_ge(s_sel, (b * KD + d) * 2 + 2)
                        nc.vector.tensor_tensor(x, x, sel[:, d], ALU.add).then_inc(s_y, 1)

                dve.wait_ge(s_w, 96)
                for k in range(KD):
                    nc.vector.tensor_copy(wr_rep[:, k], wr[:, k:k + 1].to_broadcast([P, P])).then_inc(s_rep, 1)
                low_states(0)
                for n, i in enumerate(ORDER):
                    dve.wait_ge(s_whi, n + 1)
                    nc.vector.tensor_tensor(parts[1][1][:, piece(i)], whole[:, piece(i)],
                                            parts[1][0][:, piece(i)].bitcast(F32), ALU.subtract).then_inc(s_wlo, 1)
                with dve.Fori(0, B - 1) as b:
                    body(b, True)
                body(B - 1, False)


def layer1_context(nc, sb, sem, A, bank, xT, hist, ident, ones, condT, weights, raw, parts, s_w, load_next):
    with ExitStack() as own:
        def t(name, shape, dt=F32):
            return own.enter_context(nc.sbuf_tensor(name, shape, dt))

        gw, gb, tw, tb, b1, b2 = weights
        UP = KD * HID
        PIECES = raw.shape[1] // S
        w1 = [[v[:, 0:UP].rearrange("p (k f) -> p k f", k=KD) for v in q] for q in parts]
        w2 = [[v[:, UP:].rearrange("p (f d) -> p f d", f=KH) for v in q] for q in parts]
        xs = [t(f"x_part{p}", [P, KD, B, S], F32R) for p in range(2)]
        hid = [t(f"ehid_part{p}", [P, KH, S], F32R) for p in range(2)]
        full = t("ehid_full", [P, 2, S])
        tmp = t("etmp", [P, KD, S])
        sums = t("sums", [P, 3, KD, B])
        gate_in = t("gate_in", [P, 3, KD, B])
        silu_c = t("silu_c", [P, KD, B])
        mod = t("mod", [B, 2 * NE0])
        lg = t("lg", [B, 3, NE0])
        sm = t("sm", [B, 8])
        score = t("score", [B, 8])
        top = t("top", [B, 8])
        idx = t("idx", [B, 8], U32)
        idxf = t("idxf", [B, TOP0])
        wk = t("wk", [B, TOP0])
        off = t("off", [B, TOP0, 2])
        ck = t("ck", [B, TOP0, 3])
        ckd = t("ckd", [B, B, TOP0, 3])
        coef = t("coef", [P, B, TOP0, 3])

        s_ew = [sem(f"expert_loaded{k}") for k in range(TOP0)]
        s_silu = sem("cond_silu")
        s_g = sem("gate_chain")
        s_gin, s_gp, s_ex = sem("gate_in_done"), sem("gate_pre"), sem("gate_exp")
        s_idx, s_ckd, s_cf = sem("experts_chosen"), sem("coef_rows"), sem("coef_spread")
        s_coef = sem("coef_done")
        s_xhi, s_xlo = sem("x_high"), sem("x_low")
        s_whi, s_wlo = sem("weights_high"), sem("weights_low")
        s_fp, s_f, s_flo = sem("ehidden_pre"), sem("ehidden_done"), sem("ehidden_low")
        s_dp, s_d = sem("eblock_pre"), sem("eblock_done")
        s_add = sem("eblock_added")
        up = bank[1:5]
        GATE_STEPS = 6

        def place(k):
            return 1 - k

        def expert(b, k):
            return b * TOP0 + k

        with nc.Block() as block:
            @block.sync
            def _(sp):
                sp.wait_ge(s_idx, 1)
                for n in range(B * TOP0):
                    b, k = n // TOP0, n % TOP0
                    e = sp.value_load(idx[b:b + 1, k:k + 1], min_val=0, max_val=NE0 - 1)
                    one, u = bass.ds(e, 1), 1 + k
                    if n:
                        sp.wait_ge(s_wlo, n * PIECES)
                    if b:
                        sp.wait_ge(s_d, (B + n - TOP0 + 1) * KD)
                    sp.dma_start(raw[:, 0:UP].rearrange("p (k f) -> p k f", k=KD),
                                 A["L1_cond_ew1"][one].rearrange("o (k p) f -> p (o k) f", p=P)).then_inc(s_ew[k], 16)
                    sp.dma_start(raw[:, UP:].rearrange("p (f d) -> p f d", f=KH),
                                 A["L1_cond_ew2"][one].rearrange("o (f p) d -> p (o f) d", p=P)).then_inc(s_ew[k], 16)
                    sp.dma_start(b1[:, u], A["L1_cond_eb1"][one].rearrange("o p f -> p (o f)")).then_inc(s_ew[k], 16)
                    sp.dma_start(b2[:, u], A["L1_cond_eb2"][one].rearrange("o p k -> p (o k)")).then_inc(s_ew[k], 16)
                    if n == 0:
                        load_next(sp)

            @block.tensor
            def _(pe):
                def unit(m, b, q):
                    for f in range(KH):
                        if f >= len(up) or not isinstance(m, int) or m:
                            pe.wait_ge(s_f, m * KH + (f + 1 - len(up)))
                        for k in range(KD):
                            for w, x in MEET:
                                last = nc.tensor.matmul(up[f % len(up)][:], w1[q][w][:, k, f * P:(f + 1) * P],
                                                        xs[x][:, k, bass.ds(b, 1), :].rearrange("p b t -> p (b t)"),
                                                        start=(k == 0 and w == 0 and x == 0), stop=(k == KD - 1 and x == 1))
                        last.then_inc(s_fp, 1)
                    for d in range(KD):
                        if not isinstance(m, int) or m:
                            pe.wait_ge(s_d, m * KD + (d + 1 - KD))
                        for f in range(KH):
                            if d == 0:
                                pe.wait_ge(s_flo, m * KH + (f + 1))
                            for w, x in MEET:
                                last = nc.tensor.matmul(bank[5 + d][:], w2[q][w][:, f, d * P:(d + 1) * P], hid[x][:, f],
                                                        start=(f == 0 and w == 0 and x == 0), stop=(f == KH - 1 and x == 1))
                        last.then_inc(s_dp, 1)

                def shared(b):
                    pe.wait_ge(s_xlo, b + 1)
                    unit(b, b, 0)

                def chosen(b, k):
                    pe.wait_ge(s_wlo, expert(b, k) * PIECES + PIECES)
                    unit(expert(b, k) + B, b, place(k))

                shared(0)
                pe.wait_ge(s_w, 64)
                pe.wait_ge(s_silu, 1)
                for k in range(KD):
                    nc.tensor.matmul(bank[7][0:B, 0:2 * NE0], silu_c[:, k], tw[:, k], start=(k == 0), stop=False)
                nc.tensor.matmul(bank[7][0:B, 0:2 * NE0], ones[0:1, 0:B], tb[:], start=False, stop=True).then_inc(s_gp, 1)
                pe.wait_ge(s_gin, 1)
                for c in range(3 * KD):
                    nc.tensor.matmul(bank[0][0:B, 0:NE0], gate_in[:, c // KD, c % KD], gw[:, c], start=(c == 0), stop=False)
                nc.tensor.matmul(bank[0][0:B, 0:NE0], ones[0:1, 0:B], gb[:], start=False, stop=True).then_inc(s_gp, 1)
                with pe.Fori(1, B) as b:
                    shared(b)
                pe.wait_ge(s_ckd, 1)
                nc.tensor.matmul(bank[7][:, 0:B * TOP0 * 3], ones[0:B, :],
                                 ckd[:].rearrange("q b k r -> q (b k r)"), start=True, stop=True).then_inc(s_cf, 1)
                with pe.Fori(0, B) as b:
                    for k in range(TOP0):
                        chosen(b, k)

            @block.scalar
            def _(act):
                for b in range(B):
                    nc.scalar.activation(xs[0][:, :, b], xT[:, :, b, 0:S], ACT.Copy).then_inc(s_xhi, 1)
                nc.scalar.activation(silu_c[:], condT[:], ACT.Silu).then_inc(s_silu, 1)

                def unit(m, b, u, out_of, split_next=None):
                    for f in range(KH):
                        act.wait_ge(s_fp, m * KH + (f + 1))
                        if f >= 2 or not isinstance(m, int) or m:
                            act.wait_ge(s_flo, m * KH + (f - 1))
                        nc.scalar.activation(hid[0][:, f], up[f % len(up)][:], ACT.Gelu_apprx_tanh, bias=b1[:, u, f:f + 1])
                        nc.scalar.activation(full[:, f % 2], up[f % len(up)][:], ACT.Gelu_apprx_tanh,
                                             bias=b1[:, u, f:f + 1]).then_inc(s_f, 1)
                    if split_next:
                        split_next()
                    for d in range(KD):
                        act.wait_ge(s_dp, m * KD + (d + 1))
                        out_of(d)

                def split(b, k):
                    act.wait_ge(s_ew[k], b * 64 + 64)
                    for i in range(PIECES):
                        piece = slice(i * S, (i + 1) * S)
                        nc.scalar.activation(parts[place(k)][0][:, piece], raw[:, piece], ACT.Copy).then_inc(s_whi, 1)

                def shared(b, split_next=None):
                    def out_of(d):
                        nc.scalar.activation(hist[:, d, bass.ds(b, 1), :].rearrange("p b t -> p (b t)"), bank[5 + d][:],
                                             ACT.Identity, bias=b2[:, 0, d:d + 1]).then_inc(s_d, 1)

                    unit(b, b, 0, out_of, split_next)

                def chosen(b, k, split_next=None):
                    def out_of(d):
                        act.wait_ge(s_add, expert(b, k) * KD + (d + 1))
                        nc.scalar.activation(tmp[:, d], bank[5 + d][:], ACT.Identity, bias=b2[:, 1 + k, d:d + 1]).then_inc(s_d, 1)

                    unit(expert(b, k) + B, b, 1 + k, out_of, split_next)

                shared(0)
                act.wait_ge(s_g, GATE_STEPS)
                nc.scalar.activation(lg[:, 2], lg[:, 1], ACT.Exp, bias=sm[:, 0:1], accum_out=sm[:, 1:2]).then_inc(s_ex, 1)
                with act.Fori(1, B - 1) as b:
                    shared(b)
                shared(B - 1, lambda: split(0, 0))
                with act.Fori(0, B - 1) as b:
                    chosen(b, 0, lambda: split(b, 1))
                    chosen(b, 1, lambda: split(b + 1, 0))
                chosen(B - 1, 0, lambda: split(B - 1, 1))
                chosen(B - 1, 1)

            @block.gpsimd
            def _(pool):
                for b in range(1, B):
                    pool.wait_ge(s_xhi, b + 1)
                    pool.wait_ge(s_xlo, b)
                    nc.gpsimd.tensor_tensor(xs[1][:, :, b], xT[:, :, b, 0:S], xs[0][:, :, b].bitcast(F32), ALU.subtract).then_inc(s_xlo, 1)

            @block.vector
            def _(dve):
                dve.sem_inc(s_add, KD)
                done = [0]

                def chain(ins):
                    done[0] += 1
                    ins.then_inc(s_g, 1)
                    dve.wait_ge(s_g, done[0])

                def low_tile(m, f):
                    dve.wait_ge(s_f, m * KH + (f + 1))
                    nc.vector.tensor_tensor(hid[1][:, f], full[:, f % 2], hid[0][:, f].bitcast(F32), ALU.subtract).then_inc(s_flo, 1)

                def split(b, k):
                    for i in range(PIECES):
                        piece = slice(i * S, (i + 1) * S)
                        dve.wait_ge(s_whi, expert(b, k) * PIECES + (i + 1))
                        nc.vector.tensor_tensor(parts[place(k)][1][:, piece], raw[:, piece],
                                                parts[place(k)][0][:, piece].bitcast(F32), ALU.subtract).then_inc(s_wlo, 1)

                def shared(b):
                    for f in range(KH):
                        low_tile(b, f)

                def chosen(b, k, split_next=None):
                    for f in range(KH):
                        low_tile(expert(b, k) + B, f)
                    if split_next:
                        split_next()
                    for d in range(KD):
                        dve.wait_ge(s_d, (expert(b, k) + B) * KD + (d + 1))
                        if k:
                            dve.wait_ge(s_add, expert(b, k) * KD + (d + 1))
                        for i, (a, z) in enumerate(REGIONS):
                            acc = hist[:, d, bass.ds(b, 1), a:z].rearrange("p b t -> p (b t)")
                            last = nc.vector.scalar_tensor_tensor(
                                out=acc, in0=tmp[:, d, a:z], scalar=coef[:, bass.ds(b, 1), k, i:i + 1].rearrange("p b i -> p (b i)"),
                                in1=acc, op0=ALU.mult, op1=ALU.add)
                        last.then_inc(s_add, 1)

                dve.wait_ge(s_xhi, 1)
                nc.vector.tensor_tensor(xs[1][:, :, 0], xT[:, :, 0, 0:S], xs[0][:, :, 0].bitcast(F32), ALU.subtract).then_inc(s_xlo, 1)
                (h0, h1), (w0, w1_), (p0, p1) = REGIONS
                for f in range(KH):
                    low_tile(0, f)
                    if f % 2 and f // 2 < 3:
                        a, z = REGIONS[f // 2]
                        last = nc.vector.tensor_reduce(sums[:, f // 2], xT[:, :, :, a:z], AX.X, ALU.add)
                chain(last)
                nc.vector.tensor_tensor(gate_in[:, 1], sums[:, 0], sums[:, 2], ALU.add)
                chain(nc.vector.tensor_tensor(gate_in[:, 2], sums[:, 1], sums[:, 2], ALU.add))
                chain(nc.vector.tensor_tensor(gate_in[:, 0], gate_in[:, 1], sums[:, 1], ALU.add))
                nc.vector.tensor_scalar(gate_in[:, 0], gate_in[:, 0], 1.0 / S, None, ALU.mult)
                nc.vector.tensor_scalar(gate_in[:, 1], gate_in[:, 1], 1.0 / (h1 - h0 + p1 - p0), None, ALU.mult)
                nc.vector.tensor_scalar(gate_in[:, 2], gate_in[:, 2], 1.0 / (w1_ - w0 + p1 - p0), None,
                                        ALU.mult).then_inc(s_gin, 1)
                dve.wait_ge(s_gp, 2)
                chain(nc.vector.tensor_copy(mod[:], bank[7][0:B, 0:2 * NE0]))
                chain(nc.vector.scalar_tensor_tensor(out=lg[:, 0], in0=mod[:, 0:NE0], scalar=1.0, in1=bank[0][0:B, 0:NE0],
                                                     op0=ALU.add, op1=ALU.mult))
                nc.vector.memset(score[:], -1.0)
                nc.vector.tensor_tensor(lg[:, 1], lg[:, 0], mod[:, NE0:], ALU.add).then_inc(s_gin, 1)
                dve.wait_ge(s_gin, 2)
                nc.vector.tensor_reduce(sm[:, 0:1], lg[:, 1], AX.X, ALU.max, negate=True).then_inc(s_g, 1)
                done[0] += 1
                assert done[0] == GATE_STEPS
                dve.wait_ge(s_ex, 1)
                chain(nc.vector.reciprocal(sm[:, 2:3], sm[:, 1:2]))
                chain(nc.vector.tensor_scalar(score[:, 0:NE0], lg[:, 2], sm[:, 2:3], None, ALU.mult))
                chain(nc.vector.max(top[:], score[:]))
                nc.vector.max_index(idx[:], top[:], score[:]).then_inc(s_idx, 1)
                chain(nc.vector.tensor_reduce(sm[:, 3:4], top[:, 0:TOP0], AX.X, ALU.add))
                chain(nc.vector.tensor_scalar(sm[:, 4:5], sm[:, 3:4], 1e-8, None, ALU.add))
                chain(nc.vector.reciprocal(sm[:, 5:6], sm[:, 4:5]))
                chain(nc.vector.tensor_scalar(wk[:], top[:, 0:TOP0], sm[:, 5:6], None, ALU.mult))
                dve.wait_ge(s_idx, 1)
                chain(nc.vector.tensor_copy(idxf[:], idx[:, 0:TOP0]))
                nc.vector.tensor_scalar(off[:, :, 0], idxf[:], 2.0, None, ALU.not_equal)
                chain(nc.vector.tensor_scalar(off[:, :, 1], idxf[:], 1.0, None, ALU.not_equal))
                nc.vector.tensor_tensor(ck[:, :, 0], off[:, :, 0], wk[:], ALU.mult)
                nc.vector.tensor_tensor(ck[:, :, 1], off[:, :, 1], wk[:], ALU.mult)
                chain(nc.vector.tensor_copy(ck[:, :, 2], wk[:]))
                for b in range(B):
                    last = nc.vector.tensor_scalar(ckd[:, b].rearrange("q k r -> q (k r)"),
                                                   ck[:].rearrange("q k r -> q (k r)"), ident[0:B, b:b + 1], None, ALU.mult)
                last.then_inc(s_ckd, 1)
                with dve.Fori(1, B) as b:
                    shared(b)
                split(0, 0)
                dve.wait_ge(s_cf, 1)
                nc.vector.tensor_copy(coef[:].rearrange("p b k r -> p (b k r)"), bank[7][:, 0:B * TOP0 * 3]).then_inc(s_coef, 1)
                dve.wait_ge(s_coef, 1)
                with dve.Fori(0, B - 1) as b:
                    chosen(b, 0, lambda: split(b, 1))
                    chosen(b, 1, lambda: split(b + 1, 0))
                chosen(B - 1, 0, lambda: split(B - 1, 1))
                chosen(B - 1, 1)
                dve.wait_ge(s_add, KD + B * TOP0 * KD)


def routing(nc, sb, sem, A, bank, xT, hist, ident, ones, slot_row, weights, s_wg, s_w, load_next, gather, tok, ctx_rows, out, s_out):
    with ExitStack() as own:
        def t(name, shape, dt=F32):
            return own.enter_context(nc.sbuf_tensor(name, shape, dt))

        TH = T // 2
        GROUPS, GT = 2, TILES // 2
        BT = S // P
        turn, sw1, sw2 = weights
        vrev = t("vrev", [P, TH])
        shift = t("shift", [P, P])
        rows = t("rows", [P, TILES, ROW])
        sw = [t(f"shared_part{p}", [P, KF, KD, 2, P], F32R) for p in range(2)]
        x_part = [t(f"context_part{p}", [P, KD, S], F32R) for p in range(2)]
        lin, act_f = t("lin", [P, 2, S]), t("act_f", [P, KF, S])
        gates = t("gates", [P, TILES, NE])
        left = t("left", [P, TILES, NE])
        maskT = left[:].rearrange("p t e -> p (t e)")
        top8 = t("top8", [P, TILES, TOPK])
        st = t("st", [P, 4, TILES])
        cum = t("cum", [P, TH])
        before = t("before", [P, 1])
        order = t("order", [P, 2, CAP])
        slots = t("slots", [P, 4, NE])
        orow = t("orow", [P, 2, BT, D])

        s_c, s_lg, s_ex = sem("route_chain"), sem("logits_less_max"), sem("route_exp")
        s_mt, s_off = sem("mask_turned"), sem("offset_pre")
        s_ot = sem("order_turned")
        s_rt, s_rc = sem("rows_turned"), sem("rows_copied")
        s_dense, s_rows = sem("dense_done"), sem("rows_stored")
        s_v, s_z = sem("list_constants_loaded"), sem("spare_zero")
        s_whi, s_wlo = sem("shared_expert_high"), sem("shared_expert_low")
        s_xhi, s_xlo = sem("context_high"), sem("context_low")
        s_up, s_lin, s_silu = sem("up_pre"), sem("lin_copied"), sem("silu_done")
        s_act = sem("gated")
        s_tok = sem("tables_done")
        s_dp, s_base = sem("shared_pre"), sem("base_done")
        s_bt, s_bc = sem("base_turned"), sem("base_copied")
        s_sum = sem("base_summed")
        up = [(bank[0], bank[1]), (bank[2], bank[3])]
        down = [bank[4], bank[5]]

        raw_w = sw1.rearrange("p k (s f) -> p k s f", s=2)

        def columns(f):
            return raw_w[:, :, :, f * P:(f + 1) * P]

        def tile_of(i):
            return (i % 2) * HALF + i // 2

        with nc.Block() as block:
            @block.sync
            def _(sp):
                sp.dma_start(vrev[:], A["vrev"]).then_inc(s_v, 16)
                sp.dma_start(shift[:], A["shift"]).then_inc(s_v, 16)
                load_next(sp)
                sp.wait_ge(s_z, 1)
                for a, z in CAPS:
                    sp.dma_start(ctx_rows[T + a:T + z, :], cum[0:z - a, 0:ROW]).then_inc(s_rows, 16)
                    sp.dma_start(out[T + a:T + z, :], cum[0:z - a, 0:D]).then_inc(s_rows, 16)
                sp.wait_ge(s_rows, 64)
                sp.sem_inc(s_z, 1)
                sp.wait_ge(s_dense, GROUPS)
                sp.wait_ge(s_rc, TILES)
                v = ctx_rows[0:T, :].rearrange("(h j p) c -> p j h c", h=2, p=P)
                r4 = rows[:].rearrange("p (j h) c -> p j h c", h=2)
                for h in range(2):
                    sp.dma_start(v[:, :, h], r4[:, :, h]).then_inc(s_rows, 16)
                for b in range(B):
                    sp.wait_ge(s_bc, (b + 1) * KD)
                    sp.dma_start(out[b * S:(b + 1) * S, :].rearrange("(j p) d -> p j d", p=P), orow[:, b % 2]).then_inc(s_out[b % 2], 16)
                sp.wait_ge(s_rows, 96)

            @block.tensor
            def _(pe):
                pe.wait_ge(s_wg, 16)
                for i in range(TILES):
                    c = tile_of(i)
                    b, o = c * P // S, c * P % S
                    if i >= 4:
                        pe.wait_ge(s_rc, i - 3)
                    for k in range(KD):
                        last = nc.tensor.matmul(bank[i % 4][:, k * P:k * P + P + NE], hist[:, k, b, o:o + P], turn[:, k],
                                                start=(k == 0), stop=(k == KD - 1), skip_group_check=True)
                    last.then_inc(s_rt, 1)

                def turn_base(b):
                    pe.wait_ge(s_sum, b + 1)
                    for j in range(BT):
                        for k in range(KD):
                            last = nc.tensor.transpose(down[j // 2][:, (j % 2) * D + k * P:(j % 2) * D + (k + 1) * P],
                                                       xT[:, k, b, j * P:(j + 1) * P], ident[:])
                        if j % 2:
                            last.then_inc(s_bt, 1)

                pe.wait_ge(s_rc, TILES)
                for b in range(B):
                    pe.wait_ge(s_xlo, b + 1)
                    for f in range(KF):
                        if b == 0:
                            pe.wait_ge(s_wlo, f + 1)
                        n = b * KF + f
                        if n >= 2:
                            pe.wait_ge(s_silu, n - 1)
                            pe.wait_ge(s_lin, n - 1)
                        for s_ in range(2):
                            for k in range(KD):
                                for w, x in MEET:
                                    last = nc.tensor.matmul(up[n % 2][s_][:], sw[w][:, f, k, s_], x_part[x][:, k],
                                                            start=(k == 0 and w == 0 and x == 0), stop=(k == KD - 1 and x == 1))
                            last.then_inc(s_up, 1)
                        if b and f == 2:
                            turn_base(b - 1)
                        if b == B - 1 and f == 2:
                            pe.wait_ge(s_ot, 1)
                            nc.tensor.transpose(bank[6][:, 0:P], order[:, 1, 0:P], ident[:])
                            nc.tensor.transpose(bank[7][0:CAP - P, 0:P], order[:, 1, P:CAP], ident[:]).then_inc(s_ot, 1)
                    if b == 0:
                        pe.wait_ge(s_dense, GROUPS)
                        for j in range(HALF):
                            last = nc.tensor.transpose(bank[6 + j // 4][:, (j % 4) * P:(j % 4 + 1) * P],
                                                       left[:, 2 * j:2 * j + 2].rearrange("p h e -> p (h e)"), ident[:])
                        last.then_inc(s_mt, 1)
                    for d in range(KD):
                        if b:
                            pe.wait_ge(s_bc, (b - 1) * KD + d + 1)
                        for f in range(KF):
                            if d == 0:
                                pe.wait_ge(s_act, b * KF + f + 1)
                            last = nc.tensor.matmul(down[d][:], sw2[:, f, d * P:(d + 1) * P], act_f[:, f],
                                                    start=(f == 0), stop=(f == KF - 1))
                        last.then_inc(s_dp, 1)
                        if b == 0 and d == 0:
                            pe.wait_ge(s_off, 1)
                            pe.wait_ge(s_v, 32)
                            nc.tensor.matmul(bank[6][:, 0:1], shift[:], cum[:, TH - 1:TH], start=True, stop=True).then_inc(s_off, 1)
                turn_base(B - 1)

            @block.scalar
            def _(act):
                def high_context(b):
                    nc.scalar.activation(x_part[0][:], hist[:, :, b], ACT.Copy).then_inc(s_xhi, 1)

                def high_weights(f):
                    nc.scalar.activation(sw[0][:, f], columns(f), ACT.Copy).then_inc(s_whi, 1)

                high_context(0)
                act.wait_ge(s_w, 32)
                high_weights(0)

                def exp(g):
                    act.wait_ge(s_lg, g + 1)
                    nc.scalar.activation(gates[:, g * GT:(g + 1) * GT].rearrange("p t e -> p (t e)"),
                                         left[:, g * GT:(g + 1) * GT].rearrange("p t e -> p (t e)"), ACT.Exp).then_inc(s_ex, 1)

                for i in range(TILES):
                    act.wait_ge(s_rt, i + 1)
                    nc.scalar.activation(rows[:, i], bank[i % 4][:, 0:ROW], ACT.Copy).then_inc(s_rc, 1)
                    if i in (GT - 5, GT - 1):
                        high_weights(1 + i // GT + (i + 1) // GT)
                    if i == GT + 3:
                        exp(0)
                exp(1)

                def store_base(b):
                    for h in range(KD):
                        act.wait_ge(s_bt, b * KD + h + 1)
                        if h == 0 and b >= 2:
                            act.wait_ge(s_out[b % 2], 16 * (b // 2))
                        nc.scalar.activation(orow[:, b % 2, 2 * h:2 * h + 2].rearrange("p j d -> p (j d)"), down[h][:], ACT.Copy).then_inc(s_bc, 1)

                for b in range(B):
                    for f in range(KF):
                        n = b * KF + f
                        act.wait_ge(s_up, 2 * n + 1)
                        if n >= 2:
                            act.wait_ge(s_act, n - 1)
                        nc.scalar.activation(lin[:, n % 2], up[n % 2][0][:], ACT.Copy).then_inc(s_lin, 1)
                        act.wait_ge(s_up, 2 * n + 2)
                        nc.scalar.activation(act_f[:, f], up[n % 2][1][:], ACT.Silu).then_inc(s_silu, 1)
                        if b == 0 and f + 3 < KF:
                            high_weights(f + 3)
                        if b and f == 3:
                            store_base(b - 1)
                    if b < B - 1:
                        high_context(b + 1)
                    for d in range(KD):
                        act.wait_ge(s_dp, b * KD + d + 1)
                        act.wait_ge(s_xlo, b + 1)
                        nc.scalar.activation(hist[:, d, b], down[d][:], ACT.Copy).then_inc(s_base, 1)
                store_base(B - 1)

            @block.gpsimd
            def _(pool):
                nc.gpsimd.memset(cum[:, 0:ROW], 0.0).then_inc(s_z, 1)

                def low_context(b):
                    pool.wait_ge(s_xhi, b + 1)
                    nc.gpsimd.tensor_tensor(x_part[1][:], hist[:, :, b], x_part[0][:].bitcast(F32), ALU.subtract).then_inc(s_xlo, 1)

                def low_weights(f):
                    pool.wait_ge(s_whi, f + 1)
                    nc.gpsimd.tensor_tensor(sw[1][:, f], columns(f), sw[0][:, f].bitcast(F32), ALU.subtract).then_inc(s_wlo, 1)

                low_context(0)
                for f in range(3):
                    low_weights(f)
                for b in range(B):
                    for f in range(KF):
                        n = b * KF + f
                        pool.wait_ge(s_silu, n + 1)
                        nc.gpsimd.tensor_tensor(act_f[:, f], act_f[:, f], lin[:, n % 2], ALU.mult).then_inc(s_act, 1)
                        if b == 0 and f + 3 < KF:
                            low_weights(f + 3)
                        if b == B - 1 and f == KF - 2:
                            pool.wait_ge(s_tok, 2)
                            pool.wait_ge(s_rows, 96)
                            gather(pool, 0, 0)
                    if b < B - 1:
                        low_context(b + 1)
                    else:
                        gather(pool, 1, 1)
                    pool.wait_ge(s_base, (b + 1) * KD)
                    nc.gpsimd.tensor_tensor(xT[:, :, b, 0:S], xT[:, :, b, 0:S], hist[:, :, b], ALU.add).then_inc(s_sum, 1)

            @block.vector
            def _(dve):
                done = [0]

                def chain(ins):
                    done[0] += 1
                    ins.then_inc(s_c, 1)
                    dve.wait_ge(s_c, done[0])

                def spread(col, g):
                    return st[:, col, g * GT:(g + 1) * GT].unsqueeze(2).to_broadcast([P, GT, NE])

                of = [slice(g * GT, (g + 1) * GT) for g in range(GROUPS)]
                for g in range(GROUPS):
                    dve.wait_ge(s_rc, (g + 1) * GT)
                    logits = rows[:, of[g], P:P + NE]
                    chain(nc.vector.tensor_reduce(st[:, 0, of[g]], logits, AX.X, ALU.max))
                    nc.vector.tensor_tensor(left[:, of[g]], logits, spread(0, g), ALU.subtract).then_inc(s_lg, 1)
                for g in range(GROUPS):
                    dve.wait_ge(s_ex, g + 1)
                    chain(nc.vector.tensor_reduce(st[:, 1, of[g]], gates[:, of[g]], AX.X, ALU.add))
                    chain(nc.vector.reciprocal(st[:, 2, of[g]], st[:, 1, of[g]]))
                    chain(nc.vector.tensor_tensor(gates[:, of[g]], gates[:, of[g]], spread(2, g), ALU.mult))
                    for i in range(g * GT, (g + 1) * GT):
                        last = nc.vector.max(top8[:, i], gates[:, i])
                    chain(last)
                    for i in range(g * GT, (g + 1) * GT):
                        last = nc.vector.match_replace(left[:, i], top8[:, i], gates[:, i], -1.0)
                    chain(last)
                    nc.vector.tensor_reduce(st[:, 0, of[g]], top8[:, of[g]], AX.X, ALU.add)
                    chain(nc.vector.tensor_scalar(left[:, of[g]], left[:, of[g]], 0.0, None, ALU.is_lt))
                    chain(nc.vector.tensor_scalar(st[:, 1, of[g]], st[:, 0, of[g]], EPS, None, ALU.max))
                    nc.vector.reciprocal(st[:, 3, of[g]], st[:, 1, of[g]])
                    chain(nc.vector.tensor_tensor(gates[:, of[g]], gates[:, of[g]], left[:, of[g]], ALU.mult))
                    nc.vector.tensor_tensor(rows[:, of[g], P:P + NE], gates[:, of[g]], spread(3, g), ALU.mult).then_inc(s_dense, 1)
                dve.wait_ge(s_mt, 1)
                for i in range(2):
                    last = nc.vector.tensor_copy(maskT[:, 512 * i:512 * i + 512], bank[6 + i][:])
                chain(last)
                dve.wait_ge(s_z, 2)
                chain(nc.vector.tensor_tensor_scan(cum[:], ones[:, 0:1].to_broadcast([P, TH]), maskT, 0.0, ALU.mult, ALU.add))
                dve.sem_inc(s_off, 1)
                dve.wait_ge(s_off, 2)
                chain(nc.vector.tensor_copy(before[:], bank[6][:, 0:1]))
                dve.wait_ge(s_v, 32)
                chain(nc.vector.tensor_scalar(cum[:], cum[:], before[:, 0:1], float(CAP), ALU.add, ALU.is_le))
                chain(nc.vector.tensor_tensor(cum[:], cum[:], maskT, ALU.mult))
                chain(nc.vector.tensor_tensor(cum[:], cum[:], vrev[:], ALU.mult))
                for i in range(ROUNDS):
                    top = order[:, 0, 8 * i:8 * i + 8]
                    chain(nc.vector.max(top, cum[:]))
                    chain(nc.vector.match_replace(cum[:], top, cum[:], 0.0))
                nc.vector.tensor_copy(order[0:NE, 1, :], order[0:NE, 0, :])
                chain(nc.vector.tensor_copy(order[NE:P, 1, :], order[NE:P, 0, ::-1]))
                dve.sem_inc(s_ot, 1)
                dve.wait_ge(s_ot, 2)
                for c, (a, z) in enumerate(CAPS):
                    n = z - a
                    chain(nc.vector.tensor_copy(slots[0:n, 0], bank[6 + c][0:n, 0:NE]))
                    chain(nc.vector.tensor_tensor(slots[0:n, 1], slots[0:n, 0], bank[6 + c][0:n, NE:P], ALU.max))
                    chain(nc.vector.tensor_scalar(slots[0:n, 2], slots[0:n, 1], 0.0, None, ALU.is_equal))
                    chain(nc.vector.tensor_scalar(slots[0:n, 1], slots[0:n, 1], -1.0, float(T), ALU.mult, ALU.add))
                    chain(nc.vector.tensor_scalar(slots[0:n, 2], slots[0:n, 2], slot_row[0:n, c:c + 1], None, ALU.mult))
                    nc.vector.tensor_tensor(tok[c][:], slots[0:n, 1], slots[0:n, 2], ALU.add).then_inc(s_tok, 1)
                    dve.wait_ge(s_tok, c + 1)


def experts(nc, sb, sem, A, bank, ident, ring, s_w, got, s_got, gather, name_rows, s_pass, out, s_base):
    UP = KD * 2 * FFN
    w1 = [v[:, 0:UP].rearrange("p (k f) -> p k f", k=KD) for v in ring]
    w2 = [v[:, UP:].rearrange("p (f d) -> p f d", f=KF) for v in ring]
    with ExitStack() as own:
        def t(name, shape, dt=F32):
            return own.enter_context(nc.sbuf_tensor(name, shape, dt))

        to_idx = [t(f"to_row{c}", [z - a, 1], U32) for c, (a, z) in enumerate(CAPS)]
        xe = [t(f"xe{q}", [P, KD, CAP]) for q in range(2)]
        gate = t("gate_f", [P, 2, CAP])
        mid = [t(f"mid{q}", [P, KF, CAP]) for q in range(2)]
        ye = [t(f"ye{q}", [P, KD, CAP]) for q in range(2)]
        res = [[t(f"res{q}{c}", [z - a, D]) for c, (a, z) in enumerate(CAPS)] for q in range(2)]

        s_to = sem("add_rows_named")
        s_xt, s_xe = sem("tokens_turned"), sem("tokens_copied")
        s_up, s_silu, s_mid = sem("pair_pre"), sem("pair_silu"), sem("pair_done")
        s_y, s_ye = sem("down_pre"), sem("down_copied")
        s_yt, s_res, s_add = sem("down_turned"), sem("weighted"), sem("added")

        def wait(eng, s, n):
            if not isinstance(n, int) or n > 0:
                eng.wait_ge(s, n)

        def run(eng, body):
            for u in range(RING):
                body(u, u)
            with eng.Fori(1, NE // RING - 1) as i:
                for u in range(RING):
                    body(i * RING + u, u)
            for u in range(RING):
                body(NE - RING + u, u)

        def first(e):
            return isinstance(e, int) and e == 0

        def past(e, n):
            return isinstance(e, int) and e + n >= NE

        def uses(e, u):
            return e - u + RING

        with nc.Block() as block:
            @block.sync
            def _(sp):
                def load(e, u):
                    if first(e):
                        return
                    wait(sp, s_y, e - RING + 1)
                    src = A["ew"][e] if isinstance(e, int) else A["ew"][bass.ds(e, 1)].rearrange("o p n -> p (o n)")
                    sp.dma_start(ring[u][:], src).then_inc(s_w[u], 16)

                run(sp, load)

            @block.gpsimd
            def _(pool):
                def gather_again(e, u):
                    if not isinstance(e, int) or e >= RING:
                        pool.wait_ge(s_got[u], (uses(e, u) - RING) * (32 // RING))
                    gather(pool, e, u)

                def add(e, u):
                    wait(pool, s_add, e * 32)
                    if first(e):
                        for q in range(2):
                            pool.wait_ge(s_base[q], 8 * B)
                    name_rows(pool, to_idx, e, s_to)
                    pool.wait_ge(s_res, e + 1)
                    pool.sem_inc(s_pass, 1)
                    for c in range(2):
                        nc.gpsimd.indirect_dma_start(
                            out=out[:, :], out_offset=bass.IndirectOffsetOnAxis(ap=to_idx[c][:, 0:1], axis=0),
                            in_=res[u % 2][c][:], in_offset=None, compute_op=ALU.add).then_inc(s_add, 16)

                def body(e, u):
                    if not first(e):
                        add(e - 1, (u - 1) % RING)
                    if not past(e, 3):
                        gather_again(e + 3, (u + 3) % RING)

                gather_again(2, 2)
                run(pool, body)
                add(NE - 1, RING - 1)
                pool.wait_ge(s_add, NE * 32)

            @block.tensor
            def _(pe):
                def turn_in(e, u):
                    pe.wait_ge(s_got[u], uses(e, u) * (32 // RING))
                    wait(pe, s_xe, e)
                    for c, (a, z) in enumerate(CAPS):
                        for k in range(KD):
                            last = nc.tensor.transpose(bank[7][:, k * CAP + a:k * CAP + z], got[u][c][:, k * (P + NE):k * (P + NE) + P],
                                                       ident[0:z - a, 0:z - a])
                    last.then_inc(s_xt, 1)

                def turn_out(e, u):
                    pe.wait_ge(s_ye, e + 1)
                    wait(pe, s_res, e)
                    for c, (a, z) in enumerate(CAPS):
                        for k in range(KD):
                            last = nc.tensor.transpose(bank[6][0:z - a, c * D + k * P:c * D + (k + 1) * P], ye[u % 2][:, k, a:z], ident[:])
                    last.then_inc(s_yt, 1)

                def body(e, u):
                    pe.wait_ge(s_w[u], uses(e, u) * (16 // RING))
                    pe.wait_ge(s_xe, e + 1)
                    for f in range(KF):
                        wait(pe, s_mid, e * KF + (f - 2))
                        for s_ in range(2):
                            for k in range(KD):
                                last = nc.tensor.matmul(bank[f % 3][:, s_ * CAP:(s_ + 1) * CAP],
                                                        w1[u][:, k, s_ * FFN + f * P:s_ * FFN + (f + 1) * P], xe[u % 2][:, k],
                                                        start=(k == 0), stop=(k == KD - 1))
                        last.then_inc(s_up, 1)
                    if not first(e):
                        turn_out(e - 1, (u - 1) % RING)
                    if not past(e, 1):
                        turn_in(e + 1, (u + 1) % RING)
                    for d in range(KD):
                        for f in range(KF):
                            if d == 0:
                                pe.wait_ge(s_mid, e * KF + (f + 1))
                            last = nc.tensor.matmul(bank[4 + u % 2][:, d * CAP:(d + 1) * CAP], w2[u][:, f, d * P:(d + 1) * P], mid[u % 2][:, f],
                                                    start=(f == 0), stop=(f == KF - 1))
                    last.then_inc(s_y, 1)

                turn_in(0, 0)
                run(pe, body)
                turn_out(NE - 1, RING - 1)

            @block.scalar
            def _(act):
                def copy_in(e, u):
                    act.wait_ge(s_xt, e + 1)
                    nc.scalar.activation(xe[u % 2][:].rearrange("p k t -> p (k t)"), bank[7][:, 0:KD * CAP], ACT.Copy).then_inc(s_xe, 1)

                def body(e, u):
                    for f in range(KF):
                        act.wait_ge(s_up, e * KF + (f + 1))
                        wait(act, s_mid, e * KF + (f - 1))
                        nc.scalar.activation(gate[:, f % 2], bank[f % 3][:, CAP:2 * CAP], ACT.Silu).then_inc(s_silu, 1)
                    if not past(e, 1):
                        copy_in(e + 1, (u + 1) % RING)
                    act.wait_ge(s_y, e + 1)
                    nc.scalar.activation(ye[u % 2][:].rearrange("p k t -> p (k t)"), bank[4 + u % 2][:, 0:KD * CAP], ACT.Copy).then_inc(s_ye, 1)

                copy_in(0, 0)
                run(act, body)

            @block.vector
            def _(dve):
                def weigh(e, u):
                    dve.wait_ge(s_yt, e + 1)
                    wait(dve, s_add, e * 32 - 32)
                    dve.wait_ge(s_got[u], uses(e, u) * (32 // RING))
                    for c, (a, z) in enumerate(CAPS):
                        col = got[u][c][:, P + e:P + e + 1] if isinstance(e, int) else got[u][c][:, bass.ds(e + P, 1)]
                        last = nc.vector.tensor_scalar(res[u % 2][c][:], bank[6][0:z - a, c * D:(c + 1) * D], col, None, ALU.mult)
                    last.then_inc(s_res, 1)

                def body(e, u):
                    for f in range(KF):
                        dve.wait_ge(s_silu, e * KF + (f + 1))
                        nc.vector.tensor_tensor(mid[u % 2][:, f], bank[f % 3][:, 0:CAP], gate[:, f % 2], ALU.mult).then_inc(s_mid, 1)
                    if not first(e):
                        weigh(e - 1, (u - 1) % RING)

                run(dve, body)
                weigh(NE - 1, RING - 1)


def _layout(inputs):
    def f(name):
        return np.asarray(inputs[name])

    a = {k: f(k) for k in inputs if k.startswith("L0_") or k.startswith("L1_cond")}
    for n in ("L0_ffn_w_r", "L0_ffn_b1", "L0_ffn_b2", "L1_cond_sb1", "L1_cond_sb2"):
        a[n] = a[n].reshape(-1, P).T
    for n in ("L1_cond_eb1", "L1_cond_eb2"):
        a[n] = a[n].reshape(NE0, -1, P).transpose(0, 2, 1)
    a["xT"] = f("x").reshape(T, D).T
    a["condT"] = f("cond_1024").T
    wg, eye = f("L1_ffn_wg").T.reshape(KD, P, NE), np.eye(P, dtype=np.float32)
    a["turn"] = np.stack([np.concatenate([eye, wg[0]], axis=1), np.concatenate([wg[1], eye], axis=1)], axis=1)
    a["sw1T"] = f("L1_ffn_shared_w1").T
    a["sw2T"] = f("L1_ffn_shared_w2").T
    up = f("L1_ffn_expert_w1").transpose(0, 2, 1).reshape(NE, KD, P, 2 * FFN).transpose(0, 2, 1, 3).reshape(NE, P, -1)
    down = f("L1_ffn_expert_w2").transpose(0, 2, 1).reshape(NE, KF, P, D).transpose(0, 2, 1, 3).reshape(NE, P, -1)
    a["ew"] = np.concatenate([up, down], axis=2)
    a["ident"] = np.eye(P, dtype=np.float32)
    a["which"] = np.tile(np.eye(B, dtype=np.float32), (1, SEG))
    a["shift"] = np.eye(P, k=NE, dtype=np.float32)
    half = np.arange(T // 2, dtype=np.float32)
    a["vrev"] = np.repeat(np.stack([T - half, T // 2 - half]), NE, axis=0).astype(np.float32)
    a["slot_row"] = np.stack([np.arange(P), np.arange(P, 2 * P)], axis=1).astype(np.float32)
    return {k: np.ascontiguousarray(v) for k, v in a.items()}


def kernel(**inputs):
    import concourse.bacc as bacc
    from concourse.bass_utils import run_bass_kernel_spmd

    nc = bacc.Bacc("TRN2", target_bir_lowering=False, num_devices=1)
    arrays = {f"in_{k}": v for k, v in _layout(inputs).items()}
    A = {k[3:]: nc.dram_tensor(k, v.shape, mybir.dt.from_np(v.dtype), kind="ExternalInput").ap() for k, v in arrays.items()}
    out = nc.dram_tensor("out_rows", (T + CAP, D), F32, kind="ExternalOutput").ap()
    program(nc, A, out)
    r = run_bass_kernel_spmd(nc, [arrays], core_ids=[0])
    return r.results[0]["out_rows"][0:T].reshape(B, S, D)
```
